# Optimizing a Trainium2 kernel written in Bass

```python
import numpy as np
import jax
import jax.numpy as jnp

def _softmax(x, axis=-1):
    return jax.nn.softmax(x, axis=axis)

def _gelu(x):
    return jax.nn.gelu(x, approximate=True)

def _silu(x):
    return jax.nn.silu(x)

def _sigmoid(x):
    return jax.nn.sigmoid(x)

def _layernorm(x, axis=-1, eps=1e-05):
    m = jnp.mean(x, axis=axis, keepdims=True)
    v = jnp.var(x, axis=axis, keepdims=True)
    return (x - m) / jnp.sqrt(v + eps)

def _scatter_add(tgt, idx, src, axis=0):
    return tgt.at[idx].add(src)

def _segment_sum(src, seg, n):
    return jax.ops.segment_sum(src, seg, n)
kernel_name = 'mk_gnn_resnorm_d2_gnn_r8_46cb7a'

def setup_inputs(seed: int=0):
    np.random.seed(seed)
    _w = jnp.asarray

    def _rec_inputs():
        import jax
        import jax.numpy as jnp
        _gk = jax.random.key(seed)
        x = -0.0003713 + 1 * jax.random.normal(jax.random.fold_in(_gk, 1), (6250, 256), jnp.float32)
        _s = jax.random.randint(jax.random.fold_in(_gk, 2), (50000,), 0, 6250, jnp.int32)
        _d = jax.random.randint(jax.random.fold_in(_gk, 3), (50000,), 0, 6250, jnp.int32)
        _loop = jnp.arange(6250, dtype=jnp.int32)
        src = jnp.concatenate([_s, _d, _loop])
        dst = jnp.concatenate([_d, _s, _loop])
        _o = jnp.argsort(dst, stable=True)
        src = src[_o]
        dst = dst[_o]
        return (x, src, dst)
    x, src, dst = _rec_inputs()

    def _L0_gnn_setup():
        import jax, jax.numpy as jnp
        import numpy as np
        N, M, E = (6250, 1250, 62500)
        IN_CH, OUT_CH, HEADS = (256, 32, 8)
        NEG_SLOPE = 0.2
        EPS = 1e-16
        key = jax.random.key(seed)
        k1, k2, k3, k4, k5, k6 = jax.random.split(key, 6)
        x = jax.random.normal(k1, (N, IN_CH), dtype=jnp.float32)
        node_idx = jax.random.randint(k2, (E,), 0, N, dtype=jnp.int32)
        edge_idx = jax.random.randint(k3, (E,), 0, M, dtype=jnp.int32)
        hyperedge_index = jnp.stack([node_idx, edge_idx], axis=0)
        hyperedge_attr = jax.random.normal(k4, (M, IN_CH), dtype=jnp.float32)
        W = jax.random.normal(k5, (IN_CH, HEADS * OUT_CH), dtype=jnp.float32) / np.sqrt(IN_CH)
        att = jax.random.normal(k6, (1, HEADS, 2 * OUT_CH), dtype=jnp.float32) / np.sqrt(2 * OUT_CH)
        return {'x': x, 'hyperedge_index': hyperedge_index, 'hyperedge_attr': hyperedge_attr, 'W': W, 'att': att}
    _L0_gnn_all = _L0_gnn_setup()
    _L0_gnn_in = {k: v for k, v in _L0_gnn_all.items() if k in ('hyperedge_attr', 'W', 'att')}
    del _L0_gnn_all

    def _L1_gnn_setup():
        import jax, jax.numpy as jnp
        import numpy as np
        N_NODES = 2048
        N_EDGES = 32768
        D_IN = 256
        D = 256
        H = 512
        E = 64
        TOP_K = 2
        CAP = 1024
        BN_EPS = 1e-05

        def _moe_ff(x, Wg, bg, w1, b1, w2, b2):
            N = x.shape[0]
            logits = x @ Wg + bg
            vals, idx = jax.lax.top_k(logits, TOP_K)
            gates = jax.nn.softmax(vals, axis=-1)
            e_flat = idx.reshape(-1)
            g_flat = gates.reshape(-1)
            tok = jnp.arange(N * TOP_K) // TOP_K
            order = jnp.argsort(e_flat)
            e_s, tok_s, g_s = (e_flat[order], tok[order], g_flat[order])
            counts = jnp.bincount(e_flat, length=E)
            offs = jnp.concatenate([jnp.zeros((1,), counts.dtype), jnp.cumsum(counts)[:-1]])
            rank = jnp.arange(N * TOP_K) - offs[e_s]
            valid = rank < CAP
            slot = jnp.where(valid, e_s * CAP + rank, E * CAP)
            buf = jnp.zeros((E * CAP + 1, D), x.dtype).at[slot].set(x[tok_s])
            h = buf[:E * CAP].reshape(E, CAP, D)
            h1 = jax.nn.gelu(jnp.einsum('ecd,edh->ech', h, w1) + b1[:, None, :], approximate=False)
            h2 = jnp.einsum('ech,ehd->ecd', h1, w2) + b2[:, None, :]
            out_buf = h2.reshape(E * CAP, D)
            y_s = jnp.where(valid[:, None], out_buf[jnp.minimum(slot, E * CAP - 1)], 0.0)
            return jnp.zeros((N, D), x.dtype).at[tok_s].add(g_s[:, None] * y_s)

        def _forward(feats, W_gc, b_gc, W_res, b_res, Wg, bg, w1, b1, w2, b2, gamma, beta, src, dst):
            n = feats.shape[0]
            ones = jnp.ones((src.shape[0],), feats.dtype)
            deg_out = jnp.clip(jax.ops.segment_sum(ones, src, num_segments=n), 1.0)
            deg_in = jnp.clip(jax.ops.segment_sum(ones, dst, num_segments=n), 1.0)
            h = feats * jax.lax.rsqrt(deg_out)[:, None]
            m = jax.ops.segment_sum(h[src], dst, num_segments=n) * jax.lax.rsqrt(deg_in)[:, None]
            gc = m @ W_gc + b_gc
            x = gc + (feats @ W_res + b_res)
            core = _moe_ff(x, Wg, bg, w1, b1, w2, b2)
            y = x + core
            mean = jnp.mean(y, axis=0)
            var = jnp.mean((y - mean) ** 2, axis=0)
            return (y - mean) * jax.lax.rsqrt(var + BN_EPS) * gamma + beta
        key = jax.random.key(seed)
        ks = jax.random.split(key, 16)
        s = lambda d: 1.0 / np.sqrt(d)
        inp = {'feats': jax.random.normal(ks[0], (N_NODES, D_IN), jnp.float32), 'W_gc': jax.random.normal(ks[1], (D_IN, D), jnp.float32) * s(D_IN), 'b_gc': jnp.zeros((D,), jnp.float32), 'W_res': jax.random.normal(ks[2], (D_IN, D), jnp.float32) * s(D_IN), 'b_res': jnp.zeros((D,), jnp.float32), 'Wg': jax.random.normal(ks[3], (D, E), jnp.float32) * s(D), 'bg': jnp.zeros((E,), jnp.float32), 'w1': jax.random.normal(ks[4], (E, D, H), jnp.float32) * s(D), 'b1': jnp.zeros((E, H), jnp.float32), 'w2': jax.random.normal(ks[5], (E, H, D), jnp.float32) * s(H), 'b2': jnp.zeros((E, D), jnp.float32), 'gamma': jnp.ones((D,), jnp.float32), 'beta': jnp.zeros((D,), jnp.float32), 'src': jax.random.randint(ks[6], (N_EDGES,), 0, N_NODES), 'dst': jax.random.randint(ks[7], (N_EDGES,), 0, N_NODES)}
        return inp
    _L1_gnn_all = _L1_gnn_setup()
    _L1_gnn_in = {k: v for k, v in _L1_gnn_all.items() if k in ('W_gc', 'b_gc', 'W_res', 'b_res', 'Wg', 'bg', 'w1', 'b1', 'w2', 'b2', 'gamma', 'beta')}
    del _L1_gnn_all
    return {'x': x, 'src': src, 'dst': dst, 'L0_gnn_hyperedge_attr': _L0_gnn_in['hyperedge_attr'], 'L0_gnn_W': _L0_gnn_in['W'], 'L0_gnn_att': _L0_gnn_in['att'], 'L1_gnn_W_gc': _L1_gnn_in['W_gc'], 'L1_gnn_b_gc': _L1_gnn_in['b_gc'], 'L1_gnn_W_res': _L1_gnn_in['W_res'], 'L1_gnn_b_res': _L1_gnn_in['b_res'], 'L1_gnn_Wg': _L1_gnn_in['Wg'], 'L1_gnn_bg': _L1_gnn_in['bg'], 'L1_gnn_w1': _L1_gnn_in['w1'], 'L1_gnn_b1': _L1_gnn_in['b1'], 'L1_gnn_w2': _L1_gnn_in['w2'], 'L1_gnn_b2': _L1_gnn_in['b2'], 'L1_gnn_gamma': _L1_gnn_in['gamma'], 'L1_gnn_beta': _L1_gnn_in['beta']}

def reference(x, src, dst, L0_gnn_hyperedge_attr, L0_gnn_W, L0_gnn_att, L1_gnn_W_gc, L1_gnn_b_gc, L1_gnn_W_res, L1_gnn_b_res, L1_gnn_Wg, L1_gnn_bg, L1_gnn_w1, L1_gnn_b1, L1_gnn_w2, L1_gnn_b2, L1_gnn_gamma, L1_gnn_beta):
    import jax
    import jax.numpy as jnp

    def _L0_gnn_ref(x, hyperedge_index, hyperedge_attr, W, att):
        import jax, jax.numpy as jnp
        import numpy as np
        N, M, E = (6250, 1250, 62500)
        IN_CH, OUT_CH, HEADS = (256, 32, 8)
        NEG_SLOPE = 0.2
        EPS = 1e-16
        node = hyperedge_index[0]
        edge = hyperedge_index[1]
        num_nodes = x.shape[0]
        num_edges = hyperedge_attr.shape[0]
        xh = (x @ W).reshape(num_nodes, HEADS, OUT_CH)
        eh = (hyperedge_attr @ W).reshape(num_edges, HEADS, OUT_CH)
        x_i = xh[node]
        x_j = eh[edge]
        alpha = jnp.sum(jnp.concatenate([x_i, x_j], axis=-1) * att, axis=-1)
        alpha = jax.nn.leaky_relu(alpha, NEG_SLOPE)
        amax = jax.ops.segment_max(alpha, node, num_segments=num_nodes)
        alpha = jnp.exp(alpha - amax[node])
        asum = jax.ops.segment_sum(alpha, node, num_segments=num_nodes)
        alpha = alpha / (asum[node] + EPS)
        ones = jnp.ones((node.shape[0],), dtype=x.dtype)
        D = jax.ops.segment_sum(ones, node, num_segments=num_nodes)
        Dinv = jnp.where(D > 0, 1.0 / D, 0.0)
        B = jax.ops.segment_sum(ones, edge, num_segments=num_edges)
        Binv = jnp.where(B > 0, 1.0 / B, 0.0)
        msg1 = Binv[edge][:, None, None] * alpha[:, :, None] * x_i
        out_e = jax.ops.segment_sum(msg1, edge, num_segments=num_edges)
        msg2 = Dinv[node][:, None, None] * alpha[:, :, None] * out_e[edge]
        out_n = jax.ops.segment_sum(msg2, node, num_segments=num_nodes)
        return out_n.reshape(num_nodes, HEADS * OUT_CH)

    def _L1_gnn_ref(feats, W_gc, b_gc, W_res, b_res, Wg, bg, w1, b1, w2, b2, gamma, beta, src, dst):
        import jax, jax.numpy as jnp
        import numpy as np
        N_NODES = 2048
        N_EDGES = 32768
        D_IN = 256
        D = 256
        H = 512
        E = 64
        TOP_K = 2
        CAP = 1024
        BN_EPS = 1e-05

        def _moe_ff(x, Wg, bg, w1, b1, w2, b2):
            N = x.shape[0]
            logits = x @ Wg + bg
            vals, idx = jax.lax.top_k(logits, TOP_K)
            gates = jax.nn.softmax(vals, axis=-1)
            e_flat = idx.reshape(-1)
            g_flat = gates.reshape(-1)
            tok = jnp.arange(N * TOP_K) // TOP_K
            order = jnp.argsort(e_flat)
            e_s, tok_s, g_s = (e_flat[order], tok[order], g_flat[order])
            counts = jnp.bincount(e_flat, length=E)
            offs = jnp.concatenate([jnp.zeros((1,), counts.dtype), jnp.cumsum(counts)[:-1]])
            rank = jnp.arange(N * TOP_K) - offs[e_s]
            valid = rank < CAP
            slot = jnp.where(valid, e_s * CAP + rank, E * CAP)
            buf = jnp.zeros((E * CAP + 1, D), x.dtype).at[slot].set(x[tok_s])
            h = buf[:E * CAP].reshape(E, CAP, D)
            h1 = jax.nn.gelu(jnp.einsum('ecd,edh->ech', h, w1) + b1[:, None, :], approximate=False)
            h2 = jnp.einsum('ech,ehd->ecd', h1, w2) + b2[:, None, :]
            out_buf = h2.reshape(E * CAP, D)
            y_s = jnp.where(valid[:, None], out_buf[jnp.minimum(slot, E * CAP - 1)], 0.0)
            return jnp.zeros((N, D), x.dtype).at[tok_s].add(g_s[:, None] * y_s)

        def _forward(feats, W_gc, b_gc, W_res, b_res, Wg, bg, w1, b1, w2, b2, gamma, beta, src, dst):
            n = feats.shape[0]
            ones = jnp.ones((src.shape[0],), feats.dtype)
            deg_out = jnp.clip(jax.ops.segment_sum(ones, src, num_segments=n), 1.0)
            deg_in = jnp.clip(jax.ops.segment_sum(ones, dst, num_segments=n), 1.0)
            h = feats * jax.lax.rsqrt(deg_out)[:, None]
            m = jax.ops.segment_sum(h[src], dst, num_segments=n) * jax.lax.rsqrt(deg_in)[:, None]
            gc = m @ W_gc + b_gc
            x = gc + (feats @ W_res + b_res)
            core = _moe_ff(x, Wg, bg, w1, b1, w2, b2)
            y = x + core
            mean = jnp.mean(y, axis=0)
            var = jnp.mean((y - mean) ** 2, axis=0)
            return (y - mean) * jax.lax.rsqrt(var + BN_EPS) * gamma + beta
        return _forward(feats, W_gc, b_gc, W_res, b_res, Wg, bg, w1, b1, w2, b2, gamma, beta, src, dst)
    edge_index = jnp.stack([src, dst])
    x = _layernorm(x + _L0_gnn_ref(x, edge_index, L0_gnn_hyperedge_attr, L0_gnn_W, L0_gnn_att), axis=-1)
    x = _layernorm(x + _L1_gnn_ref(x, L1_gnn_W_gc, L1_gnn_b_gc, L1_gnn_W_res, L1_gnn_b_res, L1_gnn_Wg, L1_gnn_bg, L1_gnn_w1, L1_gnn_b1, L1_gnn_w2, L1_gnn_b2, L1_gnn_gamma, L1_gnn_beta, src, dst), axis=-1)
    return x

_drawn_inputs = setup_inputs


def setup_inputs(seed=0):
    import zlib

    import numpy as np

    out = dict(_drawn_inputs(seed))
    spreads = {'L1_gnn_b_gc': (0.0, 0.1),
     'L1_gnn_b_res': (0.0, 0.1),
     'L1_gnn_bg': (0.0, 0.1),
     'L1_gnn_b1': (0.0, 0.1),
     'L1_gnn_b2': (0.0, 0.1),
     'L1_gnn_gamma': (1.0, 0.2),
     'L1_gnn_beta': (0.0, 0.1)}
    factors = {'L0_gnn_hyperedge_attr': 8.0, 'L0_gnn_W': 5.096, 'L0_gnn_att': 8.0}
    for name, (base, spread) in spreads.items():
        noise = np.random.default_rng([zlib.crc32(name.encode()), seed]).standard_normal(out[name].shape)
        drawn = base * np.exp(spread * noise) if base else spread * noise
        out[name] = jnp.asarray(drawn.astype(out[name].dtype))
    for name, factor in factors.items():
        out[name] = (out[name] * factor).astype(out[name].dtype)
    return out
```

```python
from contextlib import ExitStack

import concourse.bass as bass
from concourse import mybir

F32 = mybir.dt.float32
F16 = mybir.dt.float16
BF16 = mybir.dt.bfloat16
I32 = mybir.dt.int32
U32 = mybir.dt.uint32
ALU = mybir.AluOpType
ACT = mybir.ActivationFunctionType
X = mybir.AxisListType.X

P = 128
NODES, FEAT = 6250, 256
NTILE = -(-NODES // P)
LAST = NODES - (NTILE - 1) * P
EDGES = 106250
STEP = 17
ECOL = NTILE * STEP
EFULL = EDGES - (P - 1) * ECOL
NT = -(-EDGES // P) + NTILE
NTM = 7 * P
HEADS, CH = 8, 32
HYPER = 1250
HC = HYPER + 1
HCH = 10
SKIP = float(1 << 20)
BANK = 512
EPS_LN = 1e-5
EXPERTS, HID, CAP = 64, 512, 1024
MT = (2 * NODES) // P + EXPERTS
ZCOLS = 7 * FEAT
assert MT % 7 == 0
assert P * ECOL >= EDGES and 0 < EFULL <= ECOL


class Order:

    def __init__(self, eng, sem):
        self.eng, self.sem, self.base, self.n = eng, sem, 0, 0

    def __call__(self, ins):
        self.n += 1
        ins.then_inc(self.sem, 1)
        self.eng.wait_ge(self.sem, self.base + self.n)

    def enter(self, i, steps):
        self.start, self.steps = self.base + self.n, steps
        self.base, self.n = self.start + i * steps, 0

    def leave(self, count):
        assert self.n == self.steps, (self.n, self.steps)
        self.base, self.n = self.start + count * self.steps, 0


class Ctx:
    pass


def banks(base, width):
    return [(c, min(BANK, width - c)) for c in range(0, width, BANK)]


def phase_sort_and_project(nc, k):
    with ExitStack() as ctx:
        sb = lambda n, s, d: ctx.enter_context(nc.sbuf_tensor(n, s, d))
        ps = lambda n, s, d: ctx.enter_context(nc.psum_tensor(n, s, d))
        sem = k.sem
        W = sb("W", [P, 2, FEAT], F32)
        attb = sb("attb", [P, HEADS, 2 * CH], F32)
        xin = sb("xin", [P, 2, FEAT], F32)
        xT = sb("xT", [P, 2, 2, P], F32)
        eh = sb("eh", [P, HCH, FEAT], F32)
        prod = sb("prod", [P, 7 * FEAT], F32)
        bTs = sb("bTs", [HEADS, HCH * P], F32)
        key = sb("key", [P, 2, ECOL], I32)
        keyi = sb("keyi", [P, 2, ECOL], I32)
        bucket = sb("bucket", [P, ECOL], F32)
        eq = sb("eq", [P, 7, ECOL], F32)
        run = sb("run", [P, 7, ECOL], F32)
        part = sb("part", [P, ECOL], F32)
        cnt = sb("cnt", [P, NTILE], F32)
        tiles = sb("tiles", [P, NTILE], F32)
        tilesi = sb("tilesi", [P, NTILE], I32)
        ends = sb("ends", [P, NTILE], F32)
        base = sb("base", [P, NTILE], F32)
        tnum = sb("tnum", [P, 7], F32)
        cmp = sb("cmp", [P, 7, NTILE], F32)
        tabf = sb("tabf", [P, 3, 7], F32)
        tabi = sb("tabi", [P, 3, 7], I32)
        numf = sb("numf", [P, NTILE], F32)
        fill = sb("fill", [P, NT, 2], F32)
        sidx = sb("sidx", [P, 2, STEP], I32)
        spay = sb("spay", [P, 2, STEP, 2], F32)
        pT = ps("pT", [P, 2, 2, P], F32)
        pX = ps("pX", [P, 2, BANK], F32)
        pC = ps("pC", [P, 2, BANK], F32)

        s_w = sem("w_loaded")
        s_x = [sem("x_loaded0"), sem("x_loaded1")]
        s_xfree = sem("x_free")
        s_xz = sem("x_buffers_zeroed")
        s_tr = sem("x_transposed")
        s_xT = sem("xT_ready")
        s_mm = sem("projected")
        s_cp = sem("projection_copied")
        s_keys = sem("keys_loaded")
        s_kset = sem("keys_padded")
        s_const = sem("constants_ready")
        s_dve = sem("dve_order_a")
        s_pool = sem("pool_order_a")
        s_cnt = sem("counts_ready")
        s_tot = sem("totals_ready")
        s_slots = sem("slots_ready")
        s_stage = sem("edges_staged")
        s_scat = [sem("edges_scattered0"), sem("edges_scattered1")]
        s_fillr = sem("fill_ready")
        s_fill = sem("slots_prefilled")
        s_b = sem("b_ready")
        s_bT = sem("bT_ready")
        s_bTs = sem("bT_copied")
        s_out = sem("tables_stored")
        s_tabs = sem("tables_ready")
        idle = k.idle

        block = ctx.enter_context(nc.Block())

        @block.sync
        def _(sp):
            sp.dma_start(W[:, :, :], k.W.rearrange("(c p) n -> p c n", p=P)).then_inc(s_w, 16)
            sp.dma_start(attb[:, :, :], k.att[0, :, :].partition_broadcast(P)).then_inc(s_w, 16)
            sp.wait_ge(s_kset, 1)
            for j, e in enumerate((k.src, k.dst)):
                sp.dma_start(key[0:P - 1, j, :], e[0:(P - 1) * ECOL].rearrange("(p t) -> p t", t=ECOL)).then_inc(s_keys, 16)
                sp.dma_start(key[P - 1:P, j, 0:EFULL], e[(P - 1) * ECOL:EDGES].rearrange("(p t) -> p t", p=1)).then_inc(s_keys, 16)
            sp.wait_ge(s_xz, 1)
            with sp.Fori(0, NTILE // 2) as i:
                for u in range(2):
                    sp.wait_ge(s_xfree, i * 2 + u + 1)
                    sp.dma_start(xin[:, u, :], k.x[bass.ds((i * 2 + u) * P, P), :]).then_inc(s_x[u], 16)
            sp.wait_ge(s_xfree, NTILE)
            sp.dma_start(xin[0:LAST, 0, :], k.x[(NTILE - 1) * P:NODES, :]).then_inc(s_x[0], 16)
            for c in range(HCH):
                t = NTILE + c
                rows = min(P, HYPER - c * P)
                sp.wait_ge(s_xfree, t + 1)
                sp.dma_start(xin[0:rows, t % 2, :], k.attr[c * P:c * P + rows, :]).then_inc(s_x[t % 2], 16)
                if rows < P:
                    sp.dma_start(xin[rows:rows + 1, t % 2, :], k.attr[HYPER - 1:HYPER, :]).then_inc(s_x[t % 2], 16)
            sp.wait_ge(s_fillr, 1)
            sp.dma_start(k.SS.rearrange("(p t) c -> p t c", p=P), fill[:, :, :]).then_inc(s_fill, 16)
            sp.wait_ge(s_bTs, 3)
            sp.dma_start(k.bT[:, :], bTs[:, :]).then_inc(s_out, 16)
            sp.wait_ge(s_tabs, 1)
            for j in range(3):
                sp.dma_start(k.tab[j, :].rearrange("(p t) -> p t", p=P), tabi[:, j, :]).then_inc(s_out, 16)
            sp.wait_ge(s_out, 64)

        @block.gpsimd
        def _(pool):
            o = Order(pool, s_pool)
            pool.memset(k.ones[:, :], 1.0).then_inc(s_const, 1)
            pool.iota(numf[:, :], [[1, NTILE]], base=0, channel_multiplier=0,
                      allow_small_or_imprecise_dtypes=True).then_inc(s_const, 1)
            pool.iota(tnum[:, :], [[1, 7]], base=0, channel_multiplier=7,
                      allow_small_or_imprecise_dtypes=True).then_inc(s_const, 1)
            pool.iota(k.iota[:, :], [[1, P]], base=0, channel_multiplier=0,
                      allow_small_or_imprecise_dtypes=True).then_inc(s_const, 1)
            pool.iota(k.iota16[:, :], [[1, HC]], base=0, channel_multiplier=0,
                      allow_small_or_imprecise_dtypes=True).then_inc(s_const, 1)
            o(pool.memset(k.ident[:, :], 0.0))
            pool.affine_select(out=k.ident[:, :], in_=k.ident[:, :], compare_op=ALU.not_equal, fill=1.0,
                               base=0, pattern=[[-1, P]], channel_multiplier=1).then_inc(s_const, 1)
            o(pool.memset(k.upper[:, :], 1.0))
            pool.affine_select(out=k.upper[:, :], in_=k.upper[:, :], compare_op=ALU.is_gt, fill=0.0,
                               base=0, pattern=[[1, P]], channel_multiplier=-1).then_inc(s_const, 1)
            pool.memset(fill[:, :, :], -1.0).then_inc(s_fillr, 1)
            bound = pool.to_reg(P * NT - 1)
            pool.wait_ge(s_fill, 16)

            def scatter(step, u):
                pool.wait_ge(s_stage, 2 * step + 2)
                pool.sem_inc(idle["pool"], 1)
                for c in range(STEP):
                    pool.indirect_dma_start(k.SS[:, :], bass.IndirectOffsetOnAxis(ap=sidx[:, u, c:c + 1], axis=0),
                                            spay[:, u, c, :], None, bounds_check=bound,
                                            oob_is_err=False).then_inc(s_scat[u], 16)
            with pool.Fori(0, NTILE // 2) as i:
                for u in range(2):
                    scatter(i * 2 + u, u)
            scatter(NTILE - 1, 0)
            pool.wait_ge(s_scat[0], 16 * STEP * (NTILE // 2 + 1))
            pool.wait_ge(s_scat[1], 16 * STEP * (NTILE // 2))

        @block.scalar
        def _(act):
            act.sem_inc(s_xfree, 2)
            act.sem_inc(s_cp, 2)

            def project(t, u, dst):
                act.wait_ge(s_tr, t + 1)
                act.activation(xT[:, u, :, :], pT[:, u, :, :], ACT.Copy).then_inc(s_xT, 1)
                act.wait_ge(s_mm, t + 1)
                act.sem_inc(idle["act"], 1)
                act.activation(dst, pX[:, u, 0:FEAT], ACT.Copy).then_inc(s_cp, 1)
            with act.Fori(0, NTILE // 2) as i:
                for u in range(2):
                    project(i * 2 + u, u, k.big1[:, bass.ds(i * 2 + u, 1), :].rearrange("p a n -> p (a n)"))
            project(NTILE - 1, 0, k.big1[:, NTILE - 1, :])
            for c in range(HCH):
                project(NTILE + c, (NTILE + c) % 2, eh[:, c, :])

            def stage(step, u, used):
                cols = bass.ds(step * STEP, STEP)
                if used is not None:
                    act.wait_ge(s_scat[u], used)
                    act.sem_inc(idle["act"], 1)
                act.activation(sidx[:, u, :], k.slot[:, 0, cols], ACT.Copy).then_inc(s_stage, 1)
                act.activation(spay[:, u, :, :], k.pay[:, 0, cols, :], ACT.Copy).then_inc(s_stage, 1)
            act.wait_ge(s_slots, 1)
            act.sem_inc(idle["act"], 1)
            for u in range(2):
                stage(u, u, None)
            with act.Fori(1, NTILE // 2) as i:
                for u in range(2):
                    stage(i * 2 + u, u, 16 * STEP * i)
            stage(NTILE - 1, 0, 16 * STEP * (NTILE // 2))
            act.wait_ge(s_bT, 1)
            act.activation(bTs[:, 0:BANK], pC[0:HEADS, 0, :], ACT.Copy).then_inc(s_bTs, 1)
            act.activation(bTs[:, BANK:2 * BANK], pC[0:HEADS, 1, :], ACT.Copy).then_inc(s_bTs, 1)
            act.activation(bTs[:, 2 * BANK:HCH * P], pX[0:HEADS, 0, 0:2 * P], ACT.Copy).then_inc(s_bTs, 1)

        @block.tensor
        def _(pe):
            pe.wait_ge(s_const, 7)
            pe.wait_ge(s_w, 32)

            def project(t, u, loaded):
                pe.wait_ge(s_x[u], loaded)
                pe.sem_inc(idle["pe"], 1)
                for c in range(2):
                    last = pe.transpose(pT[:, u, c, :], xin[:, u, c * P:(c + 1) * P], k.ident[:, :])
                last.then_inc(s_tr, 1)
                pe.wait_ge(s_xT, t + 1)
                pe.sem_inc(s_xfree, 1)
                pe.wait_ge(s_cp, t + 1)
                pe.sem_inc(idle["pe"], 1)
                for c in range(2):
                    last = pe.matmul(pX[:, u, 0:FEAT], xT[:, u, c, :], W[:, c, :], start=(c == 0), stop=(c == 1))
                last.then_inc(s_mm, 1)
            with pe.Fori(0, NTILE // 2) as i:
                for u in range(2):
                    project(i * 2 + u, u, i * 16 + 16)
            project(NTILE - 1, 0, 16 * (NTILE // 2) + 16)
            for c in range(HCH):
                t = NTILE + c
                project(t, t % 2, 16 * (t // 2) + 16 + (16 if c == HCH - 1 else 0))
            for j in range(2):
                pe.wait_ge(s_cnt, j + 1)
                pe.matmul(pC[:, 0, 0:NTILE], k.ones[:, :], cnt[:, :], start=True, stop=True)
                pe.matmul(pC[:, 1, 0:NTILE], k.upper[:, :], cnt[:, :], start=True, stop=True).then_inc(s_tot, 1)
            pe.wait_ge(s_b, 1)
            pe.wait_ge(s_cp, NTILE + HCH + 2)
            for c in range(HCH):
                out = pC[0:HEADS, c // 4, (c % 4) * P:(c % 4 + 1) * P] if c < 8 else pX[0:HEADS, 0, (c - 8) * P:(c - 7) * P]
                last = pe.transpose(out, k.bE[:, c, :], k.ident[:, :])
            last.then_inc(s_bT, 1)

        @block.vector
        def _(dve):
            o = Order(dve, s_dve)
            dve.memset(key[:, :, :], NTILE * P).then_inc(s_kset, 1)
            dve.memset(xin[:, :, :], 0.0).then_inc(s_xz, 1)
            dve.wait_ge(s_keys, 64)
            dve.wait_ge(s_const, 7)
            for j in range(2):
                o(dve.tensor_scalar(keyi[:, 0, :], key[:, j, :], P - 1, None, ALU.bitwise_and))
                o(dve.tensor_copy(k.pay[:, j, :, 0], keyi[:, 0, :]))
                if j == 0:
                    o(dve.tensor_scalar(k.pay[:, 0, :, 1], key[:, 1, :], float(HYPER), None, ALU.min))
                else:
                    o(dve.tensor_copy(k.pay[:, 1, :, 1], key[:, 0, :]))
                o(dve.tensor_scalar(keyi[:, 1, :], key[:, j, :], 7, None, ALU.arith_shift_right))
                o(dve.tensor_copy(bucket[:, :], keyi[:, 1, :]))
                for r in range(NTILE // 7):
                    o(dve.tensor_tensor(eq[:, :, :], bucket[:, :].unsqueeze(1).to_broadcast([P, 7, ECOL]),
                                        numf[:, 7 * r:7 * r + 7].unsqueeze(2).to_broadcast([P, 7, ECOL]), ALU.is_equal))
                    o(dve.tensor_reduce(cnt[:, 7 * r:7 * r + 7], eq[:, :, :], X, ALU.add))
                dve.sem_inc(s_cnt, 1)
                dve.wait_ge(s_tot, j + 1)
                o(dve.tensor_scalar(tiles[:, :], pC[:, 0, 0:NTILE], float(P - 1), None, ALU.add))
                o(dve.tensor_copy(tilesi[:, :], tiles[:, :]))
                o(dve.tensor_scalar(tilesi[:, :], tilesi[:, :], 7, None, ALU.arith_shift_right))
                o(dve.tensor_copy(tiles[:, :], tilesi[:, :]))
                o(dve.tensor_scalar(tiles[:, :], tiles[:, :], 1.0, None, ALU.max))
                o(dve.tensor_tensor_scan(ends[:, :], k.ones[:, 0:NTILE], tiles[:, :], 0.0, ALU.mult, ALU.add))
                o(dve.tensor_tensor(base[:, :], ends[:, :], tiles[:, :], ALU.subtract))
                o(dve.tensor_scalar(base[:, :], base[:, :], float(P), -1.0, ALU.mult, ALU.add))
                o(dve.tensor_tensor(base[:, :], base[:, :], pC[:, 1, 0:NTILE], ALU.add))
                for r in range(NTILE // 7):
                    o(dve.tensor_tensor(eq[:, :, :], bucket[:, :].unsqueeze(1).to_broadcast([P, 7, ECOL]),
                                        numf[:, 7 * r:7 * r + 7].unsqueeze(2).to_broadcast([P, 7, ECOL]), ALU.is_equal))
                    for q in range(7):
                        last = dve.tensor_tensor_scan(run[:, q, :], k.ones[:, 0:1].to_broadcast([P, ECOL]), eq[:, q, :],
                                                      base[:, 7 * r + q:7 * r + q + 1], ALU.mult, ALU.add)
                    o(last)
                    o(dve.tensor_tensor(run[:, :, :], run[:, :, :], eq[:, :, :], ALU.mult))
                    acc = part if r else bucket_slot(k, j)
                    o(dve.tensor_reduce(acc[:, :] if r else acc, run[:, :, :].rearrange("p b t -> p t b"), X, ALU.add))
                    if r:
                        o(dve.tensor_tensor(bucket_slot(k, j), bucket_slot(k, j), part[:, :], ALU.add))
                o(dve.tensor_copy(keyi[:, 0, :], bucket_slot(k, j)))
                o(dve.tensor_scalar(keyi[:, 1, :], keyi[:, 0, :], 7, None, ALU.arith_shift_right))
                o(dve.tensor_scalar(keyi[:, 0, :], keyi[:, 0, :], P - 1, None, ALU.bitwise_and))
                o(dve.tensor_copy(part[:, :], keyi[:, 0, :]))
                o(dve.tensor_copy(bucket_slot(k, j), keyi[:, 1, :]))
                o(dve.scalar_tensor_tensor(bucket_slot(k, j), part[:, :], float(NT), bucket_slot(k, j), ALU.mult, ALU.add))
                o(dve.tensor_scalar(part[:, :], bucket[:, :], float(NTILE), SKIP, ALU.is_equal, ALU.mult))
                o(dve.tensor_tensor(bucket_slot(k, j), bucket_slot(k, j), part[:, :], ALU.max))
                dve.sem_inc(s_slots, 1)
                o(dve.tensor_tensor(cmp[:, :, :], ends[:, :].unsqueeze(1).to_broadcast([P, 7, NTILE]),
                                    tnum[:, :].unsqueeze(2).to_broadcast([P, 7, NTILE]), ALU.is_le))
                o(dve.tensor_reduce(tabf[:, j, :], cmp[:, :, :], X, ALU.add))
                o(dve.tensor_scalar(tabf[:, j, :], tabf[:, j, :], float(NTILE - 1), None, ALU.min))
                if j == 0:
                    o(dve.tensor_scalar(base[:, :], ends[:, :], -1.0, None, ALU.add))
                    o(dve.tensor_tensor(cmp[:, :, :], base[:, :].unsqueeze(1).to_broadcast([P, 7, NTILE]),
                                        tnum[:, :].unsqueeze(2).to_broadcast([P, 7, NTILE]), ALU.is_equal))
                    o(dve.tensor_reduce(tabf[:, 2, :], cmp[:, :, :], X, ALU.add))
            o(dve.tensor_copy(tabi[:, :, :], tabf[:, :, :]))
            dve.sem_inc(s_tabs, 1)
            dve.wait_ge(s_w, 32)
            dve.wait_ge(s_cp, NTILE + HCH + 2)

            def logits(dst, rows, n, half):
                w = attb[:, :, half * CH:(half + 1) * CH].unsqueeze(1).to_broadcast([P, n, HEADS, CH])
                pv = prod[:, 0:n * FEAT].rearrange("p (i h c) -> p i h c", h=HEADS, c=CH)
                o(dve.tensor_tensor(pv, rows.rearrange("p i (h c) -> p i h c", c=CH), w, ALU.mult))
                o(dve.tensor_reduce(dst, pv, X, ALU.add))
            for r in range(NTILE // 7):
                logits(k.a[:, 7 * r:7 * r + 7, :], k.big1[:, 7 * r:7 * r + 7, :], 7, 0)
            for r in range(2):
                logits(k.bE[:, 5 * r:5 * r + 5, :], eh[:, 5 * r:5 * r + 5, :], 5, 1)
            dve.sem_inc(s_b, 1)


def phase_count(nc, k):
    with ExitStack() as ctx:
        sb = lambda n, s, d: ctx.enter_context(nc.sbuf_tensor(n, s, d))
        sem = k.sem
        edges = sb("edges", [P, NT, 2], F32)
        tab = sb("tabrow", [1, 2, NTM], I32)
        ohn = sb("onehot_node", [P, 2, P], BF16)
        ohe = sb("onehot_edge", [P, 2, HC], BF16)
        zero = sb("zero", [P, HC], F32)
        snap = sb("snap", [P, HC], F32)
        run = ctx.enter_context(nc.psum_tensor("running", [P, 3 * BANK], F32))

        s_in = sem("slots_loaded")
        s_z = sem("zeros_ready")
        s_oh = sem("onehots_ready")
        s_mm = sem("counted")
        s_evac = sem("count_passed")
        s_snap = sem("count_copied")
        s_R = sem("counts_stored")
        idle = k.idle
        block = ctx.enter_context(nc.Block())

        @block.sync
        def _(sp):
            sp.dma_start(edges[:, :, :], k.SS.rearrange("(p t) c -> p t c", p=P)).then_inc(s_in, 16)
            for j, row in enumerate((0, 2)):
                sp.dma_start(tab[:, j, :], k.tab[row:row + 1, :]).then_inc(s_in, 16)

        @block.vector
        def _(dve):
            dve.memset(zero[:, :], 0.0).then_inc(s_z, 1)
            dve.memset(ohn[:, 1, :], 0.0).then_inc(s_z, 1)
            dve.memset(ohe[:, 1, :], 0.0).then_inc(s_z, 1)
            dve.sem_inc(s_mm, 1)
            dve.wait_ge(s_in, 48)
            with dve.Fori(0, NT // 2) as i:
                for u in range(2):
                    t = i * 2 + u
                    dve.wait_ge(s_mm, t + 1)
                    dve.sem_inc(idle["dve"], 1)
                    dve.tensor_scalar(ohn[:, u, :], k.iota16[:, 0:P], edges[:, bass.ds(t, 1), 0:1].rearrange("p a b -> p (a b)"),
                                      None, ALU.is_equal).then_inc(s_oh, 1)
                    dve.tensor_scalar(ohe[:, u, :], k.iota16[:, :], edges[:, bass.ds(t, 1), 1:2].rearrange("p a b -> p (a b)"),
                                      None, ALU.is_equal).then_inc(s_oh, 1)

        @block.tensor
        def _(pe):
            pe.wait_ge(s_z, 3)
            for c, w in banks(0, HC):
                last = pe.matmul(run[:, c:c + w], ohn[:, 1, :], ohe[:, 1, c:c + w], start=True, stop=True)
            last.then_inc(s_mm, 1)
            with pe.Fori(0, NT // 2) as i:
                for u in range(2):
                    t = i * 2 + u
                    pe.wait_ge(s_oh, t * 2 + 2)
                    pe.wait_ge(s_evac, t + 1)
                    pe.sem_inc(idle["pe"], 1)
                    for c, w in banks(0, HC):
                        last = pe.matmul(run[:, c:c + w], ohn[:, u, :], ohe[:, u, c:c + w], start=False, stop=True,
                                         skip_group_check=True)
                    last.then_inc(s_mm, 1)

        @block.scalar
        def _(act):
            act.sem_inc(s_evac, 1)
            act.wait_ge(s_z, 3)
            act.dma_start(k.R[0, :, :], zero[:, :]).then_inc(s_R, 16)
            act.wait_ge(s_in, 48)
            with act.Fori(0, NT) as t:
                ends = act.value_load(tab[0:1, 1, bass.ds(t, 1)], min_val=0, max_val=1)
                with act.If(ends > 0):
                    bucket = act.value_load(tab[0:1, 0, bass.ds(t, 1)], min_val=0, max_val=NTILE - 1)
                    act.wait_ge(s_mm, t + 3)
                    act.wait_ge(s_R, bucket * 16 + 16)
                    act.sem_inc(idle["act"], 1)
                    act.activation(snap[:, :], run[:, 0:HC], ACT.Copy).then_inc(s_snap, 1)
                    act.wait_ge(s_snap, bucket + 1)
                    act.sem_inc(idle["act"], 1)
                    act.dma_start(k.R[bass.ds(bucket + 1, 1), :, :].rearrange("a p n -> (a p) n"), snap[:, :]).then_inc(s_R, 16)
                act.sem_inc(s_evac, 1)
            act.wait_ge(s_R, 16 * (NTILE + 1))


def phase_softmax(nc, k):
    with ExitStack() as ctx:
        sb = lambda n, s, d: ctx.enter_context(nc.sbuf_tensor(n, s, d))
        ps = lambda n, s, d: ctx.enter_context(nc.psum_tensor(n, s, d))
        sem = k.sem
        bbc = sb("bbc", [P, HEADS, HC], F32)
        Ra = sb("Ra", [P, HC], F32)
        Rb = sb("Rb", [P, HC], F32)
        C = sb("C", [P, HCH * P], F32)
        M = sb("M", [P, HC], F32)
        low = sb("low", [P, 2, HC], F32)
        Pb = sb("Pb", [P, HEADS, HC], F32)
        ctb = sb("ctb", [P, HCH, P], F32)
        urow = sb("urow", [2 * HEADS, P], F32)
        fill = low[:, :, :].rearrange("p a n -> p (a n)")[:, 0:2 * NT].rearrange("p (t c) -> p t c", c=2)
        bmax = sb("bmax", [P, HEADS], F32)
        top = sb("top", [P, HEADS], F32)
        u16 = sb("u16", [P, 2 * HEADS], F32)
        asum = sb("asum", [P, HEADS], F32)
        dinv = sb("dinv", [P, 1], F32)
        degr = sb("degr", [P, 1], F32)
        ai = sb("ai", [P, HEADS], F32)
        xs = sb("xs", [P, HEADS, CH], F32)
        sidx = sb("sidx2", [P, STEP], I32)
        spay = sb("spay2", [P, STEP, 2], F32)
        OE = ps("OE", [P, 2, 3 * BANK], F32)
        pT = ps("pT2", [P, 2, 4, P], F32)

        s_bbc = sem("b_loaded")
        s_r = sem("R_loaded")
        s_rfree = sem("R_used")
        s_c = sem("C_ready")
        s_u = sem("u_ready")
        s_t2 = sem("low_branch_ready")
        s_arg = sem("exponent_ready")
        s_e = sem("exp_ready")
        s_xs = sem("xs_ready")
        s_pm = sem("messages_added")
        s_tr = sem("C_transposed")
        s_trc = sem("transposes_copied")
        s_ctfree = sem("ct_stored")
        s_cts = sem("ct_dma")
        s_stage = sem("target_edges_staged")
        s_sfree = sem("staging_free")
        s_scat = sem("target_edges_scattered")
        s_fillr = sem("fillD_ready")
        s_fill = sem("DS_prefilled")
        s_dve = sem("dve_order_c")
        s_z = sem("oe_zeroed")
        s_end = sem("oe_copied")
        idle = k.idle
        block = ctx.enter_context(nc.Block())

        @block.sync
        def _(sp):
            sp.dma_start(bbc[:, :, :], k.bT[:, 0:HC].partition_broadcast(P)).then_inc(s_bbc, 16)
            sp.wait_ge(s_fillr, 2)
            sp.dma_start(k.DS.rearrange("(p t) c -> p t c", p=P), fill).then_inc(s_fill, 16)
            with sp.Fori(0, NTILE) as i:
                sp.wait_ge(s_rfree, i + 1)
                sp.sem_inc(idle["sp"], 1)
                sp.dma_start(Ra[:, :], k.R[bass.ds(i, 1), :, :].rearrange("a p n -> (a p) n")).then_inc(s_r, 16)
                sp.dma_start(Rb[:, :], k.R[bass.ds(i + 1, 1), :, :].rearrange("a p n -> (a p) n")).then_inc(s_r, 16)
                sp.wait_ge(s_trc, i * 4 + 4)
                sp.sem_inc(idle["sp"], 1)
                sp.dma_start(k.CT[:, :, bass.ds(i * P, P)].rearrange("c e n -> e c n"), ctb[:, :, :]).then_inc(s_cts, 16)
                sp.dma_start(k.UT[:, bass.ds(i * P, P)], urow[:, :]).then_inc(s_cts, 16)
                sp.wait_ge(s_cts, i * 32 + 32)
                sp.sem_inc(s_ctfree, 1)

        @block.gpsimd
        def _(pool):
            pool.memset(fill[:, :, 0:1], -1.0).then_inc(s_fillr, 1)
            pool.memset(fill[:, :, 1:2], 0.0).then_inc(s_fillr, 1)
            bound = pool.to_reg(P * NT - 1)
            pool.sem_inc(s_sfree, 1)
            pool.wait_ge(s_fill, 16)
            with pool.Fori(0, NTILE) as i:
                pool.wait_ge(s_stage, i * 2 + 2)
                pool.sem_inc(idle["pool"], 1)
                for c in range(STEP):
                    pool.indirect_dma_start(k.DS[:, :], bass.IndirectOffsetOnAxis(ap=sidx[:, c:c + 1], axis=0),
                                            spay[:, c, :], None, bounds_check=bound, oob_is_err=False).then_inc(s_scat, 16)
                pool.wait_ge(s_scat, i * (16 * STEP) + 16 * STEP)
                pool.sem_inc(s_sfree, 1)

        @block.vector
        def _(dve):
            o = Order(dve, s_dve)
            dve.sem_inc(s_rfree, 1)
            dve.sem_inc(s_arg, 2)
            o(dve.memset(C[:, HC:], 0.0))
            o(dve.memset(M[:, :], 0.0))
            dve.sem_inc(s_z, 1)
            dve.wait_ge(s_bbc, 16)
            dve.wait_ge(s_pm, HEADS)
            with dve.Fori(0, NTILE) as i:
                row = lambda t: t[:, bass.ds(i, 1), :].rearrange("p a n -> p (a n)")
                o.enter(i, 21)
                dve.wait_ge(s_r, i * 32 + 32)
                dve.wait_ge(s_tr, i * 3 + 1)
                dve.sem_inc(idle["dve"], 1)
                o(dve.tensor_tensor(C[:, 0:HC], Rb[:, :], Ra[:, :], ALU.subtract))
                dve.sem_inc(s_rfree, 1)
                dve.sem_inc(s_c, 1)
                o(dve.tensor_scalar(M[:, :], C[:, 0:HC], 0.0, -1e30, ALU.is_equal, ALU.mult))
                o(dve.tensor_reduce(degr[:, :], C[:, 0:HC], X, ALU.add))
                dve.sem_inc(idle["dve"], 1)
                dve.tensor_copy(k.deg[:, bass.ds(i, 1)], degr[:, :])
                dve.tensor_copy(ai[:, :], row(k.a))
                for h in range(HEADS):
                    dve.wait_ge(s_pm, i * HEADS + h + 1)
                    dve.sem_inc(idle["dve"], 1)
                    last = dve.tensor_tensor_reduce(Pb[:, h, :], bbc[:, h, :], M[:, :], 1.0, -3e38, ALU.add, ALU.max, bmax[:, h:h + 1])
                o(last)
                o(dve.tensor_tensor(bmax[:, :], bmax[:, :], ai[:, :], ALU.add))
                o(dve.scalar_tensor_tensor(top[:, :], bmax[:, :], 0.2, bmax[:, :], ALU.mult, ALU.max))
                o(dve.tensor_tensor(u16[:, 0:HEADS], ai[:, :], top[:, :], ALU.subtract))
                o(dve.scalar_tensor_tensor(u16[:, HEADS:], ai[:, :], 0.2, top[:, :], ALU.mult, ALU.subtract))
                dve.sem_inc(s_u, 1)

                def weights(h):
                    dve.wait_ge(s_e, i * HEADS + h + 1)
                    return dve.scalar_tensor_tensor(Pb[:, h, :], Pb[:, h, :], 1.0, C[:, 0:HC], ALU.mult, ALU.mult,
                                                    accum_out=asum[:, h:h + 1])
                for h in range(HEADS):
                    dve.wait_ge(s_t2, i * HEADS + h + 1)
                    dve.scalar_tensor_tensor(Pb[:, h, :], Pb[:, h, :], u16[:, h:h + 1], low[:, h % 2, :],
                                             ALU.add, ALU.max).then_inc(s_arg, 1)
                    if h:
                        o(weights(h - 1))
                o(weights(HEADS - 1))
                o(dve.tensor_scalar(asum[:, :], asum[:, :], 1e-16, None, ALU.add))
                o(dve.reciprocal(asum[:, :], asum[:, :]))
                dve.wait_ge(s_pm, i * HEADS + HEADS)
                dve.sem_inc(idle["dve"], 1)
                dve.tensor_tensor(xs[:, :, :], row(k.big1).rearrange("p (h c) -> p h c", c=CH),
                                  asum[:, :].unsqueeze(2).to_broadcast([P, HEADS, CH]), ALU.mult).then_inc(s_xs, 1)
                o(dve.tensor_scalar(dinv[:, :], degr[:, :], 1.0, None, ALU.max))
                o(dve.reciprocal(dinv[:, :], dinv[:, :]))
                o(dve.tensor_scalar(row(k.rD), asum[:, :], dinv[:, :], None, ALU.mult))
                o.leave(NTILE)
            dve.wait_ge(s_pm, HEADS * (NTILE + 1))
            o(dve.tensor_copy(k.oeT[:, :, 0:HYPER], OE[:, :, 0:HYPER]))

        @block.scalar
        def _(act):
            act.wait_ge(s_bbc, 16)
            act.sem_inc(s_ctfree, 1)
            act.wait_ge(s_fill, 16)
            with act.Fori(0, NTILE) as i:
                cols = bass.ds(i * STEP, STEP)
                act.wait_ge(s_sfree, i + 1)
                act.sem_inc(idle["act"], 1)
                act.activation(sidx[:, :], k.slot[:, 1, cols], ACT.Copy).then_inc(s_stage, 1)
                act.activation(spay[:, :, :], k.pay[:, 1, cols, :], ACT.Copy).then_inc(s_stage, 1)
                act.wait_ge(s_u, i + 1)
                for h in range(HEADS + 1):
                    if h < HEADS:
                        act.wait_ge(s_arg, i * HEADS + h + 1)
                        act.activation(low[:, h % 2, :], Pb[:, h, :], ACT.Identity, bias=u16[:, HEADS + h:HEADS + h + 1],
                                       scale=0.2).then_inc(s_t2, 1)
                    if h:
                        act.wait_ge(s_arg, i * HEADS + h + 2)
                        act.activation(Pb[:, h - 1, :], Pb[:, h - 1, :], ACT.Exp).then_inc(s_e, 1)
                act.wait_ge(s_ctfree, i + 1)
                act.sem_inc(idle["act"], 1)
                act.wait_ge(s_tr, i * 3 + 2)
                act.sem_inc(idle["act"], 1)
                act.activation(ctb[:, 0:4, :], pT[:, 0, :, :], ACT.Copy).then_inc(s_trc, 1)
                act.activation(ctb[:, 4:8, :], pT[:, 1, :, :], ACT.Copy).then_inc(s_trc, 1)
                act.wait_ge(s_tr, i * 3 + 4)
                act.sem_inc(idle["act"], 1)
                act.activation(ctb[:, 8:10, :], pT[:, 0, 0:2, :], ACT.Copy).then_inc(s_trc, 1)
                act.activation(urow[:, :], pT[0:2 * HEADS, 1, 0, :], ACT.Copy).then_inc(s_trc, 1)

        @block.tensor
        def _(pe):
            pe.sem_inc(s_tr, 1)
            pe.wait_ge(s_z, 1)
            for g in range(2):
                for c, w in banks(0, HC):
                    last = pe.matmul(OE[:, g, c:c + w], M[:, 0:P], M[:, c:c + w], start=True, stop=True)
            for h in range(HEADS):
                pe.sem_inc(s_pm, 1) if h else last.then_inc(s_pm, 1)
            pe.wait_ge(s_pm, HEADS)
            with pe.Fori(0, NTILE) as i:
                pe.wait_ge(s_c, i + 1)
                pe.sem_inc(idle["pe"], 1)
                for c in range(8):
                    last = pe.transpose(pT[:, c // 4, c % 4, :], C[:, c * P:(c + 1) * P], k.ident[:, :])
                last.then_inc(s_tr, 1)
                pe.wait_ge(s_trc, i * 4 + 2)
                pe.sem_inc(idle["pe"], 1)
                for c in range(8, HCH):
                    last = pe.transpose(pT[:, 0, c - 8, :], C[:, c * P:(c + 1) * P], k.ident[:, :])
                last.then_inc(s_tr, 1)
                last = pe.transpose(pT[0:2 * HEADS, 1, 0, :], u16[:, :], k.ident[:, :])
                last.then_inc(s_tr, 1)
                pe.wait_ge(s_xs, i + 1)
                pe.sem_inc(idle["pe"], 1)
                for h in range(HEADS):
                    g, j = divmod(h, 4)
                    for c, w in banks(0, HYPER):
                        last = pe.matmul(OE[CH * j:CH * j + CH, g, c:c + w], xs[:, h, :], Pb[:, h, c:c + w],
                                         start=False, stop=True, skip_group_check=True)
                    last.then_inc(s_pm, 1)


def phase_messages_back(nc, k):
    with ExitStack() as ctx:
        sb = lambda n, s, d: ctx.enter_context(nc.sbuf_tensor(n, s, d))
        ps = lambda n, s, d: ctx.enter_context(nc.psum_tensor(n, s, d))
        sem = k.sem
        NG, NL, NZ, SKEW = NTILE // 4, 4, 8, 3
        STEPS = HCH * HEADS
        oe = sb("oe", [P, HCH, FEAT], F32)
        b02 = sb("b02", [P, HCH, HEADS], F32)
        U = sb("U", [P, 2, 2 * HEADS, BANK], F32)
        CT = sb("CTs", [P, 2, HCH, BANK], F32)
        low = sb("lowD", [P, NL, BANK], F32)
        z = sb("z", [P, NZ, BANK], F32)
        flat = z[:, :, :].rearrange("p a n -> p (a n)")
        Rl, binv = flat[:, 0:HC], flat[:, 3 * BANK:3 * BANK + HYPER]
        ots = sb("ots", [P, 2, BANK], F32)
        pB = ps("pB", [P, 3 * BANK], F32)
        OT = ps("OT", [P, 2, BANK], F32)
        pN = ps("pN", [P, 4, FEAT], F32)

        s_R = sem("last_R_loaded")
        s_bc = sem("column_sums")
        s_sc = sem("oe_scaled")
        s_tp = sem("oe_transposed")
        s_oe = sem("oe_ready")
        s_ld = [sem("group_loaded0"), sem("group_loaded1")]
        s_gfree = sem("group_used")
        s_low = sem("low_ready_d")
        s_arg = sem("exponent_ready_d")
        s_cl = sem("exponent_clamped")
        s_e = sem("exp_ready_d")
        s_w = sem("weights_ready_d")
        s_mm = sem("summed_d")
        s_otc = sem("sums_copied")
        s_tr = sem("sums_transposed")
        s_y = sem("messages_stored")
        s_dve = sem("dve_order_d")
        idle = k.idle
        block = ctx.enter_context(nc.Block())

        @block.sync
        def _(sp):
            sp.dma_start(Rl, k.R[NTILE, :, :]).then_inc(s_R, 16)

            def load(g, u, w):
                cols = bass.ds(g * BANK, w)
                sp.wait_ge(s_gfree, g + 1)
                sp.sem_inc(idle["sp"], 1)
                sp.dma_start(U[:, u, :, 0:w], k.UT[:, cols].partition_broadcast(P)).then_inc(s_ld[u], 16)
                sp.dma_start(CT[:, u, :, 0:w], k.CT[:, :, cols].rearrange("c e n -> e c n")).then_inc(s_ld[u], 16)
            with sp.Fori(0, NG // 2) as i:
                for u in range(2):
                    load(i * 2 + u, u, BANK)
            load(NG, 0, P)

        def steps():
            return [(s, s // HEADS, s % HEADS) for s in range(STEPS)]

        @block.scalar
        def _(act):
            for g in range(2):
                act.wait_ge(s_tp, g + 1)
                for c0, n in ((0, 4), (4, 4), (8, 2)):
                    act.activation(oe[:, c0:c0 + n, g * P:(g + 1) * P],
                                   pB[:, c0 * P:(c0 + n) * P].rearrange("p (c n) -> p c n", c=n), ACT.Copy).then_inc(s_oe, 1)

            def group(g, u, loads, w):
                def exp(s):
                    act.wait_ge(s_cl, g * STEPS + s + 1)
                    act.activation(z[:, s % NZ, 0:w], z[:, s % NZ, 0:w], ACT.Exp).then_inc(s_e, 1)
                act.wait_ge(s_ld[u], loads)
                act.sem_inc(idle["act"], 1)
                for s, c, h in steps():
                    act.wait_ge(s_arg, g * STEPS + s + 1)
                    act.activation(low[:, s % NL, 0:w], U[:, u, HEADS + h, 0:w], ACT.Identity,
                                   bias=b02[:, c, h:h + 1]).then_inc(s_low, 1)
                    if s >= SKEW:
                        exp(s - SKEW)
                for s in range(STEPS - SKEW, STEPS):
                    exp(s)
                act.wait_ge(s_mm, g * STEPS + STEPS + NZ)
                act.sem_inc(idle["act"], 1)
                act.activation(ots[:, :, 0:w], OT[:, :, 0:w], ACT.Copy).then_inc(s_otc, 1)
            with act.Fori(0, NG // 2) as i:
                for u in range(2):
                    group(i * 2 + u, u, i * 32 + 32, BANK)
            group(NG, 0, 32 * (NG // 2) + 32, P)

        @block.gpsimd
        def _(pool):
            def group(g, w):
                for s, c, h in steps():
                    pool.wait_ge(s_arg, g * STEPS + s + 1 + NL)
                    pool.sem_inc(idle["pool"], 1)
                    pool.tensor_scalar(z[:, s % NZ, 0:w], z[:, s % NZ, 0:w], 0.0, None, ALU.min).then_inc(s_cl, 1)
            with pool.Fori(0, NG) as g:
                group(g, BANK)
            group(NG, P)

        @block.tensor
        def _(pe):
            pe.wait_ge(s_R, 16)
            for c, w in banks(0, HYPER):
                last = pe.matmul(pB[:, c:c + w], k.ones[:, :], Rl[:, c:c + w], start=True, stop=True)
            last.then_inc(s_bc, 1)
            pe.wait_ge(s_sc, 1)
            for g in range(2):
                if g:
                    pe.wait_ge(s_oe, 3)
                for c in range(HCH):
                    last = pe.transpose(pB[:, c * P:(c + 1) * P], k.oeT[:, g, c * P:(c + 1) * P], k.ident[:, :])
                last.then_inc(s_tp, 1)
            pe.wait_ge(s_oe, 6)

            def group(g, w):
                pe.wait_ge(s_otc, g + 1)
                pe.sem_inc(idle["pe"], 1)
                for s, c, h in steps():
                    j = h % 4
                    pe.wait_ge(s_w, g * STEPS + s + 1)
                    pe.matmul(OT[CH * j:CH * j + CH, h // 4, 0:w], oe[:, c, h * CH:(h + 1) * CH], z[:, s % NZ, 0:w],
                              start=(c == 0), stop=(c == HCH - 1)).then_inc(s_mm, 1)
                pe.wait_ge(s_otc, g + 2)
                pe.wait_ge(s_y, g + 1)
                pe.sem_inc(idle["pe"], 1)
                for q in range(w // P):
                    for g2 in range(2):
                        last = pe.transpose(pN[:, q, g2 * P:(g2 + 1) * P], ots[:, g2, q * P:(q + 1) * P], k.ident[:, :])
                last.then_inc(s_tr, 1)
            with pe.Fori(0, NG) as g:
                group(g, BANK)
            group(NG, P)

        @block.vector
        def _(dve):
            o = Order(dve, s_dve)
            dve.sem_inc(s_gfree, 2)
            dve.sem_inc(s_arg, NL)
            dve.sem_inc(s_mm, NZ)
            dve.sem_inc(s_otc, 1)
            dve.sem_inc(s_y, 1)
            o(dve.tensor_scalar(b02[:, :, :], k.bE[:, :, :], 0.2, None, ALU.mult))
            dve.wait_ge(s_bc, 1)
            o(dve.tensor_scalar(binv, pB[:, 0:HYPER], 1.0, None, ALU.max))
            o(dve.reciprocal(binv, binv))
            o(dve.tensor_tensor(k.oeT[:, :, 0:HYPER], k.oeT[:, :, 0:HYPER],
                                binv.unsqueeze(1).to_broadcast([P, 2, HYPER]), ALU.mult))
            o(dve.tensor_copy(k.oeT[:, :, HYPER:HC], k.oeT[:, :, HYPER - 1:HYPER]))
            o(dve.memset(k.oeT[:, :, HC:], 0.0))
            dve.sem_inc(s_sc, 1)

            def group(g, u, loads, w):
                def weights(s, c):
                    dve.wait_ge(s_e, g * STEPS + s + 1)
                    dve.tensor_tensor(z[:, s % NZ, 0:w], z[:, s % NZ, 0:w], CT[:, u, c, 0:w], ALU.mult).then_inc(s_w, 1)
                dve.wait_ge(s_ld[u], loads)
                dve.sem_inc(idle["dve"], 1)
                for s, c, h in steps():
                    dve.wait_ge(s_mm, g * STEPS + s + 1)
                    dve.wait_ge(s_low, g * STEPS + s + 1)
                    dve.scalar_tensor_tensor(z[:, s % NZ, 0:w], U[:, u, h, 0:w], k.bE[:, c, h:h + 1],
                                             low[:, s % NL, 0:w], ALU.add, ALU.max).then_inc(s_arg, 1)
                    if s >= SKEW:
                        weights(s - SKEW, (s - SKEW) // HEADS)
                for s in range(STEPS - SKEW, STEPS):
                    weights(s, s // HEADS)
                dve.wait_ge(s_w, g * STEPS + STEPS)
                dve.sem_inc(s_gfree, 1)
                n = w // P
                dve.wait_ge(s_tr, g + 1)
                dve.sem_inc(idle["dve"], 1)
                dve.tensor_tensor(k.big1[:, bass.ds(g * 4, n), :].rearrange("p i (h c) -> p i h c", c=CH),
                                  pN[:, 0:n, :].rearrange("p i (h c) -> p i h c", c=CH),
                                  k.rD[:, bass.ds(g * 4, n), :].unsqueeze(3).to_broadcast([P, n, HEADS, CH]),
                                  ALU.mult).then_inc(s_y, 1)
            with dve.Fori(0, NG // 2) as i:
                for u in range(2):
                    group(i * 2 + u, u, i * 32 + 32, BANK)
            group(NG, 0, 32 * (NG // 2) + 32, P)


def phase_first_norm(nc, k):
    with ExitStack() as ctx:
        sb = lambda n, s, d: ctx.enter_context(nc.sbuf_tensor(n, s, d))
        sem = k.sem
        K = 7
        xc = sb("xc", [P, 2, K, FEAT], F32)
        sq = sb("sq", [P, 2, K, FEAT], F32)
        mean = sb("mean", [P, NTILE], F32)
        var = sb("var", [P, NTILE], F32)
        dsq = sb("dsq", [P, NTILE], F32)
        s_x = [sem("xc_loaded0"), sem("xc_loaded1")]
        s_z = sem("xc_zeroed")
        s_used = sem("xc_used")
        s_v = sem("variance_ready")
        s_sd = sem("deviation_ready")
        s_h = sem("h_ready")
        s_st = [sem("h_stored0"), sem("h_stored1")]
        s_dve = sem("dve_order_n")
        block = ctx.enter_context(nc.Block())

        @block.sync
        def _(sp):
            for r in range(NTILE // K):
                u = r % 2
                if r < 2:
                    sp.wait_ge(s_z, 1)
                else:
                    sp.wait_ge(s_used, r - 1)
                full = K if r < NTILE // K - 1 else K - 1
                sp.dma_start(xc[:, u, 0:full, :], k.x[r * K * P:(r * K + full) * P, :].rearrange("(i p) n -> p i n", p=P)).then_inc(s_x[u], 16)
                if full < K:
                    sp.dma_start(xc[0:LAST, u, full, :], k.x[(NTILE - 1) * P:NODES, :]).then_inc(s_x[u], 16)
            for r in range(NTILE // K):
                sp.wait_ge(s_h, r + 1)
                sp.dma_start(k.H[r * K * P:(r + 1) * K * P, :].rearrange("(i p) n -> p i n", p=P), sq[:, r % 2, :, :]).then_inc(s_st[r % 2], 16)
            sp.wait_ge(s_st[0], 64)
            sp.wait_ge(s_st[1], 48)

        @block.scalar
        def _(act):
            act.wait_ge(s_v, 1)
            act.activation(var[:, :], var[:, :], ACT.Sqrt).then_inc(s_sd, 1)
            act.activation(dsq[:, :], dsq[:, :], ACT.Sqrt).then_inc(s_sd, 1)

        @block.vector
        def _(dve):
            o = Order(dve, s_dve)
            o(dve.memset(xc[:, :, :, :], 0.0))
            dve.sem_inc(s_z, 1)
            bc = lambda t, r: t[:, r * K:(r + 1) * K].unsqueeze(2).to_broadcast([P, K, FEAT])
            for r in range(NTILE // K):
                y = k.big1[:, r * K:(r + 1) * K, :]
                dve.wait_ge(s_x[r % 2], 16 * (r // 2 + 1) + (16 if r == NTILE // K - 1 else 0))
                o(dve.tensor_tensor(y, y, xc[:, r % 2, :, :], ALU.add))
                dve.sem_inc(s_used, 1)
                o(dve.tensor_reduce(mean[:, r * K:(r + 1) * K], y, X, ALU.add))
                o(dve.tensor_scalar(mean[:, r * K:(r + 1) * K], mean[:, r * K:(r + 1) * K], 1.0 / FEAT, None, ALU.mult))
                o(dve.tensor_tensor(y, y, bc(mean, r), ALU.subtract))
                o(dve.tensor_tensor(sq[:, 0, :, :], y, y, ALU.mult))
                o(dve.tensor_reduce(var[:, r * K:(r + 1) * K], sq[:, 0, :, :], X, ALU.add))
            o(dve.tensor_scalar(var[:, :], var[:, :], 1.0 / FEAT, EPS_LN, ALU.mult, ALU.add))
            o(dve.tensor_scalar(dsq[:, :], k.deg[:, :], 1.0, None, ALU.max))
            dve.sem_inc(s_v, 1)
            dve.wait_ge(s_sd, 2)
            o(dve.reciprocal(var[:, :], var[:, :]))
            o(dve.reciprocal(dsq[:, :], dsq[:, :]))
            for r in range(NTILE // K):
                y = k.big1[:, r * K:(r + 1) * K, :]
                o(dve.tensor_tensor(y, y, bc(var, r), ALU.mult))
                if r >= 2:
                    dve.wait_ge(s_st[r % 2], 16 * (r // 2))
                dve.tensor_tensor(sq[:, r % 2, :, :], y, bc(dsq, r), ALU.mult).then_inc(s_h, 1)


def phase_gather(nc, k):
    with ExitStack() as ctx:
        sb = lambda n, s, d: ctx.enter_context(nc.sbuf_tensor(n, s, d))
        ps = lambda n, s, d: ctx.enter_context(nc.psum_tensor(n, s, d))
        sem = k.sem
        Q = 8
        edges = sb("edgesT", [P, NT, 2], F32)
        tab = sb("tabrowT", [1, NTM], I32)
        idx = sb("idx", [P, 2, Q], I32)
        oh = sb("ohT", [P, 2, Q, P], F32)
        rows = sb("rows", [P, 2, Q, FEAT], F32)
        zero = sb("zeroE", [P, ZCOLS], F32)
        pm = ps("pm", [P, Q, BANK], F32)
        s_z = sem("zeroE_ready")
        s_zf = sem("expert_inputs_zeroed")
        s_in = sem("target_slots_loaded")
        s_m0 = sem("m_zeroed")
        s_idx = sem("idx_ready")
        s_oh = sem("oh_ready")
        s_g = [sem("rows_gathered0"), sem("rows_gathered1")]
        s_mm = sem("rows_summed")
        s_add = sem("m_added")
        idle = k.idle
        block = ctx.enter_context(nc.Block())
        NI = NT // Q

        @block.sync
        def _(sp):
            sp.dma_start(edges[:, :, :], k.DS.rearrange("(p t) c -> p t c", p=P)).then_inc(s_in, 16)
            sp.dma_start(tab[:, :], k.tab[1:2, :]).then_inc(s_in, 16)
            sp.wait_ge(s_z, 1)
            flat = k.xbuf.rearrange("(p r) n -> p (r n)", p=P)
            for c in range(MT * FEAT // ZCOLS):
                sp.dma_start(flat[:, c * ZCOLS:(c + 1) * ZCOLS], zero[:, :]).then_inc(s_zf, 16)
            sp.wait_ge(s_zf, 16 * (MT * FEAT // ZCOLS))

        @block.gpsimd
        def _(pool):
            bound = pool.to_reg(NTILE * P - 1)
            with pool.Fori(0, NI // 2) as i:
                for u in range(2):
                    pool.wait_ge(s_idx, i * 2 + u + 1)
                    pool.sem_inc(idle["pool"], 1)
                    for q in range(Q):
                        pool.indirect_dma_start(rows[:, u, q, :], None, k.H[:, :],
                                                bass.IndirectOffsetOnAxis(ap=idx[:, u, q:q + 1], axis=0),
                                                bounds_check=bound).then_inc(s_g[u], 16)

        @block.tensor
        def _(pe):
            with pe.Fori(0, NI // 2) as i:
                for u in range(2):
                    n = i * 2 + u
                    pe.wait_ge(s_oh, n + 1)
                    pe.wait_ge(s_g[u], i * (16 * Q) + 16 * Q)
                    pe.sem_inc(idle["pe"], 1)
                    for q in range(Q):
                        pe.wait_ge(s_add, n * Q + q + 1)
                        pe.sem_inc(idle["pe"], 1)
                        pe.matmul(pm[:, q, 0:FEAT], oh[:, u, q, :], rows[:, u, q, :], start=True, stop=True)
                        pe.matmul(pm[:, q, FEAT:FEAT + 1], oh[:, u, q, :], k.ones[:, 0:1], start=True, stop=True).then_inc(s_mm, 1)

        @block.vector
        def _(dve):
            dve.sem_inc(s_add, Q)
            dve.memset(zero[:, :], 0.0).then_inc(s_z, 1)
            dve.memset(k.big2[:, :, :], 0.0).then_inc(s_m0, 1)
            dve.wait_ge(s_m0, 1)
            dve.wait_ge(s_in, 32)

            def prepare(n, u):
                cols = bass.ds(n * Q, Q)
                dve.tensor_copy(idx[:, u, :], edges[:, cols, 1]).then_inc(s_idx, 1)
                dve.tensor_tensor(oh[:, u, :, :], k.iota[:, :].unsqueeze(1).to_broadcast([P, Q, P]),
                                  edges[:, cols, 0:1].to_broadcast([P, Q, P]), ALU.is_equal).then_inc(s_oh, 1)

            def add(n, u):
                for q in range(Q):
                    b = dve.value_load(tab[0:1, bass.ds(n * Q + q, 1)], min_val=0, max_val=NTILE - 1)
                    m = k.big2[:, bass.ds(b, 1), :].rearrange("p a n -> p (a n)")
                    dve.wait_ge(s_mm, n * Q + q + 1)
                    dve.wait_ge(s_add, n * Q + q + Q)
                    dve.sem_inc(idle["dve"], 1)
                    dve.tensor_tensor(m, m, pm[:, q, 0:FEAT + 1], ALU.add).then_inc(s_add, 1)
            for u in range(2):
                prepare(u, u)
            with dve.Fori(0, NI // 2 - 1) as i:
                for u in range(2):
                    add(i * 2 + u, u)
                    prepare(i * 2 + u + 2, u)
            for u in range(2):
                add(NI - 2 + u, u)


def phase_route(nc, k):
    with ExitStack() as ctx:
        sb = lambda n, s, d: ctx.enter_context(nc.sbuf_tensor(n, s, d))
        ps = lambda n, s, d: ctx.enter_context(nc.psum_tensor(n, s, d))
        sem = k.sem
        G, E = 7, EXPERTS
        Wc = sb("Wc", [P, 4, FEAT], F32)
        Wg = sb("Wg", [P, 2, E], F32)
        bias = sb("bias3", [P, 2, FEAT], F32)
        bg = sb("bgb", [P, E], F32)
        din = sb("din", [P, NTILE], F32)
        st = sb("st", [P, 2, 4, P], F32)
        sT = sb("sT", [P, 2, 4, P], F32)
        x3 = sb("x3", [P, 2, FEAT], F32)
        x3T = sb("x3T", [P, 2, 2, P], F32)
        L = sb("L", [P, NTILE, E], F32)
        A = [sb("A0", [P, NTILE, E], F32), sb("A1", [P, NTILE, E], F32)]
        T = sb("T", [P, NTILE, E], F32)
        rank = sb("rank", [P, NTILE, E], F32)
        before = sb("before", [P, NTILE + 1, E], F32)
        v = sb("v", [P, 2, NTILE], F32)
        first = sb("first", [P, NTILE], F32)
        valid = sb("valid", [P, NTILE], F32)
        rowmask = sb("rowmask", [P, 1], F32)
        e3 = sb("e3", [P, 3, E], F32)
        e3i = sb("e3i", [P, E], I32)
        tn2 = sb("tn2", [P, 2], F32)
        cmp2 = sb("cmp2", [P, 2, E], F32)
        t2f = sb("t2f", [P, 2], F32)
        t2i = sb("t2i", [P, 2], I32)
        pT = ps("pTf", [P, 2, 4, P], F32)
        pX = ps("pXf", [P, 2, BANK], F32)
        p3 = ps("p3", [P, 2, 2, P], F32)
        pL = ps("pL", [P, 2, E], F32)
        pR = ps("pR", [P, BANK], F32)
        pS = ps("pS", [P, BANK], F32)

        s_w = sem("f_weights_loaded")
        s_cst = sem("f_constants")
        s_sq = sem("indegree_root")
        s_din = sem("indegree_ready")
        s_m = sem("m_staged")
        s_x = sem("x2_staged")
        s_tr = sem("f_transposed")
        s_sT = sem("f_transposes_copied")
        s_mm = sem("x3_summed")
        s_x3 = sem("x3_ready")
        s_tr3 = sem("x3_transposed")
        s_x3T = sem("x3T_ready")
        s_lg = sem("logits_summed")
        s_keep = sem("x3_kept")
        s_L = sem("logits_ready")
        s_dv = sem("gate_difference")
        s_ex = sem("gate_exp")
        s_A = sem("choices_ready")
        s_pr = sem("prefix_summed")
        s_prc = sem("prefix_copied")
        s_tab = sem("expert_table_ready")
        s_out = sem("expert_table_stored")
        s_dve = sem("dve_order_f")
        idle = k.idle
        block = ctx.enter_context(nc.Block())

        def tiles(eng, body):
            with eng.Fori(0, NTILE // 2) as i:
                for u in range(2):
                    body(i * 2 + u, u)
            body(NTILE - 1, 0)

        @block.sync
        def _(sp):
            sp.dma_start(Wc[:, 0:2, :], k.W_gc.rearrange("(c p) n -> p c n", p=P)).then_inc(s_w, 16)
            sp.dma_start(Wc[:, 2:4, :], k.W_res.rearrange("(c p) n -> p c n", p=P)).then_inc(s_w, 16)
            sp.dma_start(Wg[:, :, :], k.Wg.rearrange("(c p) n -> p c n", p=P)).then_inc(s_w, 16)
            sp.dma_start(bias[:, 0, :], k.b_gc.partition_broadcast(P)).then_inc(s_w, 16)
            sp.dma_start(bias[:, 1, :], k.b_res.partition_broadcast(P)).then_inc(s_w, 16)
            sp.dma_start(bg[:, :], k.bg.partition_broadcast(P)).then_inc(s_w, 16)
            sp.wait_ge(s_tab, 1)
            sp.dma_start(k.etab.rearrange("a (p t) -> (a p) t", p=P), t2i[:, :]).then_inc(s_out, 16)
            sp.wait_ge(s_out, 16)

        @block.gpsimd
        def _(pool):
            pool.iota(tn2[:, :], [[1, 2]], base=0, channel_multiplier=2,
                      allow_small_or_imprecise_dtypes=True).then_inc(s_cst, 1)
            pool.affine_select(out=rowmask[:, :], in_=k.ones[:, 0:1], compare_op=ALU.is_ge, fill=0.0,
                               base=LAST - 1, pattern=[[0, 1]], channel_multiplier=-1).then_inc(s_cst, 1)

            def body(t, u):
                pool.wait_ge(s_tr, t + 1)
                pool.sem_inc(idle["pool"], 1)
                pool.tensor_copy(st[:, u, 2:4, :].rearrange("p c n -> p (c n)"),
                                 k.big1[:, bass.ds(t, 1), :].rearrange("p a n -> p (a n)")).then_inc(s_x, 1)
            tiles(pool, body)

        @block.tensor
        def _(pe):
            pe.wait_ge(s_w, 96)
            pe.sem_inc(s_tr, 2)
            pe.sem_inc(s_mm, 2)

            def body(t, u):
                pe.wait_ge(s_m, t + 1)
                pe.wait_ge(s_x, t + 1)
                pe.wait_ge(s_sT, t + 1)
                pe.sem_inc(idle["pe"], 1)
                for c in range(4):
                    last = pe.transpose(pT[:, u, c, :], st[:, u, c, :], k.ident[:, :])
                last.then_inc(s_tr, 1)
                pe.wait_ge(s_sT, t + 3)
                pe.wait_ge(s_x3, t + 1)
                pe.sem_inc(idle["pe"], 1)
                for c in range(4):
                    last = pe.matmul(pX[:, u, 0:FEAT], sT[:, u, c, :], Wc[:, c, :], start=(c == 0), stop=(c == 3))
                last.then_inc(s_mm, 1)
                pe.wait_ge(s_x3, t + 3)
                pe.wait_ge(s_x3T, t + 1)
                pe.sem_inc(idle["pe"], 1)
                for c in range(2):
                    last = pe.transpose(p3[:, u, c, :], x3[:, u, c * P:(c + 1) * P], k.ident[:, :])
                last.then_inc(s_tr3, 1)
                pe.wait_ge(s_x3T, t + 3)
                pe.wait_ge(s_L, t + 1)
                pe.sem_inc(idle["pe"], 1)
                for c in range(2):
                    last = pe.matmul(pL[:, u, :], x3T[:, u, c, :], Wg[:, c, :], start=(c == 0), stop=(c == 1))
                last.then_inc(s_lg, 1)
            tiles(pe, body)
            pe.wait_ge(s_A, 1)
            for r in range(NTILE // G):
                rhs = T[:, r * G:(r + 1) * G, :].rearrange("p i e -> p (i e)")
                if r:
                    pe.wait_ge(s_prc, 2 * r)
                pe.matmul(pR[:, 0:G * E], k.upper[:, :], rhs, start=True, stop=True)
                pe.matmul(pS[:, 0:G * E], k.ones[:, :], rhs, start=True, stop=True).then_inc(s_pr, 1)

        @block.scalar
        def _(act):
            act.sem_inc(s_sT, 2)
            act.sem_inc(s_x3T, 2)
            act.sem_inc(s_keep, 2)
            act.wait_ge(s_sq, 1)
            act.activation(din[:, :], din[:, :], ACT.Sqrt).then_inc(s_sq, 1)

            def body(t, u):
                act.wait_ge(s_mm, t + 1)
                act.wait_ge(s_tr, t + 3)
                act.sem_inc(idle["act"], 1)
                act.activation(sT[:, u, :, :], pT[:, u, :, :], ACT.Copy).then_inc(s_sT, 1)
                act.wait_ge(s_x3, t + 3)
                act.sem_inc(idle["act"], 1)
                act.activation(k.big2[:, bass.ds(t, 1), 0:FEAT].rearrange("p a n -> p (a n)"), x3[:, u, :],
                               ACT.Copy).then_inc(s_keep, 1)
                act.wait_ge(s_tr3, t + 1)
                act.sem_inc(idle["act"], 1)
                act.activation(x3T[:, u, :, :], p3[:, u, :, :], ACT.Copy).then_inc(s_x3T, 1)
            tiles(act, body)
            act.wait_ge(s_dv, 1)
            act.activation(k.gate[:, 1, :], v[:, 1, :], ACT.Exp).then_inc(s_ex, 1)

        @block.vector
        def _(dve):
            o = Order(dve, s_dve)
            dve.sem_inc(s_x3, 2)
            dve.sem_inc(s_L, 2)
            o(dve.tensor_scalar(din[:, :], k.big2[:, :, FEAT], 1.0, None, ALU.max))
            dve.sem_inc(s_sq, 1)
            dve.wait_ge(s_sq, 2)
            o(dve.reciprocal(din[:, :], din[:, :]))
            dve.wait_ge(s_w, 96)
            o(dve.tensor_tensor(bias[:, 0, :], bias[:, 0, :], bias[:, 1, :], ALU.add))

            def stage(t, u):
                dve.wait_ge(s_tr, t + 1)
                dve.sem_inc(idle["dve"], 1)
                dve.tensor_scalar(st[:, u, 0:2, :].rearrange("p c n -> p (c n)"),
                                  k.big2[:, bass.ds(t, 1), 0:FEAT].rearrange("p a n -> p (a n)"),
                                  din[:, bass.ds(t, 1)], None, ALU.mult).then_inc(s_m, 1)

            def body(t, u):
                stage(t, u)
                dve.wait_ge(s_mm, t + 3)
                dve.wait_ge(s_keep, t + 1)
                dve.sem_inc(idle["dve"], 1)
                dve.tensor_tensor(x3[:, u, :], pX[:, u, 0:FEAT], bias[:, 0, :], ALU.add).then_inc(s_x3, 1)
                dve.wait_ge(s_lg, t + 1)
                dve.sem_inc(idle["dve"], 1)
                dve.tensor_tensor(L[:, bass.ds(t, 1), :].rearrange("p a n -> p (a n)"), pL[:, u, :], bg[:, :],
                                  ALU.add).then_inc(s_L, 1)
            tiles(dve, body)
            dve.wait_ge(s_L, NTILE + 2)
            dve.wait_ge(s_cst, 2)
            wide = lambda t: t.unsqueeze(2).to_broadcast([P, NTILE, E])
            num = k.iota[:, 0:E].unsqueeze(1).to_broadcast([P, NTILE, E])
            for j in range(2):
                o(dve.tensor_reduce(v[:, j, :], L[:, :, :], X, ALU.max))
                o(dve.tensor_tensor(T[:, :, :], L[:, :, :], wide(v[:, j, :]), ALU.is_lt))
                o(dve.scalar_tensor_tensor(T[:, :, :], T[:, :, :], 1024.0, num, ALU.mult, ALU.add))
                o(dve.tensor_reduce(first[:, :], T[:, :, :], X, ALU.min))
                o(dve.tensor_tensor(A[j][:, :, :], num, wide(first[:, :]), ALU.is_equal))
                if j == 0:
                    o(dve.scalar_tensor_tensor(L[:, :, :], A[0][:, :, :], -1e30, L[:, :, :], ALU.mult, ALU.add))
                o(dve.tensor_scalar(A[j][:, NTILE - 1, :], A[j][:, NTILE - 1, :], rowmask[:, :], None, ALU.mult))
            o(dve.tensor_tensor(v[:, 1, :], v[:, 1, :], v[:, 0, :], ALU.subtract))
            dve.sem_inc(s_dv, 1)
            o(dve.tensor_tensor(T[:, :, :], A[0][:, :, :], A[1][:, :, :], ALU.add))
            dve.sem_inc(s_A, 1)
            for r in range(NTILE // G):
                dve.wait_ge(s_pr, r + 1)
                dve.tensor_copy(rank[:, r * G:(r + 1) * G, :].rearrange("p i e -> p (i e)"), pR[:, 0:G * E]).then_inc(s_prc, 1)
                dve.tensor_copy(before[:, r * G + 1:(r + 1) * G + 1, :].rearrange("p i e -> p (i e)"),
                                pS[:, 0:G * E]).then_inc(s_prc, 1)
            dve.wait_ge(s_prc, 2 * (NTILE // G))
            o(dve.memset(before[:, 0, :], 0.0))
            with dve.Fori(0, NTILE) as t:
                o.enter(t, 1)
                at = lambda d: before[:, bass.ds(t + d, 1), :].rearrange("p a n -> p (a n)")
                o(dve.tensor_tensor(at(1), at(1), at(0), ALU.add))
                dve.sem_inc(idle["dve"], 1)
                o.leave(NTILE)
            o(dve.tensor_tensor(rank[:, :, :], rank[:, :, :], before[:, 0:NTILE, :], ALU.add))
            o(dve.tensor_scalar(e3[:, 0, :], before[:, NTILE, :], float(CAP), float(P - 1), ALU.min, ALU.add))
            o(dve.tensor_copy(e3i[:, :], e3[:, 0, :]))
            o(dve.tensor_scalar(e3i[:, :], e3i[:, :], 7, None, ALU.arith_shift_right))
            o(dve.tensor_copy(e3[:, 0, :], e3i[:, :]))
            o(dve.tensor_tensor_scan(e3[:, 1, :], k.ones[:, 0:E], e3[:, 0, :], 0.0, ALU.mult, ALU.add))
            o(dve.tensor_tensor(e3[:, 2, :], e3[:, 1, :], e3[:, 0, :], ALU.subtract))
            o(dve.tensor_scalar(e3[:, 2, :], e3[:, 2, :], float(P), None, ALU.mult))
            o(dve.tensor_tensor(cmp2[:, :, :], e3[:, 1, :].unsqueeze(1).to_broadcast([P, 2, E]),
                                tn2[:, :].unsqueeze(2).to_broadcast([P, 2, E]), ALU.is_le))
            o(dve.tensor_reduce(t2f[:, :], cmp2[:, :, :], X, ALU.add))
            o(dve.tensor_scalar(t2f[:, :], t2f[:, :], float(E - 1), None, ALU.min))
            o(dve.tensor_copy(t2i[:, :], t2f[:, :]))
            dve.sem_inc(s_tab, 1)
            dve.wait_ge(s_ex, 1)
            o(dve.tensor_scalar(k.gate[:, 0, :], k.gate[:, 1, :], 1.0, None, ALU.add))
            o(dve.reciprocal(k.gate[:, 0, :], k.gate[:, 0, :]))
            o(dve.tensor_tensor(k.gate[:, 1, :], k.gate[:, 1, :], k.gate[:, 0, :], ALU.mult))
            o(dve.tensor_scalar(L[:, :, :], rank[:, :, :], float(CAP), None, ALU.is_lt))
            o(dve.tensor_tensor(rank[:, :, :], rank[:, :, :], e3[:, 2, :].unsqueeze(1).to_broadcast([P, NTILE, E]), ALU.add))
            for j in range(2):
                o(dve.tensor_tensor(T[:, :, :], A[j][:, :, :], L[:, :, :], ALU.mult))
                o(dve.tensor_reduce(valid[:, :], T[:, :, :], X, ALU.add))
                o(dve.tensor_tensor(T[:, :, :], T[:, :, :], rank[:, :, :], ALU.mult))
                o(dve.tensor_reduce(k.gidx[:, :, j], T[:, :, :], X, ALU.add))
                o(dve.tensor_tensor(k.gate[:, j, :], k.gate[:, j, :], valid[:, :], ALU.mult))
                o(dve.tensor_scalar(valid[:, :], valid[:, :], -SKIP, SKIP, ALU.mult, ALU.add))
                o(dve.tensor_tensor(k.sidx[:, :, j], k.gidx[:, :, j], valid[:, :], ALU.add))


def phase_dispatch(nc, k):
    with ExitStack() as ctx:
        sb = lambda n, s, d: ctx.enter_context(nc.sbuf_tensor(n, s, d))
        sem = k.sem
        idx = sb("didx", [P, 2, 2], I32)
        rows = sb("drows", [P, 2, FEAT], F32)
        s_st = sem("rows_staged")
        s_sc = [sem("rows_scattered0"), sem("rows_scattered1")]
        idle = k.idle
        block = ctx.enter_context(nc.Block())

        @block.scalar
        def _(act):
            def stage(t, u, used):
                if used is not None:
                    act.wait_ge(s_sc[u], used)
                    act.sem_inc(idle["act"], 1)
                act.activation(idx[:, u, :], k.sidx[:, bass.ds(t, 1), :].rearrange("p a n -> p (a n)"), ACT.Copy).then_inc(s_st, 1)
                act.activation(rows[:, u, :], k.big2[:, bass.ds(t, 1), 0:FEAT].rearrange("p a n -> p (a n)"), ACT.Copy).then_inc(s_st, 1)
            for u in range(2):
                stage(u, u, None)
            with act.Fori(1, NTILE // 2) as i:
                for u in range(2):
                    stage(i * 2 + u, u, i * 32)
            stage(NTILE - 1, 0, 32 * (NTILE // 2))

        @block.gpsimd
        def _(pool):
            bound = pool.to_reg(MT * P - 1)

            def scatter(t, u):
                pool.wait_ge(s_st, t * 2 + 2)
                pool.sem_inc(idle["pool"], 1)
                for j in range(2):
                    pool.indirect_dma_start(k.xbuf[:, :], bass.IndirectOffsetOnAxis(ap=idx[:, u, j:j + 1], axis=0),
                                            rows[:, u, :], None, bounds_check=bound, oob_is_err=False).then_inc(s_sc[u], 16)
            with pool.Fori(0, NTILE // 2) as i:
                for u in range(2):
                    scatter(i * 2 + u, u)
            scatter(NTILE - 1, 0)
            pool.wait_ge(s_sc[0], 32 * (NTILE // 2 + 1))
            pool.wait_ge(s_sc[1], 32 * (NTILE // 2))


def phase_experts(nc, k):
    with ExitStack() as ctx:
        sb = lambda n, s, d: ctx.enter_context(nc.sbuf_tensor(n, s, d))
        ps = lambda n, s, d: ctx.enter_context(nc.psum_tensor(n, s, d))
        sem = k.sem
        HK = HID // P
        tab = sb("etab", [1, 2 * P], I32)
        b1r = sb("b1r", [EXPERTS, HID], F32)
        b1T = sb("b1T", [P, HK, EXPERTS], F32)
        w1 = sb("w1", [P, 2, 2, HID], F32)
        w2 = sb("w2", [P, 2, HK, FEAT], F32)
        b2 = sb("b2", [1, 2, FEAT], F32)
        xt = sb("xt", [P, 2, FEAT], F32)
        xT = sb("xTe", [P, 2, 2, P], F32)
        hT = sb("hT", [P, 2, HK, P], F32)
        y = sb("ye", [P, 2, FEAT], F32)
        pT = ps("pTe", [P, 2, BANK], F32)
        pH = ps("pH", [P, 2, HK, P], F32)
        pY = ps("pY", [P, 2, BANK], F32)
        s_in = sem("expert_tables_loaded")
        s_bt = sem("b1_transposed")
        s_b = sem("b1T_ready")
        s_ld = [sem("expert_loaded0"), sem("expert_loaded1")]
        s_tr = sem("xt_transposed")
        s_xT = sem("xTe_ready")
        s_h = sem("hidden_summed")
        s_g = sem("gelu_ready")
        s_y = sem("outputs_summed")
        s_yc = sem("outputs_copied")
        s_st = [sem("outputs_stored0"), sem("outputs_stored1")]
        s_yfree = sem("output_buffer_free")
        idle = k.idle
        block = ctx.enter_context(nc.Block())

        def tiles(eng, body):
            with eng.Fori(0, MT // 2) as i:
                for u in range(2):
                    body(i * 2 + u, u, i)
            body(MT - 1, 0, MT // 2)

        @block.sync
        def _(sp):
            sp.dma_start(tab[:, :], k.etab[:, :]).then_inc(s_in, 16)
            sp.dma_start(b1r[:, :], k.b1[:, :]).then_inc(s_in, 16)
            sp.wait_ge(s_in, 32)

            def load(t, u, i):
                e = sp.value_load(tab[0:1, bass.ds(t, 1)], min_val=0, max_val=EXPERTS - 1)
                sp.wait_ge(s_y, t + 1)
                sp.sem_inc(idle["sp"], 1)
                sp.dma_start(xt[:, u, :], k.xbuf[bass.ds(t * P, P), :]).then_inc(s_ld[u], 16)
                sp.dma_start(w1[:, u, :, :], k.w1[bass.ds(e, 1), :, :].rearrange("a (c p) n -> p (a c) n", p=P)).then_inc(s_ld[u], 16)
                sp.dma_start(w2[:, u, :, :], k.w2[bass.ds(e, 1), :, :].rearrange("a (c p) n -> p (a c) n", p=P)).then_inc(s_ld[u], 16)
                sp.dma_start(b2[:, u, :], k.b2[bass.ds(e, 1), :]).then_inc(s_ld[u], 16)
            tiles(sp, load)

        @block.tensor
        def _(pe):
            pe.wait_ge(s_in, 32)
            for c in range(HK):
                last = pe.transpose(pT[:, 0, c * EXPERTS:(c + 1) * EXPERTS], b1r[:, c * P:(c + 1) * P],
                                    k.ident[0:EXPERTS, 0:EXPERTS])
            last.then_inc(s_bt, 1)
            pe.sem_inc(s_y, 2)
            pe.sem_inc(s_h, 2)
            pe.wait_ge(s_b, 1)

            def body(t, u, i):
                pe.wait_ge(s_ld[u], i * 64 + 64)
                pe.wait_ge(s_xT, t + 1)
                pe.sem_inc(idle["pe"], 1)
                for c in range(2):
                    last = pe.transpose(pT[:, u, c * P:(c + 1) * P], xt[:, u, c * P:(c + 1) * P], k.ident[:, :])
                last.then_inc(s_tr, 1)
                pe.wait_ge(s_xT, t + 3)
                pe.wait_ge(s_g, t + 1)
                pe.sem_inc(idle["pe"], 1)
                for c in range(HK):
                    for d in range(2):
                        last = pe.matmul(pH[:, u, c, :], w1[:, u, d, c * P:(c + 1) * P], xT[:, u, d, :],
                                         start=(d == 0), stop=(d == 1))
                last.then_inc(s_h, 1)
                pe.wait_ge(s_g, t + 3)
                pe.wait_ge(s_yc, t + 1)
                pe.sem_inc(idle["pe"], 1)
                pe.matmul(pY[:, u, 0:FEAT], k.ones[0:1, :], b2[:, u, :], start=True, stop=False)
                for c in range(HK):
                    last = pe.matmul(pY[:, u, 0:FEAT], hT[:, u, c, :], w2[:, u, c, :], start=False, stop=(c == HK - 1))
                last.then_inc(s_y, 1)
            tiles(pe, body)

        @block.scalar
        def _(act):
            act.wait_ge(s_in, 32)
            act.sem_inc(s_g, 2)
            act.wait_ge(s_b, 1)

            def body(t, u, i):
                e = act.value_load(tab[0:1, bass.ds(t, 1)], min_val=0, max_val=EXPERTS - 1)
                act.wait_ge(s_h, t + 3)
                act.wait_ge(s_y, t + 1)
                act.sem_inc(idle["act"], 1)
                for c in range(HK):
                    last = act.activation(hT[:, u, c, :], pH[:, u, c, :], ACT.Gelu, bias=b1T[:, c, bass.ds(e, 1)])
                last.then_inc(s_g, 1)
            tiles(act, body)

        @block.vector
        def _(dve):
            dve.wait_ge(s_bt, 1)
            dve.tensor_copy(b1T[:, :, :].rearrange("p c e -> p (c e)"), pT[:, 0, 0:HK * EXPERTS]).then_inc(s_b, 1)
            dve.sem_inc(s_xT, 2)
            dve.sem_inc(s_yc, 2)

            def body(t, u, i):
                dve.wait_ge(s_tr, t + 1)
                dve.wait_ge(s_h, t + 1)
                dve.tensor_copy(xT[:, u, :, :].rearrange("p c n -> p (c n)"), pT[:, u, 0:FEAT]).then_inc(s_xT, 1)
                dve.wait_ge(s_y, t + 3)
                dve.wait_ge(s_yfree, t + 1)
                dve.tensor_copy(y[:, u, :], pY[:, u, 0:FEAT]).then_inc(s_yc, 1)
            tiles(dve, body)

        @block.gpsimd
        def _(pool):
            pool.sem_inc(s_yfree, 1)

            def body(t, u, i):
                pool.wait_ge(s_yc, t + 3)
                pool.sem_inc(idle["pool"], 1)
                pool.dma_start(k.ybuf[bass.ds(t * P, P), :], y[:, u, :]).then_inc(s_st[u], 16)
                if isinstance(t, int) and t == MT - 1:
                    return
                if u == 0:
                    pool.wait_ge(s_st[0], i * 16 + 16)
                else:
                    pool.wait_ge(s_st[1], i * 16 + 16)
                pool.sem_inc(s_yfree, 1)
            tiles(pool, body)
            pool.wait_ge(s_st[0], 16 * (MT // 2 + 1))
            pool.wait_ge(s_st[1], 16 * (MT // 2))


def phase_combine(nc, k):
    with ExitStack() as ctx:
        sb = lambda n, s, d: ctx.enter_context(nc.sbuf_tensor(n, s, d))
        sem = k.sem
        idx = sb("cidx", [P, 2, 2], I32)
        rows = sb("crows", [P, 2, 2, FEAT], F32)
        s_idx = sem("cidx_ready")
        s_g = [sem("y_gathered0"), sem("y_gathered1")]
        s_add = sem("y_added")
        idle = k.idle
        block = ctx.enter_context(nc.Block())

        @block.gpsimd
        def _(pool):
            bound = pool.to_reg(MT * P - 1)

            def gather(t, u):
                pool.wait_ge(s_idx, t + 1)
                pool.sem_inc(idle["pool"], 1)
                for j in range(2):
                    pool.indirect_dma_start(rows[:, u, j, :], None, k.ybuf[:, :],
                                            bass.IndirectOffsetOnAxis(ap=idx[:, u, j:j + 1], axis=0),
                                            bounds_check=bound).then_inc(s_g[u], 16)
            with pool.Fori(0, NTILE // 2) as i:
                for u in range(2):
                    gather(i * 2 + u, u)
            gather(NTILE - 1, 0)

        @block.vector
        def _(dve):
            def prepare(t, u):
                dve.tensor_copy(idx[:, u, :], k.gidx[:, bass.ds(t, 1), :].rearrange("p a n -> p (a n)")).then_inc(s_idx, 1)

            def add(t, u, i):
                y = k.big2[:, bass.ds(t, 1), 0:FEAT].rearrange("p a n -> p (a n)")
                dve.wait_ge(s_g[u], i * 32 + 32)
                dve.sem_inc(idle["dve"], 1)
                for j in range(2):
                    dve.scalar_tensor_tensor(y, rows[:, u, j, :], k.gate[:, j, bass.ds(t, 1)], y, ALU.mult, ALU.add).then_inc(s_add, 1)
                    dve.wait_ge(s_add, t * 2 + j + 1)
                    dve.sem_inc(idle["dve"], 1)
            for u in range(2):
                prepare(u, u)
            with dve.Fori(0, NTILE // 2 - 1) as i:
                for u in range(2):
                    add(i * 2 + u, u, i)
                    prepare(i * 2 + u + 2, u)
            add(NTILE - 3, 0, NTILE // 2 - 1)
            prepare(NTILE - 1, 0)
            add(NTILE - 2, 1, NTILE // 2 - 1)
            add(NTILE - 1, 0, NTILE // 2)


def phase_last_norm(nc, k):
    with ExitStack() as ctx:
        sb = lambda n, s, d: ctx.enter_context(nc.sbuf_tensor(n, s, d))
        ps = lambda n, s, d: ctx.enter_context(nc.psum_tensor(n, s, d))
        sem = k.sem
        K = 7
        NR = NTILE // K
        mask = sb("maskL", [P, 1], F32)
        eps = sb("epsL", [P, 1], F32)
        col = sb("col", [P, FEAT], F32)
        col2 = sb("col2", [P, FEAT], F32)
        mean = sb("meanL", [P, FEAT], F32)
        scale = sb("scaleL", [P, FEAT], F32)
        gb = sb("gb", [P, 2, FEAT], F32)
        sq = sb("sqL", [P, K, FEAT], F32)
        mu = sb("mu", [P, NTILE], F32)
        var = sb("varL", [P, NTILE], F32)
        pc = ps("pc", [P, 2, BANK], F32)
        s_in = sem("gamma_beta_loaded")
        s_mask = sem("maskL_ready")
        s_c = sem("columns_ready")
        s_p = sem("columns_summed")
        s_r = sem("root_wanted")
        s_rd = sem("root_ready")
        s_o = sem("chunk_ready")
        s_out = sem("out_stored")
        s_dve = sem("dve_order_l")
        block = ctx.enter_context(nc.Block())

        @block.sync
        def _(sp):
            sp.dma_start(gb[:, 0, :], k.gamma.partition_broadcast(P)).then_inc(s_in, 16)
            sp.dma_start(gb[:, 1, :], k.beta.partition_broadcast(P)).then_inc(s_in, 16)
            for r in range(NR):
                sp.wait_ge(s_o, r + 1)
                full = K if r < NR - 1 else K - 1
                sp.dma_start(k.out[r * K * P:(r * K + full) * P, :].rearrange("(i p) n -> p i n", p=P),
                             k.big1[:, r * K:r * K + full, :]).then_inc(s_out, 16)
            sp.dma_start(k.out[(NTILE - 1) * P:NODES, :], k.big1[0:LAST, NTILE - 1, :]).then_inc(s_out, 16)
            sp.wait_ge(s_out, 16 * (NR + 1))

        @block.gpsimd
        def _(pool):
            pool.affine_select(out=mask[:, :], in_=k.ones[:, 0:1], compare_op=ALU.is_ge, fill=0.0,
                               base=LAST - 1, pattern=[[0, 1]], channel_multiplier=-1).then_inc(s_mask, 1)

        @block.tensor
        def _(pe):
            for j, c in enumerate((col, col2)):
                pe.wait_ge(s_c, j + 1)
                pe.matmul(pc[:, j, 0:FEAT], k.ones[:, :], c[:, :], start=True, stop=True).then_inc(s_p, 1)

        @block.scalar
        def _(act):
            act.wait_ge(s_r, 1)
            act.activation(scale[:, :], scale[:, :], ACT.Sqrt).then_inc(s_rd, 1)
            act.wait_ge(s_r, 2)
            act.activation(var[:, :], var[:, :], ACT.Sqrt).then_inc(s_rd, 1)

        @block.vector
        def _(dve):
            o = Order(dve, s_dve)
            y = k.big2[:, :, 0:FEAT]
            dve.wait_ge(s_mask, 1)
            dve.wait_ge(s_in, 32)
            o(dve.tensor_scalar(y[:, NTILE - 1, :], y[:, NTILE - 1, :], mask[:, :], None, ALU.mult))
            o(dve.tensor_reduce(col[:, :], y.rearrange("p i n -> p n i"), X, ALU.add))
            dve.sem_inc(s_c, 1)
            dve.wait_ge(s_p, 1)
            o(dve.tensor_scalar(mean[:, :], pc[:, 0, 0:FEAT], 1.0 / NODES, None, ALU.mult))
            o(dve.tensor_tensor(y, y, mean[:, :].unsqueeze(1).to_broadcast([P, NTILE, FEAT]), ALU.subtract))
            o(dve.tensor_scalar(y[:, NTILE - 1, :], y[:, NTILE - 1, :], mask[:, :], None, ALU.mult))
            for r in range(NR):
                c = y[:, r * K:(r + 1) * K, :]
                o(dve.tensor_tensor(sq[:, :, :], c, c, ALU.mult))
                o(dve.tensor_reduce((col if r else col2)[:, :], sq[:, :, :].rearrange("p i n -> p n i"), X, ALU.add))
                if r:
                    o(dve.tensor_tensor(col2[:, :], col2[:, :], col[:, :], ALU.add))
            dve.sem_inc(s_c, 1)
            dve.wait_ge(s_p, 2)
            o(dve.tensor_scalar(scale[:, :], pc[:, 1, 0:FEAT], 1.0 / NODES, EPS_LN, ALU.mult, ALU.add))
            dve.sem_inc(s_r, 1)
            dve.wait_ge(s_rd, 1)
            o(dve.reciprocal(scale[:, :], scale[:, :]))
            o(dve.tensor_tensor(scale[:, :], scale[:, :], gb[:, 0, :], ALU.mult))
            rows = lambda t: t.unsqueeze(1).to_broadcast([P, K, FEAT])
            per = lambda t, r: t[:, r * K:(r + 1) * K].unsqueeze(2).to_broadcast([P, K, FEAT])
            for r in range(NR):
                c, x = y[:, r * K:(r + 1) * K, :], k.big1[:, r * K:(r + 1) * K, :]
                o(dve.tensor_tensor(c, c, rows(scale[:, :]), ALU.mult))
                o(dve.tensor_tensor(c, c, rows(gb[:, 1, :]), ALU.add))
                o(dve.tensor_tensor(x, x, c, ALU.add))
                o(dve.tensor_reduce(mu[:, r * K:(r + 1) * K], x, X, ALU.add))
                o(dve.tensor_scalar(mu[:, r * K:(r + 1) * K], mu[:, r * K:(r + 1) * K], 1.0 / FEAT, None, ALU.mult))
                o(dve.tensor_tensor(x, x, per(mu, r), ALU.subtract))
                o(dve.tensor_tensor(sq[:, :, :], x, x, ALU.mult))
                o(dve.tensor_reduce(var[:, r * K:(r + 1) * K], sq[:, :, :], X, ALU.add))
            o(dve.tensor_scalar(var[:, :], var[:, :], 1.0 / FEAT, EPS_LN, ALU.mult, ALU.add))
            dve.sem_inc(s_r, 1)
            dve.wait_ge(s_rd, 2)
            o(dve.reciprocal(var[:, :], var[:, :]))
            for r in range(NR):
                x = k.big1[:, r * K:(r + 1) * K, :]
                dve.tensor_tensor(x, x, per(var, r), ALU.mult).then_inc(s_o, 1)


def bucket_slot(k, j):
    return k.slot[:, j, :]


PHASES = [phase_sort_and_project, phase_count, phase_softmax, phase_messages_back, phase_first_norm, phase_gather, phase_route,
          phase_dispatch, phase_experts, phase_combine, phase_last_norm]
DEBUG = []
STOP = len(PHASES)


def gnn_resnorm_kernel(nc, x, src, dst, attr, W, att, W_gc, b_gc, W_res, b_res, Wg, bg, w1, b1, w2, b2, gamma, beta, out):
    with ExitStack() as ctx:
        k = Ctx()
        k.x, k.src, k.dst, k.attr, k.W, k.att, k.out = x, src, dst, attr, W, att, out
        k.W_gc, k.b_gc, k.W_res, k.b_res, k.Wg, k.bg = W_gc, b_gc, W_res, b_res, Wg, bg
        k.w1, k.b1, k.w2, k.b2, k.gamma, k.beta = w1, b1, w2, b2, gamma, beta
        k.sem = lambda n: ctx.enter_context(nc.semaphore(n))
        k.idle = {e: k.sem("idle_" + e) for e in ("pool", "act", "pe", "sp", "dve")}
        k.dram = lambda n, s, d: nc.dram_tensor(n, s, d, kind="ExternalOutput" if n in DEBUG else "Internal").ap()
        sb = lambda n, s, d: ctx.enter_context(nc.sbuf_tensor(n, s, d))
        k.SS = k.dram("slots_by_source", (P * NT, 2), F32)
        k.DS = k.dram("slots_by_target", (P * NT, 2), F32)
        k.tab = k.dram("tile_tables", (3, NTM), I32)
        k.R = k.dram("running_counts", (NTILE + 1, P, HC), F32)
        k.CT = k.dram("counts_transposed", (HCH, P, NTILE * P), F32)
        k.UT = k.dram("exponent_rows", (2 * HEADS, NTILE * P), F32)
        k.H = k.dram("h_table", (NTILE * P, FEAT), F32)
        k.xbuf = k.dram("expert_inputs", (MT * P, FEAT), F32)
        k.ybuf = k.dram("expert_outputs", (MT * P, FEAT), F32)
        k.etab = k.dram("expert_of_tile", (1, 2 * P), I32)
        k.bT = k.dram("b_rows", (HEADS, HCH * P), F32)
        k.ident = sb("ident", [P, P], F32)
        k.upper = sb("upper", [P, P], F32)
        k.ones = sb("ones", [P, P], F32)
        k.iota = sb("iota", [P, P], F32)
        k.a = sb("a", [P, NTILE, HEADS], F32)
        k.bE = sb("bE", [P, HCH, HEADS], F32)
        k.deg = sb("deg", [P, NTILE], F32)
        k.rD = sb("rD", [P, NTILE, HEADS], F32)
        k.big1 = sb("big1", [P, NTILE, FEAT], F32)
        sort = ExitStack()
        with sort:
            k.oeT = sort.enter_context(nc.sbuf_tensor("oeT", [P, 2, HCH * P], F32))
            with ExitStack() as edges:
                k.iota16 = edges.enter_context(nc.sbuf_tensor("iota16", [P, HC], F16))
                k.slot = edges.enter_context(nc.sbuf_tensor("slot", [P, 2, ECOL], F32))
                k.pay = edges.enter_context(nc.sbuf_tensor("pay", [P, 2, ECOL, 2], F32))
                for phase in PHASES[:STOP][:3]:
                    phase(nc, k)
            for phase in PHASES[:STOP][3:4]:
                phase(nc, k)
        k.gate = sb("gate", [P, 2, NTILE], F32)
        k.sidx = sb("scatter_slot", [P, NTILE, 2], F32)
        k.gidx = sb("gather_slot", [P, NTILE, 2], F32)
        k.big2 = sb("big2", [P, NTILE, FEAT + 1], F32)
        for phase in PHASES[:STOP][4:]:
            phase(nc, k)


_INS = ["x", "src", "dst", "L0_gnn_hyperedge_attr", "L0_gnn_W", "L0_gnn_att", "L1_gnn_W_gc", "L1_gnn_b_gc",
        "L1_gnn_W_res", "L1_gnn_b_res", "L1_gnn_Wg", "L1_gnn_bg", "L1_gnn_w1", "L1_gnn_b1", "L1_gnn_w2",
        "L1_gnn_b2", "L1_gnn_gamma", "L1_gnn_beta"]


def kernel(**inputs):
    import numpy as _np
    import concourse.bacc as _bacc
    from concourse import mybir as _mybir
    from concourse.bass_utils import run_bass_kernel_spmd as _run

    nc = _bacc.Bacc("TRN2", target_bir_lowering=False, num_devices=1)
    arrays, args = {}, []
    for name in _INS:
        a = _np.ascontiguousarray(inputs[name])
        arrays[f"in_{name}_dram"] = a
        args.append(nc.dram_tensor(f"in_{name}_dram", a.shape, _mybir.dt.from_np(a.dtype), kind="ExternalInput").ap())
    args.append(nc.dram_tensor("out_0_dram", (NODES, FEAT), F32, kind="ExternalOutput").ap())
    gnn_resnorm_kernel(nc, *args)
    r = _run(nc, [arrays], core_ids=[0])
    return r.results[0]["out_0_dram"]
```

```python
from contextlib import ExitStack

import concourse.bass as bass
from concourse import mybir

F32 = mybir.dt.float32
F16 = mybir.dt.float16
BF16 = mybir.dt.bfloat16
I32 = mybir.dt.int32
U32 = mybir.dt.uint32
ALU = mybir.AluOpType
ACT = mybir.ActivationFunctionType
X = mybir.AxisListType.X

P = 128
NODES, FEAT = 6250, 256
NTILE = -(-NODES // P)
LAST = NODES - (NTILE - 1) * P
EDGES = 106250
STEP = 17
ECOL = NTILE * STEP
EFULL = EDGES - (P - 1) * ECOL
NT = -(-EDGES // P) + NTILE
NTM = 7 * P
HEADS, CH = 8, 32
HYPER = 1250
HC = HYPER + 1
HCH = 10
SKIP = float(1 << 20)
BANK = 512
EPS_LN = 1e-5
EXPERTS, HID, CAP = 64, 512, 1024
MT = (2 * NODES) // P + EXPERTS
ZCOLS = 7 * FEAT
assert MT % 7 == 0
assert P * ECOL >= EDGES and 0 < EFULL <= ECOL


class Order:

    def __init__(self, eng, sem):
        self.eng, self.sem, self.base, self.n = eng, sem, 0, 0

    def on(self, eng):
        self.eng = eng
        return self

    def __call__(self, ins):
        self.n += 1
        ins.then_inc(self.sem, 1)
        self.eng.wait_ge(self.sem, self.base + self.n)

    def enter(self, i, steps):
        self.start, self.steps = self.base + self.n, steps
        self.base, self.n = self.start + i * steps, 0

    def leave(self, count):
        assert self.n == self.steps, (self.n, self.steps)
        self.base, self.n = self.start + count * self.steps, 0


class Inputs:

    def __init__(self, sem):
        self.sem, self.total = sem, 0

    def __call__(self, amount):
        self.total += amount
        return self.sem, self.total


class Ctx:
    pass


def banks(base, width):
    return [(c, min(BANK, width - c)) for c in range(0, width, BANK)]


def phase_sort_and_project(nc, k):
    with ExitStack() as ctx:
        sb = lambda n, s, d: ctx.enter_context(nc.sbuf_tensor(n, s, d))
        ps = lambda n, s, d: ctx.enter_context(nc.psum_tensor(n, s, d))
        sem = k.sem
        W = sb("W", [P, 2, FEAT], F32)
        attb = sb("attb", [P, HEADS, 2 * CH], F32)
        xin = sb("xin", [P, 2, FEAT], F32)
        xT = sb("xT", [P, 2, 2, P], F32)
        eh = sb("eh", [P, HCH, FEAT], F32)
        prod = sb("prod", [P, 7 * FEAT], F32)
        bTs = sb("bTs", [HEADS, HCH * P], F32)
        key = sb("key", [P, 2, ECOL], I32)
        keyi = sb("keyi", [P, 2, ECOL], I32)
        bucket = sb("bucket", [P, ECOL], F32)
        eq = sb("eq", [P, 7, ECOL], F32)
        run = sb("run", [P, 7, ECOL], F32)
        part = sb("part", [P, ECOL], F32)
        cnt = sb("cnt", [P, NTILE], F32)
        tiles = sb("tiles", [P, NTILE], F32)
        tilesi = sb("tilesi", [P, NTILE], I32)
        ends = sb("ends", [P, NTILE], F32)
        base = sb("base", [P, NTILE], F32)
        tnum = sb("tnum", [P, 7], F32)
        cmp = sb("cmp", [P, 7, NTILE], F32)
        tabf = sb("tabf", [P, 2, 7], F32)
        tabi = sb("tabi", [P, 2, 7], I32)
        numf = sb("numf", [P, NTILE], F32)
        fill = sb("fill", [P, NT, 2], F32)
        sidx = sb("sidx", [P, 2, STEP], I32)
        spay = sb("spay", [P, 2, STEP, 2], F32)
        pT = ps("pT", [P, 2, 2, P], F32)
        pX = ps("pX", [P, 2, BANK], F32)
        pC = ps("pC", [P, 2, BANK], F32)

        s_w = sem("w_loaded")
        s_x = [sem("x_loaded0"), sem("x_loaded1")]
        s_xfree = sem("x_free")
        s_xz = sem("x_buffers_zeroed")
        s_tr = sem("x_transposed")
        s_xT = sem("xT_ready")
        s_mm = sem("projected")
        s_cp = sem("projection_copied")
        s_keys = sem("keys_loaded")
        s_kset = sem("keys_padded")
        s_const = sem("constants_ready")
        s_pool = sem("pool_order_a")
        s_cnt = sem("counts_ready")
        s_tot = sem("totals_ready")
        s_slots = sem("slots_ready")
        s_stage = sem("edges_staged")
        s_scat = [sem("edges_scattered0"), sem("edges_scattered1")]
        s_fillr = sem("fill_ready")
        s_fill = sem("slots_prefilled")
        s_b = sem("b_ready")
        s_bT = sem("bT_ready")
        s_bTs = sem("bT_copied")
        s_out = sem("tables_stored")
        s_tabs = sem("tables_ready")
        idle = k.idle

        block = ctx.enter_context(nc.Block())

        @block.sync
        def _(sp):
            sp.dma_start(W[:, :, :], k.W.rearrange("(c p) n -> p c n", p=P)).then_inc(s_w, 16)
            sp.dma_start(attb[:, :, :], k.att[0, :, :].partition_broadcast(P)).then_inc(s_w, 16)
            sp.wait_ge(s_kset, 1)
            for j, e in enumerate((k.src, k.dst)):
                sp.dma_start(key[0:P - 1, j, :], e[0:(P - 1) * ECOL].rearrange("(p t) -> p t", t=ECOL)).then_inc(s_keys, 16)
                sp.dma_start(key[P - 1:P, j, 0:EFULL], e[(P - 1) * ECOL:EDGES].rearrange("(p t) -> p t", p=1)).then_inc(s_keys, 16)
            sp.wait_ge(s_xz, 1)
            with sp.Fori(0, NTILE // 2) as i:
                for u in range(2):
                    sp.wait_ge(s_xfree, i * 2 + u + 1)
                    sp.dma_start(xin[:, u, :], k.x[bass.ds((i * 2 + u) * P, P), :]).then_inc(s_x[u], 16)
            sp.wait_ge(s_xfree, NTILE)
            sp.dma_start(xin[0:LAST, 0, :], k.x[(NTILE - 1) * P:NODES, :]).then_inc(s_x[0], 16)
            for c in range(HCH):
                t = NTILE + c
                rows = min(P, HYPER - c * P)
                sp.wait_ge(s_xfree, t + 1)
                sp.dma_start(xin[0:rows, t % 2, :], k.attr[c * P:c * P + rows, :]).then_inc(s_x[t % 2], 16)
                if rows < P:
                    sp.dma_start(xin[rows:rows + 1, t % 2, :], k.attr[HYPER - 1:HYPER, :]).then_inc(s_x[t % 2], 16)
            sp.wait_ge(s_fillr, 1)
            sp.dma_start(k.SS.rearrange("(p t) c -> p t c", p=P), fill[:, :, :]).then_inc(s_fill, 16)
            sp.wait_ge(s_bTs, 3)
            sp.dma_start(k.bT[:, :], bTs[:, :]).then_inc(s_out, 16)
            sp.wait_ge(s_tabs, 1)
            for j in range(2):
                sp.dma_start(k.tab[j, :].rearrange("(p t) -> p t", p=P), tabi[:, j, :]).then_inc(s_out, 16)
            sp.wait_ge(s_out, 48)

        @block.gpsimd
        def _(pool):
            o = Order(pool, s_pool)
            pool.memset(k.ones[:, :], 1.0).then_inc(s_const, 1)
            pool.iota(numf[:, :], [[1, NTILE]], base=0, channel_multiplier=0,
                      allow_small_or_imprecise_dtypes=True).then_inc(s_const, 1)
            pool.iota(tnum[:, :], [[1, 7]], base=0, channel_multiplier=7,
                      allow_small_or_imprecise_dtypes=True).then_inc(s_const, 1)
            pool.iota(k.iota[:, :], [[1, P]], base=0, channel_multiplier=0,
                      allow_small_or_imprecise_dtypes=True).then_inc(s_const, 1)
            pool.iota(k.iota16[:, :], [[1, HC]], base=0, channel_multiplier=0,
                      allow_small_or_imprecise_dtypes=True).then_inc(s_const, 1)
            o(pool.memset(k.ident[:, :], 0.0))
            pool.affine_select(out=k.ident[:, :], in_=k.ident[:, :], compare_op=ALU.not_equal, fill=1.0,
                               base=0, pattern=[[-1, P]], channel_multiplier=1).then_inc(s_const, 1)
            o(pool.memset(k.upper[:, :], 1.0))
            pool.affine_select(out=k.upper[:, :], in_=k.upper[:, :], compare_op=ALU.is_gt, fill=0.0,
                               base=0, pattern=[[1, P]], channel_multiplier=-1).then_inc(s_const, 1)
            pool.memset(fill[:, :, :], -1.0).then_inc(s_fillr, 1)
            bound = pool.to_reg(P * NT - 1)
            pool.wait_ge(s_fill, 16)

            def scatter(step, u):
                pool.wait_ge(s_stage, 2 * step + 2)
                pool.sem_inc(idle["pool"], 1)
                for c in range(STEP):
                    pool.indirect_dma_start(k.SS[:, :], bass.IndirectOffsetOnAxis(ap=sidx[:, u, c:c + 1], axis=0),
                                            spay[:, u, c, :], None, bounds_check=bound,
                                            oob_is_err=False).then_inc(s_scat[u], 16)
            with pool.Fori(0, NTILE // 2) as i:
                for u in range(2):
                    scatter(i * 2 + u, u)
            scatter(NTILE - 1, 0)
            pool.wait_ge(s_scat[0], 16 * STEP * (NTILE // 2 + 1))
            pool.wait_ge(s_scat[1], 16 * STEP * (NTILE // 2))

        @block.scalar
        def _(act):
            act.sem_inc(s_xfree, 2)
            act.sem_inc(s_cp, 2)

            def project(t, u, dst):
                act.wait_ge(s_tr, t + 1)
                act.activation(xT[:, u, :, :], pT[:, u, :, :], ACT.Copy).then_inc(s_xT, 1)
                act.wait_ge(s_mm, t + 1)
                act.sem_inc(idle["act"], 1)
                act.activation(dst, pX[:, u, 0:FEAT], ACT.Copy).then_inc(s_cp, 1)
            with act.Fori(0, NTILE // 2) as i:
                for u in range(2):
                    project(i * 2 + u, u, k.big1[:, bass.ds(i * 2 + u, 1), :].rearrange("p a n -> p (a n)"))
            project(NTILE - 1, 0, k.big1[:, NTILE - 1, :])
            for c in range(HCH):
                project(NTILE + c, (NTILE + c) % 2, eh[:, c, :])

            def stage(step, u, used):
                cols = bass.ds(step * STEP, STEP)
                if used is not None:
                    act.wait_ge(s_scat[u], used)
                    act.sem_inc(idle["act"], 1)
                act.activation(sidx[:, u, :], k.slot[:, 0, cols], ACT.Copy).then_inc(s_stage, 1)
                act.activation(spay[:, u, :, :], k.pay[:, 0, cols, :], ACT.Copy).then_inc(s_stage, 1)
            act.wait_ge(s_slots, 1)
            act.sem_inc(idle["act"], 1)
            for u in range(2):
                stage(u, u, None)
            with act.Fori(1, NTILE // 2) as i:
                for u in range(2):
                    stage(i * 2 + u, u, 16 * STEP * i)
            stage(NTILE - 1, 0, 16 * STEP * (NTILE // 2))
            act.wait_ge(s_bT, 1)
            act.activation(bTs[:, 0:BANK], pC[0:HEADS, 0, :], ACT.Copy).then_inc(s_bTs, 1)
            act.activation(bTs[:, BANK:2 * BANK], pC[0:HEADS, 1, :], ACT.Copy).then_inc(s_bTs, 1)
            act.activation(bTs[:, 2 * BANK:HCH * P], pX[0:HEADS, 0, 0:2 * P], ACT.Copy).then_inc(s_bTs, 1)

        @block.tensor
        def _(pe):
            pe.wait_ge(s_const, 7)
            pe.wait_ge(s_w, 32)

            def project(t, u, loaded):
                pe.wait_ge(s_x[u], loaded)
                pe.sem_inc(idle["pe"], 1)
                for c in range(2):
                    last = pe.transpose(pT[:, u, c, :], xin[:, u, c * P:(c + 1) * P], k.ident[:, :])
                last.then_inc(s_tr, 1)
                pe.wait_ge(s_xT, t + 1)
                pe.sem_inc(s_xfree, 1)
                pe.wait_ge(s_cp, t + 1)
                pe.sem_inc(idle["pe"], 1)
                for c in range(2):
                    last = pe.matmul(pX[:, u, 0:FEAT], xT[:, u, c, :], W[:, c, :], start=(c == 0), stop=(c == 1))
                last.then_inc(s_mm, 1)
            def totals(j):
                pe.wait_ge(s_cnt, j + 1)
                pe.matmul(pC[:, 0, 0:NTILE], k.ones[:, :], cnt[:, :], start=True, stop=True)
                pe.matmul(pC[:, 1, 0:NTILE], k.upper[:, :], cnt[:, :], start=True, stop=True).then_inc(s_tot, 1)
            totals(0)
            with pe.Fori(0, NTILE // 2) as i:
                for u in range(2):
                    project(i * 2 + u, u, i * 16 + 16)
            project(NTILE - 1, 0, 16 * (NTILE // 2) + 16)
            for c in range(HCH):
                t = NTILE + c
                project(t, t % 2, 16 * (t // 2) + 16 + (16 if c == HCH - 1 else 0))
            totals(1)
            pe.wait_ge(s_b, 1)
            pe.wait_ge(s_cp, NTILE + HCH + 2)
            for c in range(HCH):
                out = pC[0:HEADS, c // 4, (c % 4) * P:(c % 4 + 1) * P] if c < 8 else pX[0:HEADS, 0, (c - 8) * P:(c - 7) * P]
                last = pe.transpose(out, k.bE[:, c, :], k.ident[:, :])
            last.then_inc(s_bT, 1)

        @block.vector
        def _(dve):
            o = k.order.on(dve)
            dve.memset(key[:, :, :], NTILE * P).then_inc(s_kset, 1)
            dve.memset(xin[:, :, :], 0.0).then_inc(s_xz, 1)
            dve.wait_ge(s_keys, 64)
            dve.wait_ge(s_const, 7)
            for j in range(2):
                o(dve.tensor_scalar(keyi[:, 0, :], key[:, j, :], P - 1, None, ALU.bitwise_and))
                o(dve.tensor_copy(k.pay[:, j, :, 0], keyi[:, 0, :]))
                if j == 0:
                    o(dve.tensor_scalar(k.pay[:, 0, :, 1], key[:, 1, :], float(HYPER), None, ALU.min))
                else:
                    o(dve.tensor_copy(k.pay[:, 1, :, 1], key[:, 0, :]))
                o(dve.tensor_scalar(keyi[:, 1, :], key[:, j, :], 7, None, ALU.arith_shift_right))
                o(dve.tensor_copy(bucket[:, :], keyi[:, 1, :]))
                for r in range(NTILE // 7):
                    o(dve.tensor_tensor(eq[:, :, :], bucket[:, :].unsqueeze(1).to_broadcast([P, 7, ECOL]),
                                        numf[:, 7 * r:7 * r + 7].unsqueeze(2).to_broadcast([P, 7, ECOL]), ALU.is_equal))
                    o(dve.tensor_reduce(cnt[:, 7 * r:7 * r + 7], eq[:, :, :], X, ALU.add))
                dve.sem_inc(s_cnt, 1)
                dve.wait_ge(s_tot, j + 1)
                o(dve.tensor_scalar(tiles[:, :], pC[:, 0, 0:NTILE], float(P - 1), None, ALU.add))
                o(dve.tensor_copy(tilesi[:, :], tiles[:, :]))
                o(dve.tensor_scalar(tilesi[:, :], tilesi[:, :], 7, None, ALU.arith_shift_right))
                o(dve.tensor_copy(tiles[:, :], tilesi[:, :]))
                o(dve.tensor_scalar(tiles[:, :], tiles[:, :], 1.0, None, ALU.max))
                o(dve.tensor_tensor_scan(ends[:, :], k.ones[:, 0:NTILE], tiles[:, :], 0.0, ALU.mult, ALU.add))
                o(dve.tensor_tensor(base[:, :], ends[:, :], tiles[:, :], ALU.subtract))
                o(dve.tensor_scalar(base[:, :], base[:, :], float(P), -1.0, ALU.mult, ALU.add))
                o(dve.tensor_tensor(base[:, :], base[:, :], pC[:, 1, 0:NTILE], ALU.add))
                for r in range(NTILE // 7):
                    o(dve.tensor_tensor(eq[:, :, :], bucket[:, :].unsqueeze(1).to_broadcast([P, 7, ECOL]),
                                        numf[:, 7 * r:7 * r + 7].unsqueeze(2).to_broadcast([P, 7, ECOL]), ALU.is_equal))
                    for q in range(7):
                        last = dve.tensor_tensor_scan(run[:, q, :], k.ones[:, 0:1].to_broadcast([P, ECOL]), eq[:, q, :],
                                                      base[:, 7 * r + q:7 * r + q + 1], ALU.mult, ALU.add)
                    o(last)
                    o(dve.tensor_tensor(run[:, :, :], run[:, :, :], eq[:, :, :], ALU.mult))
                    acc = part if r else bucket_slot(k, j)
                    o(dve.tensor_reduce(acc[:, :] if r else acc, run[:, :, :].rearrange("p b t -> p t b"), X, ALU.add))
                    if r:
                        o(dve.tensor_tensor(bucket_slot(k, j), bucket_slot(k, j), part[:, :], ALU.add))
                o(dve.tensor_copy(keyi[:, 0, :], bucket_slot(k, j)))
                o(dve.tensor_scalar(keyi[:, 1, :], keyi[:, 0, :], 7, None, ALU.arith_shift_right))
                o(dve.tensor_scalar(keyi[:, 0, :], keyi[:, 0, :], P - 1, None, ALU.bitwise_and))
                o(dve.tensor_copy(part[:, :], keyi[:, 0, :]))
                o(dve.tensor_copy(bucket_slot(k, j), keyi[:, 1, :]))
                o(dve.scalar_tensor_tensor(bucket_slot(k, j), part[:, :], float(NT), bucket_slot(k, j), ALU.mult, ALU.add))
                o(dve.tensor_scalar(part[:, :], bucket[:, :], float(NTILE), SKIP, ALU.is_equal, ALU.mult))
                o(dve.tensor_tensor(bucket_slot(k, j), bucket_slot(k, j), part[:, :], ALU.max))
                dve.sem_inc(s_slots, 1)
                o(dve.tensor_tensor(cmp[:, :, :], ends[:, :].unsqueeze(1).to_broadcast([P, 7, NTILE]),
                                    tnum[:, :].unsqueeze(2).to_broadcast([P, 7, NTILE]), ALU.is_le))
                o(dve.tensor_reduce(tabf[:, j, :], cmp[:, :, :], X, ALU.add))
                if j == 1:
                    o(dve.tensor_scalar(tabf[:, j, :], tabf[:, j, :], float(NTILE - 1), None, ALU.min))
                if j == 0:
                    o(dve.tensor_copy(k.ends[:, :], ends[:, :]))
            o(dve.tensor_copy(tabi[:, :, :], tabf[:, :, :]))
            dve.sem_inc(s_tabs, 1)
            dve.wait_ge(s_w, 32)
            dve.wait_ge(s_cp, NTILE + HCH + 2)

            def logits(dst, rows, n, half):
                w = attb[:, :, half * CH:(half + 1) * CH].unsqueeze(1).to_broadcast([P, n, HEADS, CH])
                pv = prod[:, 0:n * FEAT].rearrange("p (i h c) -> p i h c", h=HEADS, c=CH)
                o(dve.tensor_tensor(pv, rows.rearrange("p i (h c) -> p i h c", c=CH), w, ALU.mult))
                o(dve.tensor_reduce(dst, pv, X, ALU.add))
            for r in range(NTILE // 7):
                logits(k.a[:, 7 * r:7 * r + 7, :], k.big1[:, 7 * r:7 * r + 7, :], 7, 0)
            for r in range(2):
                logits(k.bE[:, 5 * r:5 * r + 5, :], eh[:, 5 * r:5 * r + 5, :], 5, 1)
            dve.sem_inc(s_b, 1)


def phase_count(nc, k):
    with ExitStack() as ctx:
        sb = lambda n, s, d: ctx.enter_context(nc.sbuf_tensor(n, s, d))
        sem = k.sem
        Q = 4
        edges = sb("edges", [P, NT, 2], F32)
        tab = sb("tabrow", [1, NTM], I32)
        ohn = sb("onehot_node", [P, 2, Q, P], BF16)
        ohe = sb("onehot_edge", [P, 2, Q, HC], BF16)
        zero = sb("zero", [P, HC], F32)
        snap = sb("snap", [P, 2, HC], F32)
        run = ctx.enter_context(nc.psum_tensor("running", [P, 3 * BANK], F32))

        s_in, loaded = k.inputs(32)
        s_z = sem("zeros_ready")
        s_oh = sem("onehots_ready")
        s_mm = sem("counted")
        s_used = sem("onehots_used")
        s_evac = sem("bucket_passed")
        s_go = sem("tile_may_count")
        s_snap = sem("count_copied")
        s_R = [sem("counts_stored0"), sem("counts_stored1")]
        idle = k.idle
        block = ctx.enter_context(nc.Block())

        @block.sync
        def _(sp):
            sp.dma_start(edges[:, :, :], k.SS.rearrange("(p t) c -> p t c", p=P)).then_inc(s_in, 16)
            sp.dma_start(tab[:, :], k.tab[0:1, :]).then_inc(s_in, 16)
            sp.wait_ge(s_in, loaded)
            with sp.Fori(0, NT // Q) as i:
                for q in range(Q):
                    bucket = sp.value_load(tab[0:1, bass.ds(i * Q + q, 1)], min_val=0, max_val=NTILE)
                    sp.wait_ge(s_evac, bucket + 1)
                    sp.sem_inc(s_go, 1)

        @block.vector
        def _(dve):
            dve.memset(zero[:, :], 0.0).then_inc(s_z, 1)
            dve.memset(ohn[:, 1, :, :], 0.0).then_inc(s_z, 1)
            dve.memset(ohe[:, 1, 0, :], 0.0).then_inc(s_z, 1)
            dve.wait_ge(s_in, loaded)
            with dve.Fori(0, NT // (2 * Q)) as i:
                for u in range(2):
                    n = i * 2 + u
                    dve.wait_ge(s_used, n + 1)
                    dve.sem_inc(idle["dve"], 1)
                    for q in range(Q):
                        e = edges[:, bass.ds(n * Q + q, 1), :].rearrange("p a b -> p (a b)")
                        dve.tensor_scalar(ohn[:, u, q, :], k.iota16[:, 0:P], e[:, 0:1], None, ALU.is_equal).then_inc(s_oh, 1)
                        dve.tensor_scalar(ohe[:, u, q, :], k.iota16[:, :], e[:, 1:2], None, ALU.is_equal).then_inc(s_oh, 1)

        @block.tensor
        def _(pe):
            pe.wait_ge(s_z, 3)
            for c, w in banks(0, HC):
                last = pe.matmul(run[:, c:c + w], ohn[:, 1, 0, :], ohe[:, 1, 0, c:c + w], start=True, stop=True)
            last.then_inc(s_mm, 1)
            pe.wait_ge(s_mm, 1)
            pe.sem_inc(s_used, 2)
            with pe.Fori(0, NT // (2 * Q)) as i:
                for u in range(2):
                    n = i * 2 + u
                    for q in range(Q):
                        pe.wait_ge(s_oh, n * (2 * Q) + 2 * q + 2)
                        pe.wait_ge(s_go, n * Q + q + 1)
                        pe.sem_inc(idle["pe"], 1)
                        for c, w in banks(0, HC):
                            last = pe.matmul(run[:, c:c + w], ohn[:, u, q, :], ohe[:, u, q, c:c + w], start=False,
                                             stop=True, skip_group_check=True)
                        last.then_inc(s_mm, 1)
                    pe.wait_ge(s_mm, n * Q + Q + 1)
                    pe.sem_inc(s_used, 1)

        @block.scalar
        def _(act):
            act.sem_inc(s_evac, 1)
            act.wait_ge(s_z, 3)
            act.dma_start(k.R[0, :, :], zero[:, :]).then_inc(s_R[1], 16)
            act.wait_ge(s_in, loaded)

            def bucket(b, u, stored):
                ends = act.value_load(k.ends[0:1, bass.ds(b, 1)], min_val=1, max_val=NT)
                act.wait_ge(s_mm, ends + 1)
                if stored is not None:
                    act.wait_ge(s_R[u], stored)
                act.sem_inc(idle["act"], 1)
                act.activation(snap[:, u, :], run[:, 0:HC], ACT.Copy).then_inc(s_snap, 1)
                act.wait_ge(s_snap, b + 1)
                act.sem_inc(s_evac, 1)
                act.dma_start(k.R[bass.ds(b + 1, 1), :, :].rearrange("a p n -> (a p) n"), snap[:, u, :]).then_inc(s_R[u], 16)
            bucket(0, 0, None)
            bucket(1, 1, None)
            with act.Fori(1, NTILE // 2) as i:
                for u in range(2):
                    bucket(i * 2 + u, u, 16 * i + (16 if u else 0))
            bucket(NTILE - 1, 0, 16 * (NTILE // 2))
            act.wait_ge(s_R[0], 16 * (NTILE // 2 + 1))
            act.wait_ge(s_R[1], 16 * (NTILE // 2 + 1))


def phase_softmax(nc, k):
    with ExitStack() as ctx:
        sb = lambda n, s, d: ctx.enter_context(nc.sbuf_tensor(n, s, d))
        ps = lambda n, s, d: ctx.enter_context(nc.psum_tensor(n, s, d))
        sem = k.sem
        bbc = sb("bbc", [P, HEADS, HC], F32)
        Ra = sb("Ra", [P, HC], F32)
        Rb = sb("Rb", [P, HC], F32)
        C = sb("C", [P, 2, HCH * P], F32)
        M = sb("M", [P, HC], F32)
        low = sb("low", [P, 2, HC], F32)
        Pb = sb("Pb", [P, HEADS, HC], F32)
        ctb = sb("ctb", [P, HCH, P], F32)
        urow = sb("urow", [2 * HEADS, P], F32)
        fill = low[:, :, :].rearrange("p a n -> p (a n)")[:, 0:2 * NT].rearrange("p (t c) -> p t c", c=2)
        bmax = sb("bmax", [P, HEADS], F32)
        top = sb("top", [P, HEADS], F32)
        u16 = sb("u16", [P, 2 * HEADS], F32)
        asum = sb("asum", [P, HEADS], F32)
        dinv = sb("dinv", [P, 1], F32)
        degr = sb("degr", [P, 2], F32)
        ai = sb("ai", [P, 2, HEADS], F32)
        xs = sb("xs", [P, HEADS, CH], F32)
        sidx = sb("sidx2", [P, STEP], I32)
        spay = sb("spay2", [P, STEP, 2], F32)
        OE = ps("OE", [P, 2, 3 * BANK], F32)
        pT = ps("pT2", [P, 2, 4, P], F32)

        s_bbc = sem("b_loaded")
        s_r = sem("R_loaded")
        s_rfree = sem("R_used")
        s_c = sem("C_ready")
        s_u = sem("u_ready")
        s_t2 = sem("low_branch_ready")
        s_arg = sem("exponent_ready")
        s_e = sem("exp_ready")
        s_xs = sem("xs_ready")
        s_pm = sem("messages_added")
        s_tr = sem("C_transposed")
        s_cc = sem("C_transposes_copied")
        s_ut = sem("u_transposed")
        s_uc = sem("u_copied")
        s_uts = sem("u_dma")
        s_ufree = sem("u_stored")
        s_ctfree = sem("ct_stored")
        s_cts = sem("ct_dma")
        s_stage = sem("target_edges_staged")
        s_sfree = sem("staging_free")
        s_scat = sem("target_edges_scattered")
        s_fillr = sem("fillD_ready")
        s_fill = sem("DS_prefilled")
        s_z = sem("oe_zeroed")
        s_end = sem("oe_copied")
        idle = k.idle
        block = ctx.enter_context(nc.Block())

        @block.sync
        def _(sp):
            sp.dma_start(bbc[:, :, :], k.bT[:, 0:HC].partition_broadcast(P)).then_inc(s_bbc, 16)
            sp.wait_ge(s_fillr, 2)
            sp.dma_start(k.DS.rearrange("(p t) c -> p t c", p=P), fill).then_inc(s_fill, 16)

            def load(i):
                sp.wait_ge(s_rfree, i + 1)
                sp.sem_inc(idle["sp"], 1)
                sp.dma_start(Ra[:, :], k.R[bass.ds(i, 1), :, :].rearrange("a p n -> (a p) n")).then_inc(s_r, 16)
                sp.dma_start(Rb[:, :], k.R[bass.ds(i + 1, 1), :, :].rearrange("a p n -> (a p) n")).then_inc(s_r, 16)

            def store(i):
                sp.wait_ge(s_cc, i * 3 + 3)
                sp.sem_inc(idle["sp"], 1)
                sp.dma_start(k.CT[:, :, bass.ds(i * P, P)].rearrange("c e n -> e c n"), ctb[:, :, :]).then_inc(s_cts, 16)
                sp.wait_ge(s_cts, i * 16 + 16)
                sp.sem_inc(s_ctfree, 1)
                sp.wait_ge(s_uc, i + 1)
                sp.sem_inc(idle["sp"], 1)
                sp.dma_start(k.UT[:, bass.ds(i * P, P)], urow[:, :]).then_inc(s_uts, 16)
                sp.wait_ge(s_uts, i * 16 + 16)
                sp.sem_inc(s_ufree, 1)
            load(0)
            with sp.Fori(0, NTILE - 1) as i:
                load(i + 1)
                store(i)
            store(NTILE - 1)

        @block.gpsimd
        def _(pool):
            pool.memset(fill[:, :, 0:1], -1.0).then_inc(s_fillr, 1)
            pool.memset(fill[:, :, 1:2], 0.0).then_inc(s_fillr, 1)
            bound = pool.to_reg(P * NT - 1)
            pool.sem_inc(s_sfree, 1)
            pool.wait_ge(s_fill, 16)
            with pool.Fori(0, NTILE) as i:
                pool.wait_ge(s_stage, i * 2 + 2)
                pool.sem_inc(idle["pool"], 1)
                for c in range(STEP):
                    pool.indirect_dma_start(k.DS[:, :], bass.IndirectOffsetOnAxis(ap=sidx[:, c:c + 1], axis=0),
                                            spay[:, c, :], None, bounds_check=bound, oob_is_err=False).then_inc(s_scat, 16)
                pool.wait_ge(s_scat, i * (16 * STEP) + 16 * STEP)
                pool.sem_inc(s_sfree, 1)

        @block.vector
        def _(dve):
            o = k.order.on(dve)
            dve.sem_inc(s_rfree, 1)
            dve.sem_inc(s_arg, 2)
            o(dve.memset(C[:, :, HC:], 0.0))
            o(dve.memset(M[:, :], 0.0))
            dve.sem_inc(s_z, 1)
            dve.wait_ge(s_bbc, 16)
            dve.wait_ge(s_pm, HEADS)

            def counts(i, u):
                dve.wait_ge(s_r, i * 32 + 32)
                dve.sem_inc(idle["dve"], 1)
                o(dve.scalar_tensor_tensor(C[:, u, 0:HC], Rb[:, :], 1.0, Ra[:, :], ALU.mult, ALU.subtract,
                                           accum_out=degr[:, u:u + 1]))
                dve.sem_inc(s_rfree, 1)
                dve.sem_inc(s_c, 1)
                o(dve.tensor_scalar(M[:, :], C[:, u, 0:HC], 0.0, -1e30, ALU.is_equal, ALU.mult))
                dve.sem_inc(idle["dve"], 1)
                o(dve.tensor_copy(k.deg[:, bass.ds(i, 1)], degr[:, u:u + 1]))
                dve.sem_inc(idle["dve"], 1)
                o(dve.tensor_copy(ai[:, u, :], k.a[:, bass.ds(i, 1), :].rearrange("p a n -> p (a n)")))

            def tile(i, u, more):
                row = lambda t: t[:, bass.ds(i, 1), :].rearrange("p a n -> p (a n)")
                for h in range(HEADS):
                    dve.wait_ge(s_pm, i * HEADS + h + 1)
                    dve.sem_inc(idle["dve"], 1)
                    last = dve.tensor_tensor_reduce(Pb[:, h, :], bbc[:, h, :], M[:, :], 1.0, -3e38, ALU.add, ALU.max, bmax[:, h:h + 1])
                o(last)
                o(dve.tensor_tensor(bmax[:, :], bmax[:, :], ai[:, u, :], ALU.add))
                o(dve.scalar_tensor_tensor(top[:, :], bmax[:, :], 0.2, bmax[:, :], ALU.mult, ALU.max))
                dve.wait_ge(s_ut, i + 1)
                dve.sem_inc(idle["dve"], 1)
                o(dve.tensor_tensor(u16[:, 0:HEADS], ai[:, u, :], top[:, :], ALU.subtract))
                o(dve.scalar_tensor_tensor(u16[:, HEADS:], ai[:, u, :], 0.2, top[:, :], ALU.mult, ALU.subtract))
                dve.sem_inc(s_u, 1)
                if more:
                    counts(i + 1, 1 - u)

                def weights(h):
                    dve.wait_ge(s_e, i * HEADS + h + 1)
                    last = dve.scalar_tensor_tensor(Pb[:, h, :], Pb[:, h, :], 1.0, C[:, u, 0:HC], ALU.mult, ALU.mult,
                                                    accum_out=asum[:, h:h + 1])
                    if h % 2 == 0:
                        return
                    o(last)
                    two = asum[:, h - 1:h + 1]
                    o(dve.tensor_scalar(two, two, 1e-16, None, ALU.add))
                    o(dve.reciprocal(two, two))
                    dve.tensor_tensor(xs[:, h - 1:h + 1, :],
                                      row(k.big1)[:, (h - 1) * CH:(h + 1) * CH].rearrange("p (h c) -> p h c", c=CH),
                                      two.unsqueeze(2).to_broadcast([P, 2, CH]), ALU.mult).then_inc(s_xs, 1)
                for h in range(HEADS):
                    dve.wait_ge(s_t2, i * HEADS + h + 1)
                    dve.scalar_tensor_tensor(Pb[:, h, :], Pb[:, h, :], u16[:, h:h + 1], low[:, h % 2, :],
                                             ALU.add, ALU.max).then_inc(s_arg, 1)
                    if h:
                        weights(h - 1)
                weights(HEADS - 1)
                o(dve.tensor_scalar(dinv[:, :], degr[:, u:u + 1], 1.0, None, ALU.max))
                o(dve.reciprocal(dinv[:, :], dinv[:, :]))
                o(dve.tensor_scalar(row(k.rD), asum[:, :], dinv[:, :], None, ALU.mult))
            counts(0, 0)
            with dve.Fori(0, NTILE // 2) as i:
                o.enter(i, 2 * 24)
                for u in range(2):
                    tile(i * 2 + u, u, True)
                o.leave(NTILE // 2)
            tile(NTILE - 1, 0, False)
            dve.wait_ge(s_pm, HEADS * (NTILE + 1))
            o(dve.tensor_copy(k.oeT[:, :, 0:HYPER], OE[:, :, 0:HYPER]))

        @block.scalar
        def _(act):
            act.wait_ge(s_bbc, 16)
            act.wait_ge(s_fill, 16)

            def counts(i):
                act.wait_ge(s_ctfree, i + 1)
                act.wait_ge(s_tr, i * 2 + 1)
                act.sem_inc(idle["act"], 1)
                act.activation(ctb[:, 0:4, :], pT[:, 0, :, :], ACT.Copy).then_inc(s_cc, 1)
                act.activation(ctb[:, 4:8, :], pT[:, 1, :, :], ACT.Copy).then_inc(s_cc, 1)
                act.wait_ge(s_tr, i * 2 + 2)
                act.sem_inc(idle["act"], 1)
                act.activation(ctb[:, 8:10, :], pT[:, 0, 0:2, :], ACT.Copy).then_inc(s_cc, 1)

            def tile(i, more):
                cols = bass.ds(i * STEP, STEP)
                act.wait_ge(s_sfree, i + 1)
                act.sem_inc(idle["act"], 1)
                act.activation(sidx[:, :], k.slot[:, 1, cols], ACT.Copy).then_inc(s_stage, 1)
                act.activation(spay[:, :, :], k.pay[:, 1, cols, :], ACT.Copy).then_inc(s_stage, 1)
                act.wait_ge(s_u, i + 1)
                for h in range(HEADS + 1):
                    if h < HEADS:
                        act.wait_ge(s_arg, i * HEADS + h + 1)
                        act.activation(low[:, h % 2, :], Pb[:, h, :], ACT.Identity, bias=u16[:, HEADS + h:HEADS + h + 1],
                                       scale=0.2).then_inc(s_t2, 1)
                    if h:
                        act.wait_ge(s_arg, i * HEADS + h + 2)
                        act.activation(Pb[:, h - 1, :], Pb[:, h - 1, :], ACT.Exp).then_inc(s_e, 1)
                act.wait_ge(s_ufree, i + 1)
                act.wait_ge(s_ut, i + 2)
                act.sem_inc(idle["act"], 1)
                act.activation(urow[:, :], pT[0:2 * HEADS, 1, 0, :], ACT.Copy).then_inc(s_uc, 1)
                if more:
                    counts(i + 1)
            act.sem_inc(s_ctfree, 1)
            act.sem_inc(s_ufree, 1)
            counts(0)
            with act.Fori(0, NTILE // 2) as i:
                for u in range(2):
                    tile(i * 2 + u, True)
            tile(NTILE - 1, False)

        @block.tensor
        def _(pe):
            pe.sem_inc(s_ut, 1)
            pe.wait_ge(s_z, 1)
            for g in range(2):
                for c, w in banks(0, HC):
                    last = pe.matmul(OE[:, g, c:c + w], M[:, 0:P], M[:, c:c + w], start=True, stop=True)
            last.then_inc(s_pm, 1)
            pe.wait_ge(s_pm, 1)
            pe.sem_inc(s_pm, HEADS - 1)

            def counts(i, u, first):
                pe.wait_ge(s_c, i + 1)
                if not first:
                    pe.wait_ge(s_uc, i)
                    pe.wait_ge(s_cc, i * 3)
                pe.sem_inc(idle["pe"], 1)
                for c in range(8):
                    last = pe.transpose(pT[:, c // 4, c % 4, :], C[:, u, c * P:(c + 1) * P], k.ident[:, :])
                last.then_inc(s_tr, 1)
                pe.wait_ge(s_cc, i * 3 + 2)
                pe.sem_inc(idle["pe"], 1)
                for c in range(8, HCH):
                    last = pe.transpose(pT[:, 0, c - 8, :], C[:, u, c * P:(c + 1) * P], k.ident[:, :])
                last.then_inc(s_tr, 1)

            def tile(i, u, more):
                for h in range(HEADS):
                    g, j = divmod(h, 4)
                    if h % 2 == 0:
                        pe.wait_ge(s_xs, i * (HEADS // 2) + h // 2 + 1)
                        pe.sem_inc(idle["pe"], 1)
                    for c, w in banks(0, HYPER):
                        last = pe.matmul(OE[CH * j:CH * j + CH, g, c:c + w], xs[:, h, :], Pb[:, h, c:c + w],
                                         start=False, stop=True, skip_group_check=True)
                    last.then_inc(s_pm, 1)
                pe.wait_ge(s_u, i + 1)
                pe.sem_inc(idle["pe"], 1)
                pe.transpose(pT[0:2 * HEADS, 1, 0, :], u16[:, :], k.ident[:, :]).then_inc(s_ut, 1)
                if more:
                    counts(i + 1, 1 - u, False)
            counts(0, 0, True)
            with pe.Fori(0, NTILE // 2) as i:
                for u in range(2):
                    tile(i * 2 + u, u, True)
            tile(NTILE - 1, 0, False)


def phase_messages_back(nc, k):
    with ExitStack() as ctx:
        sb = lambda n, s, d: ctx.enter_context(nc.sbuf_tensor(n, s, d))
        ps = lambda n, s, d: ctx.enter_context(nc.psum_tensor(n, s, d))
        sem = k.sem
        NG, NL, NZ, SKEW = NTILE // 4, 4, 8, 3
        STEPS = HCH * HEADS
        oe = sb("oe", [P, HCH, FEAT], F32)
        b02 = sb("b02", [P, HCH, HEADS], F32)
        U = sb("U", [P, 2, 2 * HEADS, BANK], F32)
        CT = sb("CTs", [P, 2, HCH, BANK], F32)
        low = sb("lowD", [P, NL, BANK], F32)
        z = sb("z", [P, NZ, BANK], F32)
        flat = z[:, :, :].rearrange("p a n -> p (a n)")
        Rl, binv = flat[:, 0:HC], flat[:, 3 * BANK:3 * BANK + HYPER]
        ots = sb("ots", [P, 2, BANK], F32)
        pB = ps("pB", [P, 3 * BANK], F32)
        OT = ps("OT", [P, 2, BANK], F32)
        pN = ps("pN", [P, 4, FEAT], F32)

        s_R = sem("last_R_loaded")
        s_bc = sem("column_sums")
        s_sc = sem("oe_scaled")
        s_tp = sem("oe_transposed")
        s_oe = sem("oe_ready")
        s_ld = [sem("group_loaded0"), sem("group_loaded1")]
        s_gfree = sem("group_used")
        s_low = sem("low_ready_d")
        s_arg = sem("exponent_ready_d")
        s_cl = sem("exponent_clamped")
        s_e = sem("exp_ready_d")
        s_w = sem("weights_ready_d")
        s_mm = sem("summed_d")
        s_otc = sem("sums_copied")
        s_tr = sem("sums_transposed")
        s_y = sem("messages_stored")
        idle = k.idle
        block = ctx.enter_context(nc.Block())

        @block.sync
        def _(sp):
            sp.dma_start(Rl, k.R[NTILE, :, :]).then_inc(s_R, 16)

            def load(g, u, w):
                cols = bass.ds(g * BANK, w)
                sp.wait_ge(s_gfree, g + 1)
                sp.sem_inc(idle["sp"], 1)
                sp.dma_start(U[:, u, :, 0:w], k.UT[:, cols].partition_broadcast(P)).then_inc(s_ld[u], 16)
                sp.dma_start(CT[:, u, :, 0:w], k.CT[:, :, cols].rearrange("c e n -> e c n")).then_inc(s_ld[u], 16)
            with sp.Fori(0, NG // 2) as i:
                for u in range(2):
                    load(i * 2 + u, u, BANK)
            load(NG, 0, P)

        def steps():
            return [(s, s // HEADS, s % HEADS) for s in range(STEPS)]

        @block.scalar
        def _(act):
            for g in range(2):
                act.wait_ge(s_tp, g + 1)
                for c0, n in ((0, 4), (4, 4), (8, 2)):
                    act.activation(oe[:, c0:c0 + n, g * P:(g + 1) * P],
                                   pB[:, c0 * P:(c0 + n) * P].rearrange("p (c n) -> p c n", c=n), ACT.Copy).then_inc(s_oe, 1)

            def group(g, u, loads, w):
                def exp(s):
                    act.wait_ge(s_cl, g * STEPS + s + 1)
                    act.activation(z[:, s % NZ, 0:w], z[:, s % NZ, 0:w], ACT.Exp).then_inc(s_e, 1)
                act.wait_ge(s_ld[u], loads)
                act.sem_inc(idle["act"], 1)
                for s, c, h in steps():
                    act.wait_ge(s_arg, g * STEPS + s + 1)
                    act.activation(low[:, s % NL, 0:w], U[:, u, HEADS + h, 0:w], ACT.Identity,
                                   bias=b02[:, c, h:h + 1]).then_inc(s_low, 1)
                    if s >= SKEW:
                        exp(s - SKEW)
                for s in range(STEPS - SKEW, STEPS):
                    exp(s)
                act.wait_ge(s_mm, g * STEPS + STEPS + NZ)
                act.sem_inc(idle["act"], 1)
                act.activation(ots[:, :, 0:w], OT[:, :, 0:w], ACT.Copy).then_inc(s_otc, 1)
            with act.Fori(0, NG // 2) as i:
                for u in range(2):
                    group(i * 2 + u, u, i * 32 + 32, BANK)
            group(NG, 0, 32 * (NG // 2) + 32, P)

        @block.gpsimd
        def _(pool):
            def group(g, w):
                for s, c, h in steps():
                    pool.wait_ge(s_arg, g * STEPS + s + 1 + NL)
                    pool.sem_inc(idle["pool"], 1)
                    pool.tensor_scalar(z[:, s % NZ, 0:w], z[:, s % NZ, 0:w], 0.0, None, ALU.min).then_inc(s_cl, 1)
            with pool.Fori(0, NG) as g:
                group(g, BANK)
            group(NG, P)

        @block.tensor
        def _(pe):
            pe.wait_ge(s_R, 16)
            for c, w in banks(0, HYPER):
                last = pe.matmul(pB[:, c:c + w], k.ones[:, :], Rl[:, c:c + w], start=True, stop=True)
            last.then_inc(s_bc, 1)
            pe.wait_ge(s_sc, 1)
            for g in range(2):
                if g:
                    pe.wait_ge(s_oe, 3)
                for c in range(HCH):
                    last = pe.transpose(pB[:, c * P:(c + 1) * P], k.oeT[:, g, c * P:(c + 1) * P], k.ident[:, :])
                last.then_inc(s_tp, 1)
            pe.wait_ge(s_oe, 6)

            def group(g, w):
                pe.wait_ge(s_otc, g + 1)
                pe.sem_inc(idle["pe"], 1)
                for s, c, h in steps():
                    j = h % 4
                    pe.wait_ge(s_w, g * STEPS + s + 1)
                    pe.matmul(OT[CH * j:CH * j + CH, h // 4, 0:w], oe[:, c, h * CH:(h + 1) * CH], z[:, s % NZ, 0:w],
                              start=(c == 0), stop=(c == HCH - 1)).then_inc(s_mm, 1)
                pe.wait_ge(s_otc, g + 2)
                pe.wait_ge(s_y, g + 1)
                pe.sem_inc(idle["pe"], 1)
                for q in range(w // P):
                    for g2 in range(2):
                        last = pe.transpose(pN[:, q, g2 * P:(g2 + 1) * P], ots[:, g2, q * P:(q + 1) * P], k.ident[:, :])
                last.then_inc(s_tr, 1)
            with pe.Fori(0, NG) as g:
                group(g, BANK)
            group(NG, P)

        @block.vector
        def _(dve):
            o = k.order.on(dve)
            dve.sem_inc(s_gfree, 2)
            dve.sem_inc(s_arg, NL)
            dve.sem_inc(s_mm, NZ)
            dve.sem_inc(s_otc, 1)
            dve.sem_inc(s_y, 1)
            o(dve.tensor_scalar(b02[:, :, :], k.bE[:, :, :], 0.2, None, ALU.mult))
            dve.wait_ge(s_bc, 1)
            o(dve.tensor_scalar(binv, pB[:, 0:HYPER], 1.0, None, ALU.max))
            o(dve.reciprocal(binv, binv))
            o(dve.tensor_tensor(k.oeT[:, :, 0:HYPER], k.oeT[:, :, 0:HYPER],
                                binv.unsqueeze(1).to_broadcast([P, 2, HYPER]), ALU.mult))
            o(dve.tensor_copy(k.oeT[:, :, HYPER:HC], k.oeT[:, :, HYPER - 1:HYPER]))
            o(dve.memset(k.oeT[:, :, HC:], 0.0))
            dve.sem_inc(s_sc, 1)

            def group(g, u, loads, w):
                def weights(s, c):
                    dve.wait_ge(s_e, g * STEPS + s + 1)
                    dve.tensor_tensor(z[:, s % NZ, 0:w], z[:, s % NZ, 0:w], CT[:, u, c, 0:w], ALU.mult).then_inc(s_w, 1)
                dve.wait_ge(s_ld[u], loads)
                dve.sem_inc(idle["dve"], 1)
                for s, c, h in steps():
                    dve.wait_ge(s_mm, g * STEPS + s + 1)
                    dve.wait_ge(s_low, g * STEPS + s + 1)
                    dve.scalar_tensor_tensor(z[:, s % NZ, 0:w], U[:, u, h, 0:w], k.bE[:, c, h:h + 1],
                                             low[:, s % NL, 0:w], ALU.add, ALU.max).then_inc(s_arg, 1)
                    if s >= SKEW:
                        weights(s - SKEW, (s - SKEW) // HEADS)
                for s in range(STEPS - SKEW, STEPS):
                    weights(s, s // HEADS)
                dve.wait_ge(s_w, g * STEPS + STEPS)
                dve.sem_inc(s_gfree, 1)
                n = w // P
                dve.wait_ge(s_tr, g + 1)
                dve.sem_inc(idle["dve"], 1)
                dve.tensor_tensor(k.big1[:, bass.ds(g * 4, n), :].rearrange("p i (h c) -> p i h c", c=CH),
                                  pN[:, 0:n, :].rearrange("p i (h c) -> p i h c", c=CH),
                                  k.rD[:, bass.ds(g * 4, n), :].unsqueeze(3).to_broadcast([P, n, HEADS, CH]),
                                  ALU.mult).then_inc(s_y, 1)
            with dve.Fori(0, NG // 2) as i:
                for u in range(2):
                    group(i * 2 + u, u, i * 32 + 32, BANK)
            group(NG, 0, 32 * (NG // 2) + 32, P)


def phase_first_norm(nc, k):
    with ExitStack() as ctx:
        sb = lambda n, s, d: ctx.enter_context(nc.sbuf_tensor(n, s, d))
        sem = k.sem
        K = 7
        xc = sb("xc", [P, 2, K, FEAT], F32)
        sq = sb("sq", [P, 2, K, FEAT], F32)
        mean = sb("mean", [P, NTILE], F32)
        var = sb("var", [P, NTILE], F32)
        dsq = sb("dsq", [P, NTILE], F32)
        s_x = [sem("xc_loaded0"), sem("xc_loaded1")]
        s_z = sem("xc_zeroed")
        s_used = sem("xc_used")
        s_v = sem("variance_ready")
        s_sd = sem("deviation_ready")
        s_h = sem("h_ready")
        s_st = [sem("h_stored0"), sem("h_stored1")]
        block = ctx.enter_context(nc.Block())

        @block.sync
        def _(sp):
            for r in range(NTILE // K):
                u = r % 2
                if r < 2:
                    sp.wait_ge(s_z, 1)
                else:
                    sp.wait_ge(s_used, r - 1)
                full = K if r < NTILE // K - 1 else K - 1
                sp.dma_start(xc[:, u, 0:full, :], k.x[r * K * P:(r * K + full) * P, :].rearrange("(i p) n -> p i n", p=P)).then_inc(s_x[u], 16)
                if full < K:
                    sp.dma_start(xc[0:LAST, u, full, :], k.x[(NTILE - 1) * P:NODES, :]).then_inc(s_x[u], 16)
            for r in range(NTILE // K):
                sp.wait_ge(s_h, r + 1)
                sp.dma_start(k.H[r * K * P:(r + 1) * K * P, :].rearrange("(i p) n -> p i n", p=P), sq[:, r % 2, :, :]).then_inc(s_st[r % 2], 16)
            sp.wait_ge(s_st[0], 64)
            sp.wait_ge(s_st[1], 48)

        @block.scalar
        def _(act):
            act.wait_ge(s_v, 1)
            act.activation(var[:, :], var[:, :], ACT.Sqrt).then_inc(s_sd, 1)
            act.activation(dsq[:, :], dsq[:, :], ACT.Sqrt).then_inc(s_sd, 1)

        @block.vector
        def _(dve):
            o = k.order.on(dve)
            o(dve.memset(xc[:, :, :, :], 0.0))
            dve.sem_inc(s_z, 1)
            bc = lambda t, r: t[:, r * K:(r + 1) * K].unsqueeze(2).to_broadcast([P, K, FEAT])
            for r in range(NTILE // K):
                y = k.big1[:, r * K:(r + 1) * K, :]
                dve.wait_ge(s_x[r % 2], 16 * (r // 2 + 1) + (16 if r == NTILE // K - 1 else 0))
                o(dve.tensor_tensor(y, y, xc[:, r % 2, :, :], ALU.add))
                dve.sem_inc(s_used, 1)
                o(dve.tensor_reduce(mean[:, r * K:(r + 1) * K], y, X, ALU.add))
                o(dve.tensor_scalar(mean[:, r * K:(r + 1) * K], mean[:, r * K:(r + 1) * K], 1.0 / FEAT, None, ALU.mult))
                o(dve.tensor_tensor(y, y, bc(mean, r), ALU.subtract))
                o(dve.tensor_tensor(sq[:, 0, :, :], y, y, ALU.mult))
                o(dve.tensor_reduce(var[:, r * K:(r + 1) * K], sq[:, 0, :, :], X, ALU.add))
            o(dve.tensor_scalar(var[:, :], var[:, :], 1.0 / FEAT, EPS_LN, ALU.mult, ALU.add))
            o(dve.tensor_scalar(dsq[:, :], k.deg[:, :], 1.0, None, ALU.max))
            dve.sem_inc(s_v, 1)
            dve.wait_ge(s_sd, 2)
            o(dve.reciprocal(var[:, :], var[:, :]))
            o(dve.reciprocal(dsq[:, :], dsq[:, :]))
            for r in range(NTILE // K):
                y = k.big1[:, r * K:(r + 1) * K, :]
                o(dve.tensor_tensor(y, y, bc(var, r), ALU.mult))
                if r >= 2:
                    dve.wait_ge(s_st[r % 2], 16 * (r // 2))
                dve.tensor_tensor(sq[:, r % 2, :, :], y, bc(dsq, r), ALU.mult).then_inc(s_h, 1)


def phase_gather(nc, k):
    with ExitStack() as ctx:
        sb = lambda n, s, d: ctx.enter_context(nc.sbuf_tensor(n, s, d))
        ps = lambda n, s, d: ctx.enter_context(nc.psum_tensor(n, s, d))
        sem = k.sem
        Q, B = 4, 4
        edges = sb("edgesT", [P, NT, 2], F32)
        tab = sb("tabrowT", [1, NTM], I32)
        idx = sb("idx", [P, B, Q], I32)
        oh = sb("ohT", [P, B, Q, P], F32)
        rows = sb("rows", [P, B, Q, FEAT], F32)
        zero = sb("zeroE", [P, ZCOLS], F32)
        pm = ps("pm", [P, 2 * Q, BANK], F32)
        s_z = sem("zeroE_ready")
        s_zf = sem("expert_inputs_zeroed")
        s_in, loaded = k.inputs(32)
        s_m0 = sem("m_zeroed")
        s_idx = sem("idx_ready")
        s_oh = sem("oh_ready")
        s_g = [sem("rows_gathered%d" % b) for b in range(B)]
        s_mm = sem("rows_summed")
        s_add = sem("m_added")
        idle = k.idle
        block = ctx.enter_context(nc.Block())
        NI = NT // Q

        @block.sync
        def _(sp):
            sp.dma_start(edges[:, :, :], k.DS.rearrange("(p t) c -> p t c", p=P)).then_inc(s_in, 16)
            sp.dma_start(tab[:, :], k.tab[1:2, :]).then_inc(s_in, 16)
            sp.wait_ge(s_z, 1)
            flat = k.xbuf.rearrange("(p r) n -> p (r n)", p=P)
            for c in range(MT * FEAT // ZCOLS):
                sp.dma_start(flat[:, c * ZCOLS:(c + 1) * ZCOLS], zero[:, :]).then_inc(s_zf, 16)
            sp.wait_ge(s_zf, 16 * (MT * FEAT // ZCOLS))

        @block.gpsimd
        def _(pool):
            bound = pool.to_reg(NTILE * P - 1)
            with pool.Fori(0, NI // B) as i:
                for u in range(B):
                    pool.wait_ge(s_idx, i * B + u + 1)
                    pool.sem_inc(idle["pool"], 1)
                    for q in range(Q):
                        pool.indirect_dma_start(rows[:, u, q, :], None, k.H[:, :],
                                                bass.IndirectOffsetOnAxis(ap=idx[:, u, q:q + 1], axis=0),
                                                bounds_check=bound).then_inc(s_g[u], 16)

        @block.tensor
        def _(pe):
            with pe.Fori(0, NI // B) as i:
                for u in range(B):
                    n = i * B + u
                    pe.wait_ge(s_oh, n + 1)
                    pe.wait_ge(s_g[u], i * (16 * Q) + 16 * Q)
                    pe.sem_inc(idle["pe"], 1)
                    for q in range(Q):
                        pe.wait_ge(s_add, n * Q + q + 1)
                        pe.sem_inc(idle["pe"], 1)
                        bank = (u % 2) * Q + q
                        pe.matmul(pm[:, bank, 0:FEAT], oh[:, u, q, :], rows[:, u, q, :], start=True, stop=True)
                        pe.matmul(pm[:, bank, FEAT:FEAT + 1], oh[:, u, q, :], k.ones[:, 0:1], start=True, stop=True).then_inc(s_mm, 1)

        @block.vector
        def _(dve):
            dve.sem_inc(s_add, 2 * Q)
            dve.memset(zero[:, :], 0.0).then_inc(s_z, 1)
            dve.memset(k.big2[:, :, :], 0.0).then_inc(s_m0, 1)
            dve.wait_ge(s_m0, 1)
            dve.wait_ge(s_in, loaded)

            def prepare(n, u):
                cols = bass.ds(n * Q, Q)
                dve.tensor_copy(idx[:, u, :], edges[:, cols, 1]).then_inc(s_idx, 1)
                dve.tensor_tensor(oh[:, u, :, :], k.iota[:, :].unsqueeze(1).to_broadcast([P, Q, P]),
                                  edges[:, cols, 0:1].to_broadcast([P, Q, P]), ALU.is_equal).then_inc(s_oh, 1)

            def add(n, u, more):
                if more:
                    dve.wait_ge(s_mm, n * Q + Q)
                    dve.sem_inc(idle["dve"], 1)
                    prepare(n + B, u)
                for q in range(Q):
                    b = dve.value_load(tab[0:1, bass.ds(n * Q + q, 1)], min_val=0, max_val=NTILE - 1)
                    m = k.big2[:, bass.ds(b, 1), :].rearrange("p a n -> p (a n)")
                    dve.wait_ge(s_mm, n * Q + q + 1)
                    dve.wait_ge(s_add, n * Q + q + 2 * Q)
                    dve.sem_inc(idle["dve"], 1)
                    dve.tensor_tensor(m, m, pm[:, (u % 2) * Q + q, 0:FEAT + 1], ALU.add).then_inc(s_add, 1)
            for u in range(B):
                prepare(u, u)
            with dve.Fori(0, NI // B - 1) as i:
                for u in range(B):
                    add(i * B + u, u, True)
            for u in range(B):
                add(NI - B + u, u, False)


def phase_route(nc, k):
    with ExitStack() as ctx:
        sb = lambda n, s, d: ctx.enter_context(nc.sbuf_tensor(n, s, d))
        ps = lambda n, s, d: ctx.enter_context(nc.psum_tensor(n, s, d))
        sem = k.sem
        G, E = 7, EXPERTS
        Wc = sb("Wc", [P, 4, FEAT], F32)
        Wg = sb("Wg", [P, 2, E], F32)
        bias = sb("bias3", [P, 2, FEAT], F32)
        bg = sb("bgb", [P, E], F32)
        din = sb("din", [P, NTILE], F32)
        st = sb("st", [P, 2, 4, P], F32)
        sT = sb("sT", [P, 2, 4, P], F32)
        x3 = sb("x3", [P, 2, FEAT], F32)
        x3T = sb("x3T", [P, 2, 2, P], F32)
        L = sb("L", [P, NTILE, E], F32)
        A = [sb("A0", [P, NTILE, E], F32), sb("A1", [P, NTILE, E], F32)]
        T = sb("T", [P, NTILE, E], F32)
        rank = sb("rank", [P, NTILE, E], F32)
        before = sb("before", [P, NTILE + 1, E], F32)
        v = sb("v", [P, 2, NTILE], F32)
        first = sb("first", [P, NTILE], F32)
        valid = sb("valid", [P, NTILE], F32)
        rowmask = sb("rowmask", [P, 1], F32)
        e3 = sb("e3", [P, 3, E], F32)
        e3i = sb("e3i", [P, E], I32)
        tn2 = sb("tn2", [P, 2], F32)
        cmp2 = sb("cmp2", [P, 2, E], F32)
        t2f = sb("t2f", [P, 2], F32)
        t2i = sb("t2i", [P, 2], I32)
        pT = ps("pTf", [P, 2, 4, P], F32)
        pX = ps("pXf", [P, 2, BANK], F32)
        p3 = ps("p3", [P, 2, 2, P], F32)
        pL = ps("pL", [P, 2, E], F32)
        pR = ps("pR", [P, BANK], F32)
        pS = ps("pS", [P, BANK], F32)

        s_w, loaded = k.inputs(96)
        s_cst = sem("f_constants")
        s_sq = sem("indegree_root")
        s_din = sem("indegree_ready")
        s_m = sem("m_staged")
        s_x = sem("x2_staged")
        s_tr = sem("f_transposed")
        s_sT = sem("f_transposes_copied")
        s_mm = sem("x3_summed")
        s_x3 = sem("x3_ready")
        s_tr3 = sem("x3_transposed")
        s_x3T = sem("x3T_ready")
        s_lg = sem("logits_summed")
        s_keep = sem("x3_kept")
        s_L = sem("logits_ready")
        s_dv = sem("gate_difference")
        s_ex = sem("gate_exp")
        s_A = sem("choices_ready")
        s_pr = sem("prefix_summed")
        s_prc = sem("prefix_copied")
        s_tab = sem("expert_table_ready")
        s_out = sem("expert_table_stored")
        idle = k.idle
        block = ctx.enter_context(nc.Block())

        def tiles(eng, body):
            with eng.Fori(0, NTILE // 2) as i:
                for u in range(2):
                    body(i * 2 + u, u)
            body(NTILE - 1, 0)

        @block.sync
        def _(sp):
            sp.dma_start(Wc[:, 0:2, :], k.W_gc.rearrange("(c p) n -> p c n", p=P)).then_inc(s_w, 16)
            sp.dma_start(Wc[:, 2:4, :], k.W_res.rearrange("(c p) n -> p c n", p=P)).then_inc(s_w, 16)
            sp.dma_start(Wg[:, :, :], k.Wg.rearrange("(c p) n -> p c n", p=P)).then_inc(s_w, 16)
            sp.dma_start(bias[:, 0, :], k.b_gc.partition_broadcast(P)).then_inc(s_w, 16)
            sp.dma_start(bias[:, 1, :], k.b_res.partition_broadcast(P)).then_inc(s_w, 16)
            sp.dma_start(bg[:, :], k.bg.partition_broadcast(P)).then_inc(s_w, 16)
            sp.wait_ge(s_tab, 1)
            sp.dma_start(k.etab.rearrange("a (p t) -> (a p) t", p=P), t2i[:, :]).then_inc(s_out, 16)
            sp.wait_ge(s_out, 16)

        @block.gpsimd
        def _(pool):
            pool.iota(tn2[:, :], [[1, 2]], base=0, channel_multiplier=2,
                      allow_small_or_imprecise_dtypes=True).then_inc(s_cst, 1)
            pool.affine_select(out=rowmask[:, :], in_=k.ones[:, 0:1], compare_op=ALU.is_ge, fill=0.0,
                               base=LAST - 1, pattern=[[0, 1]], channel_multiplier=-1).then_inc(s_cst, 1)

            def body(t, u):
                pool.wait_ge(s_tr, t + 1)
                pool.sem_inc(idle["pool"], 1)
                pool.tensor_copy(st[:, u, 2:4, :].rearrange("p c n -> p (c n)"),
                                 k.big1[:, bass.ds(t, 1), :].rearrange("p a n -> p (a n)")).then_inc(s_x, 1)
            tiles(pool, body)

        @block.tensor
        def _(pe):
            pe.wait_ge(s_w, loaded)
            pe.sem_inc(s_tr, 2)
            pe.sem_inc(s_mm, 2)

            def body(t, u):
                pe.wait_ge(s_m, t + 1)
                pe.wait_ge(s_x, t + 1)
                pe.wait_ge(s_sT, t + 1)
                pe.sem_inc(idle["pe"], 1)
                for c in range(4):
                    last = pe.transpose(pT[:, u, c, :], st[:, u, c, :], k.ident[:, :])
                last.then_inc(s_tr, 1)
                pe.wait_ge(s_sT, t + 3)
                pe.wait_ge(s_x3, t + 1)
                pe.sem_inc(idle["pe"], 1)
                for c in range(4):
                    last = pe.matmul(pX[:, u, 0:FEAT], sT[:, u, c, :], Wc[:, c, :], start=(c == 0), stop=(c == 3))
                last.then_inc(s_mm, 1)
                pe.wait_ge(s_x3, t + 3)
                pe.wait_ge(s_x3T, t + 1)
                pe.sem_inc(idle["pe"], 1)
                for c in range(2):
                    last = pe.transpose(p3[:, u, c, :], x3[:, u, c * P:(c + 1) * P], k.ident[:, :])
                last.then_inc(s_tr3, 1)
                pe.wait_ge(s_x3T, t + 3)
                pe.wait_ge(s_L, t + 1)
                pe.sem_inc(idle["pe"], 1)
                for c in range(2):
                    last = pe.matmul(pL[:, u, :], x3T[:, u, c, :], Wg[:, c, :], start=(c == 0), stop=(c == 1))
                last.then_inc(s_lg, 1)
            tiles(pe, body)
            pe.wait_ge(s_A, 1)
            for r in range(NTILE // G):
                rhs = T[:, r * G:(r + 1) * G, :].rearrange("p i e -> p (i e)")
                if r:
                    pe.wait_ge(s_prc, 2 * r)
                pe.matmul(pR[:, 0:G * E], k.upper[:, :], rhs, start=True, stop=True)
                pe.matmul(pS[:, 0:G * E], k.ones[:, :], rhs, start=True, stop=True).then_inc(s_pr, 1)

        @block.scalar
        def _(act):
            act.sem_inc(s_sT, 2)
            act.sem_inc(s_x3T, 2)
            act.sem_inc(s_keep, 2)
            act.wait_ge(s_sq, 1)
            act.activation(din[:, :], din[:, :], ACT.Sqrt).then_inc(s_sq, 1)

            def body(t, u):
                act.wait_ge(s_mm, t + 1)
                act.wait_ge(s_tr, t + 3)
                act.sem_inc(idle["act"], 1)
                act.activation(sT[:, u, :, :], pT[:, u, :, :], ACT.Copy).then_inc(s_sT, 1)
                act.wait_ge(s_x3, t + 3)
                act.sem_inc(idle["act"], 1)
                act.activation(k.big2[:, bass.ds(t, 1), 0:FEAT].rearrange("p a n -> p (a n)"), x3[:, u, :],
                               ACT.Copy).then_inc(s_keep, 1)
                act.wait_ge(s_tr3, t + 1)
                act.sem_inc(idle["act"], 1)
                act.activation(x3T[:, u, :, :], p3[:, u, :, :], ACT.Copy).then_inc(s_x3T, 1)
            tiles(act, body)
            act.wait_ge(s_dv, 1)
            act.activation(k.gate[:, 1, :], v[:, 1, :], ACT.Exp).then_inc(s_ex, 1)

        @block.vector
        def _(dve):
            o = k.order.on(dve)
            dve.sem_inc(s_x3, 2)
            dve.sem_inc(s_L, 2)
            o(dve.tensor_scalar(din[:, :], k.big2[:, :, FEAT], 1.0, None, ALU.max))
            dve.sem_inc(s_sq, 1)
            dve.wait_ge(s_sq, 2)
            o(dve.reciprocal(din[:, :], din[:, :]))
            dve.wait_ge(s_w, loaded)
            o(dve.tensor_tensor(bias[:, 0, :], bias[:, 0, :], bias[:, 1, :], ALU.add))

            def stage(t, u):
                dve.wait_ge(s_tr, t + 1)
                dve.sem_inc(idle["dve"], 1)
                dve.tensor_scalar(st[:, u, 0:2, :].rearrange("p c n -> p (c n)"),
                                  k.big2[:, bass.ds(t, 1), 0:FEAT].rearrange("p a n -> p (a n)"),
                                  din[:, bass.ds(t, 1)], None, ALU.mult).then_inc(s_m, 1)

            def body(t, u):
                stage(t, u)
                dve.wait_ge(s_mm, t + 3)
                dve.wait_ge(s_keep, t + 1)
                dve.sem_inc(idle["dve"], 1)
                dve.tensor_tensor(x3[:, u, :], pX[:, u, 0:FEAT], bias[:, 0, :], ALU.add).then_inc(s_x3, 1)
                dve.wait_ge(s_lg, t + 1)
                dve.sem_inc(idle["dve"], 1)
                dve.tensor_tensor(L[:, bass.ds(t, 1), :].rearrange("p a n -> p (a n)"), pL[:, u, :], bg[:, :],
                                  ALU.add).then_inc(s_L, 1)
            tiles(dve, body)
            dve.wait_ge(s_L, NTILE + 2)
            dve.wait_ge(s_cst, 2)
            wide = lambda t: t.unsqueeze(2).to_broadcast([P, NTILE, E])
            num = k.iota[:, 0:E].unsqueeze(1).to_broadcast([P, NTILE, E])
            for j in range(2):
                o(dve.tensor_reduce(v[:, j, :], L[:, :, :], X, ALU.max))
                o(dve.tensor_tensor(T[:, :, :], L[:, :, :], wide(v[:, j, :]), ALU.is_lt))
                o(dve.scalar_tensor_tensor(T[:, :, :], T[:, :, :], 1024.0, num, ALU.mult, ALU.add))
                o(dve.tensor_reduce(first[:, :], T[:, :, :], X, ALU.min))
                o(dve.tensor_tensor(A[j][:, :, :], num, wide(first[:, :]), ALU.is_equal))
                if j == 0:
                    o(dve.scalar_tensor_tensor(L[:, :, :], A[0][:, :, :], -1e30, L[:, :, :], ALU.mult, ALU.add))
                o(dve.tensor_scalar(A[j][:, NTILE - 1, :], A[j][:, NTILE - 1, :], rowmask[:, :], None, ALU.mult))
            o(dve.tensor_tensor(v[:, 1, :], v[:, 1, :], v[:, 0, :], ALU.subtract))
            dve.sem_inc(s_dv, 1)
            o(dve.tensor_tensor(T[:, :, :], A[0][:, :, :], A[1][:, :, :], ALU.add))
            dve.sem_inc(s_A, 1)
            for r in range(NTILE // G):
                dve.wait_ge(s_pr, r + 1)
                dve.tensor_copy(rank[:, r * G:(r + 1) * G, :].rearrange("p i e -> p (i e)"), pR[:, 0:G * E]).then_inc(s_prc, 1)
                dve.tensor_copy(before[:, r * G + 1:(r + 1) * G + 1, :].rearrange("p i e -> p (i e)"),
                                pS[:, 0:G * E]).then_inc(s_prc, 1)
            dve.wait_ge(s_prc, 2 * (NTILE // G))
            o(dve.memset(before[:, 0, :], 0.0))
            with dve.Fori(0, NTILE) as t:
                o.enter(t, 1)
                at = lambda d: before[:, bass.ds(t + d, 1), :].rearrange("p a n -> p (a n)")
                o(dve.tensor_tensor(at(1), at(1), at(0), ALU.add))
                dve.sem_inc(idle["dve"], 1)
                o.leave(NTILE)
            o(dve.tensor_tensor(rank[:, :, :], rank[:, :, :], before[:, 0:NTILE, :], ALU.add))
            o(dve.tensor_scalar(e3[:, 0, :], before[:, NTILE, :], float(CAP), float(P - 1), ALU.min, ALU.add))
            o(dve.tensor_copy(e3i[:, :], e3[:, 0, :]))
            o(dve.tensor_scalar(e3i[:, :], e3i[:, :], 7, None, ALU.arith_shift_right))
            o(dve.tensor_copy(e3[:, 0, :], e3i[:, :]))
            o(dve.tensor_tensor_scan(e3[:, 1, :], k.ones[:, 0:E], e3[:, 0, :], 0.0, ALU.mult, ALU.add))
            o(dve.tensor_tensor(e3[:, 2, :], e3[:, 1, :], e3[:, 0, :], ALU.subtract))
            o(dve.tensor_scalar(e3[:, 2, :], e3[:, 2, :], float(P), None, ALU.mult))
            o(dve.tensor_tensor(cmp2[:, :, :], e3[:, 1, :].unsqueeze(1).to_broadcast([P, 2, E]),
                                tn2[:, :].unsqueeze(2).to_broadcast([P, 2, E]), ALU.is_le))
            o(dve.tensor_reduce(t2f[:, :], cmp2[:, :, :], X, ALU.add))
            o(dve.tensor_scalar(t2f[:, :], t2f[:, :], float(E - 1), None, ALU.min))
            o(dve.tensor_copy(t2i[:, :], t2f[:, :]))
            dve.sem_inc(s_tab, 1)
            dve.wait_ge(s_ex, 1)
            o(dve.tensor_scalar(k.gate[:, 0, :], k.gate[:, 1, :], 1.0, None, ALU.add))
            o(dve.reciprocal(k.gate[:, 0, :], k.gate[:, 0, :]))
            o(dve.tensor_tensor(k.gate[:, 1, :], k.gate[:, 1, :], k.gate[:, 0, :], ALU.mult))
            o(dve.tensor_scalar(L[:, :, :], rank[:, :, :], float(CAP), None, ALU.is_lt))
            o(dve.tensor_tensor(rank[:, :, :], rank[:, :, :], e3[:, 2, :].unsqueeze(1).to_broadcast([P, NTILE, E]), ALU.add))
            for j in range(2):
                o(dve.tensor_tensor(T[:, :, :], A[j][:, :, :], L[:, :, :], ALU.mult))
                o(dve.tensor_reduce(valid[:, :], T[:, :, :], X, ALU.add))
                o(dve.tensor_tensor(T[:, :, :], T[:, :, :], rank[:, :, :], ALU.mult))
                o(dve.tensor_reduce(k.gidx[:, :, j], T[:, :, :], X, ALU.add))
                o(dve.tensor_tensor(k.gate[:, j, :], k.gate[:, j, :], valid[:, :], ALU.mult))
                o(dve.tensor_scalar(valid[:, :], valid[:, :], -SKIP, SKIP, ALU.mult, ALU.add))
                o(dve.tensor_tensor(k.sidx[:, :, j], k.gidx[:, :, j], valid[:, :], ALU.add))


def phase_dispatch(nc, k):
    with ExitStack() as ctx:
        sb = lambda n, s, d: ctx.enter_context(nc.sbuf_tensor(n, s, d))
        sem = k.sem
        idx = sb("didx", [P, 2, 2], I32)
        rows = sb("drows", [P, 2, FEAT], F32)
        s_st = sem("rows_staged")
        s_sc = [sem("rows_scattered0"), sem("rows_scattered1")]
        idle = k.idle
        block = ctx.enter_context(nc.Block())

        @block.scalar
        def _(act):
            def stage(t, u, used):
                if used is not None:
                    act.wait_ge(s_sc[u], used)
                    act.sem_inc(idle["act"], 1)
                act.activation(idx[:, u, :], k.sidx[:, bass.ds(t, 1), :].rearrange("p a n -> p (a n)"), ACT.Copy).then_inc(s_st, 1)
                act.activation(rows[:, u, :], k.big2[:, bass.ds(t, 1), 0:FEAT].rearrange("p a n -> p (a n)"), ACT.Copy).then_inc(s_st, 1)
            for u in range(2):
                stage(u, u, None)
            with act.Fori(1, NTILE // 2) as i:
                for u in range(2):
                    stage(i * 2 + u, u, i * 32)
            stage(NTILE - 1, 0, 32 * (NTILE // 2))

        @block.gpsimd
        def _(pool):
            bound = pool.to_reg(MT * P - 1)

            def scatter(t, u):
                pool.wait_ge(s_st, t * 2 + 2)
                pool.sem_inc(idle["pool"], 1)
                for j in range(2):
                    pool.indirect_dma_start(k.xbuf[:, :], bass.IndirectOffsetOnAxis(ap=idx[:, u, j:j + 1], axis=0),
                                            rows[:, u, :], None, bounds_check=bound, oob_is_err=False).then_inc(s_sc[u], 16)
            with pool.Fori(0, NTILE // 2) as i:
                for u in range(2):
                    scatter(i * 2 + u, u)
            scatter(NTILE - 1, 0)
            pool.wait_ge(s_sc[0], 32 * (NTILE // 2 + 1))
            pool.wait_ge(s_sc[1], 32 * (NTILE // 2))


def phase_experts(nc, k):
    with ExitStack() as ctx:
        sb = lambda n, s, d: ctx.enter_context(nc.sbuf_tensor(n, s, d))
        ps = lambda n, s, d: ctx.enter_context(nc.psum_tensor(n, s, d))
        sem = k.sem
        HK = HID // P
        B = 4
        tab = sb("etab", [1, 2 * P], I32)
        b1r = sb("b1r", [EXPERTS, HID], F32)
        b1T = sb("b1T", [P, HK, EXPERTS], F32)
        w1 = sb("w1", [P, B, 2, HID], F32)
        w2 = sb("w2", [P, B, HK, FEAT], F32)
        b2 = sb("b2", [1, B, FEAT], F32)
        xt = sb("xt", [P, B, FEAT], F32)
        xT = sb("xTe", [P, 2, 2, P], F32)
        hT = sb("hT", [P, 2, HK, P], F32)
        y = sb("ye", [P, 2, FEAT], F32)
        pT = ps("pTe", [P, 2, BANK], F32)
        pH = ps("pH", [P, 2, HK, P], F32)
        pY = ps("pY", [P, 2, BANK], F32)
        s_in, loaded = k.inputs(32)
        s_bt = sem("b1_transposed")
        s_b = sem("b1T_ready")
        s_ld = [sem("expert_loaded%d" % b) for b in range(B)]
        s_tr = sem("xt_transposed")
        s_xT = sem("xTe_ready")
        s_h = sem("hidden_summed")
        s_g = sem("gelu_ready")
        s_y = sem("outputs_summed")
        s_yc = sem("outputs_copied")
        s_st = [sem("outputs_stored0"), sem("outputs_stored1")]
        s_yfree = sem("output_buffer_free")
        idle = k.idle
        block = ctx.enter_context(nc.Block())

        def tiles(eng, body):
            with eng.Fori(0, MT // B) as i:
                for u in range(B):
                    body(i * B + u, u, i)
            body(MT - 1, 0, MT // B)

        @block.sync
        def _(sp):
            sp.dma_start(tab[:, :], k.etab[:, :]).then_inc(s_in, 16)
            sp.dma_start(b1r[:, :], k.b1[:, :]).then_inc(s_in, 16)
            sp.wait_ge(s_in, loaded)

            def load(t, u, i):
                e = sp.value_load(tab[0:1, bass.ds(t, 1)], min_val=0, max_val=EXPERTS - 1)
                sp.wait_ge(s_y, t + 1)
                sp.sem_inc(idle["sp"], 1)
                sp.dma_start(xt[:, u, :], k.xbuf[bass.ds(t * P, P), :]).then_inc(s_ld[u], 16)
                sp.dma_start(w1[:, u, :, :], k.w1[bass.ds(e, 1), :, :].rearrange("a (c p) n -> p (a c) n", p=P)).then_inc(s_ld[u], 16)
                sp.dma_start(w2[:, u, :, :], k.w2[bass.ds(e, 1), :, :].rearrange("a (c p) n -> p (a c) n", p=P)).then_inc(s_ld[u], 16)
                sp.dma_start(b2[:, u, :], k.b2[bass.ds(e, 1), :]).then_inc(s_ld[u], 16)
            tiles(sp, load)

        @block.tensor
        def _(pe):
            pe.wait_ge(s_in, loaded)
            for c in range(HK):
                last = pe.transpose(pT[:, 0, c * EXPERTS:(c + 1) * EXPERTS], b1r[:, c * P:(c + 1) * P],
                                    k.ident[0:EXPERTS, 0:EXPERTS])
            last.then_inc(s_bt, 1)
            pe.sem_inc(s_y, B)
            pe.sem_inc(s_h, 2)
            pe.wait_ge(s_b, 1)

            def hidden(t, w, loaded):
                u = w % 2
                pe.wait_ge(s_ld[w], loaded)
                pe.wait_ge(s_xT, t + 1)
                pe.sem_inc(idle["pe"], 1)
                for c in range(2):
                    last = pe.transpose(pT[:, u, c * P:(c + 1) * P], xt[:, w, c * P:(c + 1) * P], k.ident[:, :])
                last.then_inc(s_tr, 1)
                pe.wait_ge(s_xT, t + 3)
                pe.wait_ge(s_g, t + 1)
                pe.sem_inc(idle["pe"], 1)
                for c in range(HK):
                    for d in range(2):
                        last = pe.matmul(pH[:, u, c, :], w1[:, w, d, c * P:(c + 1) * P], xT[:, u, d, :],
                                         start=(d == 0), stop=(d == 1))
                last.then_inc(s_h, 1)

            def outputs(t, w):
                u = w % 2
                pe.wait_ge(s_yc, t + 1)
                pe.sem_inc(idle["pe"], 1)
                pe.matmul(pY[:, u, 0:FEAT], k.ones[0:1, :], b2[:, w, :], start=True, stop=False)
                pe.wait_ge(s_g, t + 3)
                pe.sem_inc(idle["pe"], 1)
                for c in range(HK):
                    last = pe.matmul(pY[:, u, 0:FEAT], hT[:, u, c, :], w2[:, w, c, :], start=False, stop=(c == HK - 1))
                last.then_inc(s_y, 1)

            hidden(0, 0, 64)
            with pe.Fori(0, MT // B) as i:
                for u in range(B):
                    hidden(i * B + u + 1, (u + 1) % B, i * 64 + (128 if u == B - 1 else 64))
                    outputs(i * B + u, u)
            outputs(MT - 1, 0)

        @block.scalar
        def _(act):
            act.wait_ge(s_in, loaded)
            act.sem_inc(s_g, 2)
            act.wait_ge(s_b, 1)

            def body(t, u, i):
                e = act.value_load(tab[0:1, bass.ds(t, 1)], min_val=0, max_val=EXPERTS - 1)
                act.wait_ge(s_h, t + 3)
                act.wait_ge(s_y, t + B - 1)
                act.sem_inc(idle["act"], 1)
                for c in range(HK):
                    last = act.activation(hT[:, u % 2, c, :], pH[:, u % 2, c, :], ACT.Gelu, bias=b1T[:, c, bass.ds(e, 1)])
                last.then_inc(s_g, 1)
            tiles(act, body)

        @block.vector
        def _(dve):
            dve.wait_ge(s_bt, 1)
            dve.tensor_copy(b1T[:, :, :].rearrange("p c e -> p (c e)"), pT[:, 0, 0:HK * EXPERTS]).then_inc(s_b, 1)
            dve.sem_inc(s_xT, 2)
            dve.sem_inc(s_yc, 2)

            def rows(t, u):
                dve.wait_ge(s_tr, t + 1)
                dve.wait_ge(s_h, t + 1)
                dve.tensor_copy(xT[:, u % 2, :, :].rearrange("p c n -> p (c n)"), pT[:, u % 2, 0:FEAT]).then_inc(s_xT, 1)

            def outputs(t, u):
                dve.wait_ge(s_y, t + B + 1)
                dve.wait_ge(s_yfree, t + 1)
                dve.tensor_copy(y[:, u % 2, :], pY[:, u % 2, 0:FEAT]).then_inc(s_yc, 1)
            rows(0, 0)
            with dve.Fori(0, MT // B) as i:
                for u in range(B):
                    rows(i * B + u + 1, u + 1)
                    outputs(i * B + u, u)
            outputs(MT - 1, 0)

        @block.gpsimd
        def _(pool):
            pool.sem_inc(s_yfree, 2)

            def store(t, u, stored):
                pool.wait_ge(s_yc, t + 3)
                pool.sem_inc(idle["pool"], 1)
                pool.dma_start(k.ybuf[bass.ds(t * P, P), :], y[:, u, :]).then_inc(s_st[u], 16)
                pool.wait_ge(s_st[u], stored)
                pool.sem_inc(s_yfree, 1)
            with pool.Fori(0, MT // 2) as i:
                for u in range(2):
                    store(i * 2 + u, u, i * 16 + 16)
            store(MT - 1, 0, 16 * (MT // 2) + 16)


def phase_combine(nc, k):
    with ExitStack() as ctx:
        sb = lambda n, s, d: ctx.enter_context(nc.sbuf_tensor(n, s, d))
        sem = k.sem
        idx = sb("cidx", [P, 2, 2], I32)
        rows = sb("crows", [P, 2, 2, FEAT], F32)
        s_idx = sem("cidx_ready")
        s_g = [sem("y_gathered0"), sem("y_gathered1")]
        s_add = sem("y_added")
        idle = k.idle
        block = ctx.enter_context(nc.Block())

        @block.gpsimd
        def _(pool):
            bound = pool.to_reg(MT * P - 1)

            def gather(t, u):
                pool.wait_ge(s_idx, t + 1)
                pool.sem_inc(idle["pool"], 1)
                for j in range(2):
                    pool.indirect_dma_start(rows[:, u, j, :], None, k.ybuf[:, :],
                                            bass.IndirectOffsetOnAxis(ap=idx[:, u, j:j + 1], axis=0),
                                            bounds_check=bound).then_inc(s_g[u], 16)
            with pool.Fori(0, NTILE // 2) as i:
                for u in range(2):
                    gather(i * 2 + u, u)
            gather(NTILE - 1, 0)

        @block.vector
        def _(dve):
            def prepare(t, u):
                dve.tensor_copy(idx[:, u, :], k.gidx[:, bass.ds(t, 1), :].rearrange("p a n -> p (a n)")).then_inc(s_idx, 1)

            def add(t, u, i):
                y = k.big2[:, bass.ds(t, 1), 0:FEAT].rearrange("p a n -> p (a n)")
                dve.wait_ge(s_g[u], i * 32 + 32)
                dve.sem_inc(idle["dve"], 1)
                for j in range(2):
                    dve.scalar_tensor_tensor(y, rows[:, u, j, :], k.gate[:, j, bass.ds(t, 1)], y, ALU.mult, ALU.add).then_inc(s_add, 1)
                    dve.wait_ge(s_add, t * 2 + j + 1)
                    dve.sem_inc(idle["dve"], 1)
            for u in range(2):
                prepare(u, u)
            with dve.Fori(0, NTILE // 2 - 1) as i:
                for u in range(2):
                    add(i * 2 + u, u, i)
                    prepare(i * 2 + u + 2, u)
            add(NTILE - 3, 0, NTILE // 2 - 1)
            prepare(NTILE - 1, 0)
            add(NTILE - 2, 1, NTILE // 2 - 1)
            add(NTILE - 1, 0, NTILE // 2)


def phase_last_norm(nc, k):
    with ExitStack() as ctx:
        sb = lambda n, s, d: ctx.enter_context(nc.sbuf_tensor(n, s, d))
        ps = lambda n, s, d: ctx.enter_context(nc.psum_tensor(n, s, d))
        sem = k.sem
        K = 7
        NR = NTILE // K
        mask = sb("maskL", [P, 1], F32)
        eps = sb("epsL", [P, 1], F32)
        col = sb("col", [P, FEAT], F32)
        col2 = sb("col2", [P, FEAT], F32)
        mean = sb("meanL", [P, FEAT], F32)
        scale = sb("scaleL", [P, FEAT], F32)
        gb = sb("gb", [P, 2, FEAT], F32)
        sq = sb("sqL", [P, K, FEAT], F32)
        mu = sb("mu", [P, NTILE], F32)
        var = sb("varL", [P, NTILE], F32)
        pc = ps("pc", [P, 2, BANK], F32)
        s_in, loaded = k.inputs(32)
        s_mask = sem("maskL_ready")
        s_c = sem("columns_ready")
        s_p = sem("columns_summed")
        s_r = sem("root_wanted")
        s_rd = sem("root_ready")
        s_o = sem("chunk_ready")
        s_out = sem("out_stored")
        block = ctx.enter_context(nc.Block())

        @block.sync
        def _(sp):
            sp.dma_start(gb[:, 0, :], k.gamma.partition_broadcast(P)).then_inc(s_in, 16)
            sp.dma_start(gb[:, 1, :], k.beta.partition_broadcast(P)).then_inc(s_in, 16)
            for r in range(NR):
                sp.wait_ge(s_o, r + 1)
                full = K if r < NR - 1 else K - 1
                sp.dma_start(k.out[r * K * P:(r * K + full) * P, :].rearrange("(i p) n -> p i n", p=P),
                             k.big1[:, r * K:r * K + full, :]).then_inc(s_out, 16)
            sp.dma_start(k.out[(NTILE - 1) * P:NODES, :], k.big1[0:LAST, NTILE - 1, :]).then_inc(s_out, 16)
            sp.wait_ge(s_out, 16 * (NR + 1))

        @block.gpsimd
        def _(pool):
            pool.affine_select(out=mask[:, :], in_=k.ones[:, 0:1], compare_op=ALU.is_ge, fill=0.0,
                               base=LAST - 1, pattern=[[0, 1]], channel_multiplier=-1).then_inc(s_mask, 1)

        @block.tensor
        def _(pe):
            for j, c in enumerate((col, col2)):
                pe.wait_ge(s_c, j + 1)
                pe.matmul(pc[:, j, 0:FEAT], k.ones[:, :], c[:, :], start=True, stop=True).then_inc(s_p, 1)

        @block.scalar
        def _(act):
            act.wait_ge(s_r, 1)
            act.activation(scale[:, :], scale[:, :], ACT.Sqrt).then_inc(s_rd, 1)
            act.wait_ge(s_r, 2)
            act.activation(var[:, :], var[:, :], ACT.Sqrt).then_inc(s_rd, 1)

        @block.vector
        def _(dve):
            o = k.order.on(dve)
            y = k.big2[:, :, 0:FEAT]
            dve.wait_ge(s_mask, 1)
            dve.wait_ge(s_in, loaded)
            o(dve.tensor_scalar(y[:, NTILE - 1, :], y[:, NTILE - 1, :], mask[:, :], None, ALU.mult))
            o(dve.tensor_reduce(col[:, :], y.rearrange("p i n -> p n i"), X, ALU.add))
            dve.sem_inc(s_c, 1)
            dve.wait_ge(s_p, 1)
            o(dve.tensor_scalar(mean[:, :], pc[:, 0, 0:FEAT], 1.0 / NODES, None, ALU.mult))
            o(dve.tensor_tensor(y, y, mean[:, :].unsqueeze(1).to_broadcast([P, NTILE, FEAT]), ALU.subtract))
            o(dve.tensor_scalar(y[:, NTILE - 1, :], y[:, NTILE - 1, :], mask[:, :], None, ALU.mult))
            for r in range(NR):
                c = y[:, r * K:(r + 1) * K, :]
                o(dve.tensor_tensor(sq[:, :, :], c, c, ALU.mult))
                o(dve.tensor_reduce((col if r else col2)[:, :], sq[:, :, :].rearrange("p i n -> p n i"), X, ALU.add))
                if r:
                    o(dve.tensor_tensor(col2[:, :], col2[:, :], col[:, :], ALU.add))
            dve.sem_inc(s_c, 1)
            dve.wait_ge(s_p, 2)
            o(dve.tensor_scalar(scale[:, :], pc[:, 1, 0:FEAT], 1.0 / NODES, EPS_LN, ALU.mult, ALU.add))
            dve.sem_inc(s_r, 1)
            dve.wait_ge(s_rd, 1)
            o(dve.reciprocal(scale[:, :], scale[:, :]))
            o(dve.tensor_tensor(scale[:, :], scale[:, :], gb[:, 0, :], ALU.mult))
            rows = lambda t: t.unsqueeze(1).to_broadcast([P, K, FEAT])
            per = lambda t, r: t[:, r * K:(r + 1) * K].unsqueeze(2).to_broadcast([P, K, FEAT])
            for r in range(NR):
                c, x = y[:, r * K:(r + 1) * K, :], k.big1[:, r * K:(r + 1) * K, :]
                o(dve.tensor_tensor(c, c, rows(scale[:, :]), ALU.mult))
                o(dve.tensor_tensor(c, c, rows(gb[:, 1, :]), ALU.add))
                o(dve.tensor_tensor(x, x, c, ALU.add))
                o(dve.tensor_reduce(mu[:, r * K:(r + 1) * K], x, X, ALU.add))
                o(dve.tensor_scalar(mu[:, r * K:(r + 1) * K], mu[:, r * K:(r + 1) * K], 1.0 / FEAT, None, ALU.mult))
                o(dve.tensor_tensor(x, x, per(mu, r), ALU.subtract))
                o(dve.tensor_tensor(sq[:, :, :], x, x, ALU.mult))
                o(dve.tensor_reduce(var[:, r * K:(r + 1) * K], sq[:, :, :], X, ALU.add))
            o(dve.tensor_scalar(var[:, :], var[:, :], 1.0 / FEAT, EPS_LN, ALU.mult, ALU.add))
            dve.sem_inc(s_r, 1)
            dve.wait_ge(s_rd, 2)
            o(dve.reciprocal(var[:, :], var[:, :]))
            for r in range(NR):
                x = k.big1[:, r * K:(r + 1) * K, :]
                dve.tensor_tensor(x, x, per(var, r), ALU.mult).then_inc(s_o, 1)


def bucket_slot(k, j):
    return k.slot[:, j, :]


PHASES = [phase_sort_and_project, phase_count, phase_softmax, phase_messages_back, phase_first_norm, phase_gather, phase_route,
          phase_dispatch, phase_experts, phase_combine, phase_last_norm]
DEBUG = []
STOP = len(PHASES)


def gnn_resnorm_kernel(nc, x, src, dst, attr, W, att, W_gc, b_gc, W_res, b_res, Wg, bg, w1, b1, w2, b2, gamma, beta, out):
    with ExitStack() as ctx:
        k = Ctx()
        k.x, k.src, k.dst, k.attr, k.W, k.att, k.out = x, src, dst, attr, W, att, out
        k.W_gc, k.b_gc, k.W_res, k.b_res, k.Wg, k.bg = W_gc, b_gc, W_res, b_res, Wg, bg
        k.w1, k.b1, k.w2, k.b2, k.gamma, k.beta = w1, b1, w2, b2, gamma, beta
        k.sem = lambda n: ctx.enter_context(nc.semaphore(n))
        k.idle = {e: k.sem("idle_" + e) for e in ("pool", "act", "pe", "sp", "dve")}
        k.inputs = Inputs(k.sem("inputs_loaded"))
        k.order = Order(None, k.sem("dve_order"))
        k.dram = lambda n, s, d: nc.dram_tensor(n, s, d, kind="ExternalOutput" if n in DEBUG else "Internal").ap()
        sb = lambda n, s, d: ctx.enter_context(nc.sbuf_tensor(n, s, d))
        k.SS = k.dram("slots_by_source", (P * NT, 2), F32)
        k.DS = k.dram("slots_by_target", (P * NT, 2), F32)
        k.tab = k.dram("tile_tables", (2, NTM), I32)
        k.R = k.dram("running_counts", (NTILE + 1, P, HC), F32)
        k.CT = k.dram("counts_transposed", (HCH, P, NTILE * P), F32)
        k.UT = k.dram("exponent_rows", (2 * HEADS, NTILE * P), F32)
        k.H = k.dram("h_table", (NTILE * P, FEAT), F32)
        k.xbuf = k.dram("expert_inputs", (MT * P, FEAT), F32)
        k.ybuf = k.dram("expert_outputs", (MT * P, FEAT), F32)
        k.etab = k.dram("expert_of_tile", (1, 2 * P), I32)
        k.bT = k.dram("b_rows", (HEADS, HCH * P), F32)
        k.ident = sb("ident", [P, P], F32)
        k.upper = sb("upper", [P, P], F32)
        k.ones = sb("ones", [P, P], F32)
        k.iota = sb("iota", [P, P], F32)
        k.a = sb("a", [P, NTILE, HEADS], F32)
        k.bE = sb("bE", [P, HCH, HEADS], F32)
        k.ends = sb("ends_int", [P, NTILE], I32)
        k.deg = sb("deg", [P, NTILE], F32)
        k.rD = sb("rD", [P, NTILE, HEADS], F32)
        k.big1 = sb("big1", [P, NTILE, FEAT], F32)
        sort = ExitStack()
        with sort:
            k.oeT = sort.enter_context(nc.sbuf_tensor("oeT", [P, 2, HCH * P], F32))
            with ExitStack() as edges:
                k.iota16 = edges.enter_context(nc.sbuf_tensor("iota16", [P, HC], F16))
                k.slot = edges.enter_context(nc.sbuf_tensor("slot", [P, 2, ECOL], F32))
                k.pay = edges.enter_context(nc.sbuf_tensor("pay", [P, 2, ECOL, 2], F32))
                for phase in PHASES[:STOP][:3]:
                    phase(nc, k)
            for phase in PHASES[:STOP][3:4]:
                phase(nc, k)
        k.gate = sb("gate", [P, 2, NTILE], F32)
        k.sidx = sb("scatter_slot", [P, NTILE, 2], F32)
        k.gidx = sb("gather_slot", [P, NTILE, 2], F32)
        k.big2 = sb("big2", [P, NTILE, FEAT + 1], F32)
        for phase in PHASES[:STOP][4:]:
            phase(nc, k)


_INS = ["x", "src", "dst", "L0_gnn_hyperedge_attr", "L0_gnn_W", "L0_gnn_att", "L1_gnn_W_gc", "L1_gnn_b_gc",
        "L1_gnn_W_res", "L1_gnn_b_res", "L1_gnn_Wg", "L1_gnn_bg", "L1_gnn_w1", "L1_gnn_b1", "L1_gnn_w2",
        "L1_gnn_b2", "L1_gnn_gamma", "L1_gnn_beta"]


def kernel(**inputs):
    import numpy as _np
    import concourse.bacc as _bacc
    from concourse import mybir as _mybir
    from concourse.bass_utils import run_bass_kernel_spmd as _run

    nc = _bacc.Bacc("TRN2", target_bir_lowering=False, num_devices=1)
    arrays, args = {}, []
    for name in _INS:
        a = _np.ascontiguousarray(inputs[name])
        arrays[f"in_{name}_dram"] = a
        args.append(nc.dram_tensor(f"in_{name}_dram", a.shape, _mybir.dt.from_np(a.dtype), kind="ExternalInput").ap())
    args.append(nc.dram_tensor("out_0_dram", (NODES, FEAT), F32, kind="ExternalOutput").ap())
    gnn_resnorm_kernel(nc, *args)
    r = _run(nc, [arrays], core_ids=[0])
    return r.results[0]["out_0_dram"]
```

```python
from contextlib import ExitStack

import concourse.bass as bass
from concourse import mybir

F32 = mybir.dt.float32
F16 = mybir.dt.float16
BF16 = mybir.dt.bfloat16
I32 = mybir.dt.int32
ALU = mybir.AluOpType
ACT = mybir.ActivationFunctionType
X = mybir.AxisListType.X

P = 128
NODES, FEAT = 6250, 256
NTILE = -(-NODES // P)
LAST = NODES - (NTILE - 1) * P
EDGES = 106250
STEP = 17
ECOL = NTILE * STEP
CHUNK = 7 * STEP
EFULL = EDGES - (P - 1) * ECOL
PAIR = 2 * P
NT = -(-2 * (EDGES // PAIR + NTILE) // 16) * 16
NTM = 4 * P
HEADS, CH = 8, 32
HYPER = 1250
HC = HYPER + 1
HCH = 10
SKIP = float(1 << 20)
BANK = 512
EPS_LN = 1e-5
EXPERTS, HID, CAP = 64, 512, 1024
MT = (2 * NODES) // P + EXPERTS
ZCOLS = 7 * FEAT
assert MT % 7 == 0 and NT // 2 <= NTM
assert P * ECOL >= EDGES and 0 < EFULL <= ECOL


class Order:

    def __init__(self, eng, sem):
        self.eng, self.sem, self.base, self.n = eng, sem, 0, 0

    def on(self, eng):
        self.eng = eng
        return self

    def __call__(self, ins):
        self.n += 1
        ins.then_inc(self.sem, 1)
        self.eng.wait_ge(self.sem, self.base + self.n)

    def enter(self, i, steps):
        self.start, self.steps = self.base + self.n, steps
        self.base, self.n = self.start + i * steps, 0

    def leave(self, count):
        assert self.n == self.steps, (self.n, self.steps)
        self.base, self.n = self.start + count * self.steps, 0


class Shared:

    def __init__(self, sem):
        self.sem, self.total = sem, 0

    def __call__(self, amount):
        self.total += amount
        return self.sem, self.total


class Ctx:
    pass


def banks(base, width):
    return [(c, min(BANK, width - c)) for c in range(0, width, BANK)]


def phase_sort_and_project(nc, k):
    with ExitStack() as ctx:
        sb = lambda n, s, d: ctx.enter_context(nc.sbuf_tensor(n, s, d))
        ps = lambda n, s, d: ctx.enter_context(nc.psum_tensor(n, s, d))
        sem = k.sem
        W = sb("W", [P, 2, FEAT], F32)
        attb = sb("attb", [P, HEADS, 2 * CH], F32)
        xin = sb("xin", [P, 2, FEAT], F32)
        xT = sb("xT", [P, 2, 2, P], F32)
        eh = sb("eh", [P, HCH, FEAT], F32)
        prod = sb("prod", [P, 7 * FEAT], F32)
        bTs = sb("bTs", [HEADS, HCH * P], F32)
        key = sb("key", [P, 2, ECOL], I32)
        keyi = sb("keyi", [P, 2, ECOL], I32)
        bucket = sb("bucket", [P, ECOL], F32)
        eq = sb("eq", [P, NTILE, CHUNK], F32)
        run = sb("run", [P, NTILE, CHUNK], F32)
        part = sb("part", [P, ECOL], F32)
        cnt = sb("cnt", [P, NTILE], F32)
        tiles = sb("tiles", [P, NTILE], F32)
        tilesi = sb("tilesi", [P, NTILE], I32)
        ends = sb("ends", [P, NTILE], F32)
        base = sb("base", [P, NTILE], F32)
        tnum = sb("tnum", [P, 4], F32)
        cmp = sb("cmp", [P, 4, NTILE], F32)
        tabf = sb("tabf", [P, 3, 4], F32)
        tabi = sb("tabi", [P, 3, 4], I32)
        numf = sb("numf", [P, NTILE], F32)
        fill = sb("fill", [P, NT, 2], F32)
        sidx = sb("sidx", [P, 2, STEP], I32)
        spay = sb("spay", [P, 2, STEP, 2], F32)
        pT = ps("pT", [P, 2, 2, P], F32)
        pX = ps("pX", [P, 2, BANK], F32)
        pC = ps("pC", [P, 2, BANK], F32)

        s_w = sem("w_loaded")
        s_x = [sem("x_loaded0"), sem("x_loaded1")]
        s_xfree = sem("x_free")
        s_xz = sem("x_buffers_zeroed")
        s_tr = sem("x_transposed")
        s_xT = sem("xT_ready")
        s_mm = sem("projected")
        s_cp = sem("projection_copied")
        s_keys = sem("keys_loaded")
        s_kset = sem("keys_padded")
        s_const = sem("constants_ready")
        s_pool = sem("pool_order_a")
        s_cnt = sem("counts_ready")
        s_tot = sem("totals_ready")
        s_slots = sem("slots_ready")
        s_stage = sem("edges_staged")
        s_scat = [sem("edges_scattered0"), sem("edges_scattered1")]
        s_fillr = sem("fill_ready")
        s_fill = sem("slots_prefilled")
        s_b = sem("b_ready")
        s_bT = sem("bT_ready")
        s_bTs = sem("bT_copied")
        s_out, stored = k.stores(64)
        s_tabs = sem("tables_ready")
        idle = k.idle

        block = ctx.enter_context(nc.Block())

        @block.sync
        def _(sp):
            sp.dma_start(W[:, :, :], k.W.rearrange("(c p) n -> p c n", p=P)).then_inc(s_w, 16)
            sp.dma_start(attb[:, :, :], k.att[0, :, :].partition_broadcast(P)).then_inc(s_w, 16)
            sp.wait_ge(s_kset, 1)
            for j, e in enumerate((k.src, k.dst)):
                sp.dma_start(key[0:P - 1, j, :], e[0:(P - 1) * ECOL].rearrange("(p t) -> p t", t=ECOL)).then_inc(s_keys, 16)
                sp.dma_start(key[P - 1:P, j, 0:EFULL], e[(P - 1) * ECOL:EDGES].rearrange("(p t) -> p t", p=1)).then_inc(s_keys, 16)
            sp.wait_ge(s_fillr, 1)
            sp.dma_start(k.SS.rearrange("(p t) c -> p t c", p=P), fill[:, :, :]).then_inc(s_fill, 16)
            sp.wait_ge(s_xz, 1)
            with sp.Fori(0, NTILE // 2) as i:
                for u in range(2):
                    sp.wait_ge(s_xfree, i * 2 + u + 1)
                    sp.dma_start(xin[:, u, :], k.x[bass.ds((i * 2 + u) * P, P), :]).then_inc(s_x[u], 16)
            sp.wait_ge(s_xfree, NTILE)
            sp.dma_start(xin[0:LAST, 0, :], k.x[(NTILE - 1) * P:NODES, :]).then_inc(s_x[0], 16)
            for c in range(HCH):
                t = NTILE + c
                rows = min(P, HYPER - c * P)
                sp.wait_ge(s_xfree, t + 1)
                sp.dma_start(xin[0:rows, t % 2, :], k.attr[c * P:c * P + rows, :]).then_inc(s_x[t % 2], 16)
                if rows < P:
                    sp.dma_start(xin[rows:rows + 1, t % 2, :], k.attr[HYPER - 1:HYPER, :]).then_inc(s_x[t % 2], 16)
            sp.wait_ge(s_bTs, 3)
            sp.dma_start(k.bT[:, :], bTs[:, :]).then_inc(s_out, 16)
            sp.wait_ge(s_tabs, 1)
            for j in range(3):
                sp.dma_start(k.tab[j, :].rearrange("(p t) -> p t", p=P), tabi[:, j, :]).then_inc(s_out, 16)
            sp.wait_ge(s_out, stored)

        @block.gpsimd
        def _(pool):
            o = Order(pool, s_pool)
            pool.memset(k.ones[:, :], 1.0).then_inc(s_const, 1)
            pool.iota(numf[:, :], [[1, NTILE]], base=0, channel_multiplier=0,
                      allow_small_or_imprecise_dtypes=True).then_inc(s_const, 1)
            pool.iota(tnum[:, :], [[2, 4]], base=0, channel_multiplier=8,
                      allow_small_or_imprecise_dtypes=True).then_inc(s_const, 1)
            pool.iota(k.iota[:, :], [[1, P]], base=0, channel_multiplier=0,
                      allow_small_or_imprecise_dtypes=True).then_inc(s_const, 1)
            pool.iota(k.iota16[:, :], [[1, HC]], base=0, channel_multiplier=0,
                      allow_small_or_imprecise_dtypes=True).then_inc(s_const, 1)
            o(pool.memset(k.ident[:, :], 0.0))
            pool.affine_select(out=k.ident[:, :], in_=k.ident[:, :], compare_op=ALU.not_equal, fill=1.0,
                               base=0, pattern=[[-1, P]], channel_multiplier=1).then_inc(s_const, 1)
            o(pool.memset(k.upper[:, :], 1.0))
            pool.affine_select(out=k.upper[:, :], in_=k.upper[:, :], compare_op=ALU.is_gt, fill=0.0,
                               base=0, pattern=[[1, P]], channel_multiplier=-1).then_inc(s_const, 1)
            pool.memset(fill[:, :, :], -1.0).then_inc(s_fillr, 1)
            bound = pool.to_reg(P * NT - 1)
            pool.wait_ge(s_fill, 16)

            def scatter(step, u):
                pool.wait_ge(s_stage, 2 * step + 2)
                pool.sem_inc(idle["pool"], 1)
                for c in range(STEP):
                    pool.indirect_dma_start(k.SS[:, :], bass.IndirectOffsetOnAxis(ap=sidx[:, u, c:c + 1], axis=0),
                                            spay[:, u, c, :], None, bounds_check=bound,
                                            oob_is_err=False).then_inc(s_scat[u], 16)
            with pool.Fori(0, NTILE // 2) as i:
                for u in range(2):
                    scatter(i * 2 + u, u)
            scatter(NTILE - 1, 0)
            pool.wait_ge(s_scat[0], 16 * STEP * (NTILE // 2 + 1))
            pool.wait_ge(s_scat[1], 16 * STEP * (NTILE // 2))

        @block.scalar
        def _(act):
            act.sem_inc(s_xfree, 2)
            act.sem_inc(s_cp, 2)

            def project(t, u, dst):
                act.wait_ge(s_tr, t + 1)
                act.activation(xT[:, u, :, :], pT[:, u, :, :], ACT.Copy).then_inc(s_xT, 1)
                act.wait_ge(s_mm, t + 1)
                act.sem_inc(idle["act"], 1)
                act.activation(dst, pX[:, u, 0:FEAT], ACT.Copy).then_inc(s_cp, 1)
            def stage(step, u, used):
                cols = bass.ds(step * STEP, STEP)
                if used is not None:
                    act.wait_ge(s_scat[u], used)
                    act.sem_inc(idle["act"], 1)
                act.wait_ge(s_slots, step + 1)
                act.sem_inc(idle["act"], 1)
                act.activation(sidx[:, u, :], k.slot[:, 0, cols], ACT.Copy).then_inc(s_stage, 1)
                act.activation(spay[:, u, :, :], k.pay[:, 0, cols, :], ACT.Copy).then_inc(s_stage, 1)
            row = lambda t: k.big1[:, bass.ds(t, 1), :].rearrange("p a n -> p (a n)")
            for u in range(2):
                project(u, u, row(u))
                stage(u, u, None)
            with act.Fori(1, NTILE // 2) as i:
                for u in range(2):
                    stage(i * 2 + u, u, 16 * STEP * i)
                    project(i * 2 + u, u, row(i * 2 + u))
            stage(NTILE - 1, 0, 16 * STEP * (NTILE // 2))
            project(NTILE - 1, 0, row(NTILE - 1))
            for c in range(HCH):
                project(NTILE + c, (NTILE + c) % 2, eh[:, c, :])
            act.wait_ge(s_bT, 1)
            act.activation(bTs[:, 0:BANK], pC[0:HEADS, 0, :], ACT.Copy).then_inc(s_bTs, 1)
            act.activation(bTs[:, BANK:2 * BANK], pC[0:HEADS, 1, :], ACT.Copy).then_inc(s_bTs, 1)
            act.activation(bTs[:, 2 * BANK:HCH * P], pX[0:HEADS, 0, 0:2 * P], ACT.Copy).then_inc(s_bTs, 1)

        @block.tensor
        def _(pe):
            pe.wait_ge(s_const, 7)
            pe.wait_ge(s_w, 32)

            def project(t, u, loaded):
                pe.wait_ge(s_x[u], loaded)
                pe.sem_inc(idle["pe"], 1)
                for c in range(2):
                    last = pe.transpose(pT[:, u, c, :], xin[:, u, c * P:(c + 1) * P], k.ident[:, :])
                last.then_inc(s_tr, 1)
                pe.wait_ge(s_xT, t + 1)
                pe.sem_inc(s_xfree, 1)
                pe.wait_ge(s_cp, t + 1)
                pe.sem_inc(idle["pe"], 1)
                for c in range(2):
                    last = pe.matmul(pX[:, u, 0:FEAT], xT[:, u, c, :], W[:, c, :], start=(c == 0), stop=(c == 1))
                last.then_inc(s_mm, 1)
            def totals(j):
                pe.wait_ge(s_cnt, j + 1)
                pe.matmul(pC[:, 0, 0:NTILE], k.ones[:, :], cnt[:, :], start=True, stop=True)
                pe.matmul(pC[:, 1, 0:NTILE], k.upper[:, :], cnt[:, :], start=True, stop=True).then_inc(s_tot, 1)
            totals(0)
            with pe.Fori(0, 8) as i:
                for u in range(2):
                    project(i * 2 + u, u, i * 16 + 16)
            totals(1)
            with pe.Fori(8, NTILE // 2) as i:
                for u in range(2):
                    project(i * 2 + u, u, i * 16 + 16)
            project(NTILE - 1, 0, 16 * (NTILE // 2) + 16)
            for c in range(HCH):
                t = NTILE + c
                project(t, t % 2, 16 * (t // 2) + 16 + (16 if c == HCH - 1 else 0))
            pe.wait_ge(s_b, 1)
            pe.wait_ge(s_cp, NTILE + HCH + 2)
            for c in range(HCH):
                out = pC[0:HEADS, c // 4, (c % 4) * P:(c % 4 + 1) * P] if c < 8 else pX[0:HEADS, 0, (c - 8) * P:(c - 7) * P]
                last = pe.transpose(out, k.bE[:, c, :], k.ident[:, :])
            last.then_inc(s_bT, 1)

        @block.vector
        def _(dve):
            o = k.order.on(dve)
            dve.memset(key[:, :, :], NTILE * P).then_inc(s_kset, 1)
            dve.memset(xin[:, :, :], 0.0).then_inc(s_xz, 1)
            dve.wait_ge(s_keys, 64)
            dve.wait_ge(s_const, 7)
            for j in range(2):
                o(dve.tensor_scalar(keyi[:, 0, :], key[:, j, :], P - 1, None, ALU.bitwise_and))
                o(dve.tensor_copy(k.pay[:, j, :, 0], keyi[:, 0, :]))
                if j == 0:
                    o(dve.tensor_scalar(k.pay[:, 0, :, 1], key[:, 1, :], float(HYPER), None, ALU.min))
                else:
                    o(dve.tensor_copy(k.pay[:, 1, :, 1], key[:, 0, :]))
                o(dve.tensor_scalar(keyi[:, 1, :], key[:, j, :], 7, None, ALU.arith_shift_right))
                o(dve.tensor_copy(bucket[:, :], keyi[:, 1, :]))
                eq7 = eq[:, :, :].rearrange("p a n -> p (a n)").rearrange("p (b t) -> p b t", b=7)
                for r in range(NTILE // 7):
                    o(dve.tensor_tensor(eq7, bucket[:, :].unsqueeze(1).to_broadcast([P, 7, ECOL]),
                                        numf[:, 7 * r:7 * r + 7].unsqueeze(2).to_broadcast([P, 7, ECOL]), ALU.is_equal))
                    o(dve.tensor_reduce(cnt[:, 7 * r:7 * r + 7], eq7, X, ALU.add))
                dve.sem_inc(s_cnt, 1)
                dve.wait_ge(s_tot, j + 1)
                o(dve.tensor_scalar(tiles[:, :], pC[:, 0, 0:NTILE], float(PAIR - 1), None, ALU.add))
                o(dve.tensor_copy(tilesi[:, :], tiles[:, :]))
                o(dve.tensor_scalar(tilesi[:, :], tilesi[:, :], 8, None, ALU.arith_shift_right))
                o(dve.tensor_copy(tiles[:, :], tilesi[:, :]))
                o(dve.tensor_scalar(tiles[:, :], tiles[:, :], 1.0, 2.0, ALU.max, ALU.mult))
                o(dve.tensor_tensor_scan(ends[:, :], k.ones[:, 0:NTILE], tiles[:, :], 0.0, ALU.mult, ALU.add))
                o(dve.tensor_tensor(base[:, :], ends[:, :], tiles[:, :], ALU.subtract))
                o(dve.tensor_scalar(base[:, :], base[:, :], float(P), -1.0, ALU.mult, ALU.add))
                o(dve.tensor_tensor(base[:, :], base[:, :], pC[:, 1, 0:NTILE], ALU.add))
                for r in range(ECOL // CHUNK):
                    cols = slice(r * CHUNK, (r + 1) * CHUNK)
                    slot, kd, km, pt = k.slot[:, j, cols], keyi[:, 0, cols], keyi[:, 1, cols], part[:, cols]
                    o(dve.tensor_tensor(eq[:, :, :], bucket[:, cols].unsqueeze(1).to_broadcast([P, NTILE, CHUNK]),
                                        numf[:, :].unsqueeze(2).to_broadcast([P, NTILE, CHUNK]), ALU.is_equal))
                    for b in range(NTILE):
                        last = dve.tensor_tensor_scan(run[:, b, :], k.ones[:, 0:CHUNK], eq[:, b, :], base[:, b:b + 1], ALU.mult, ALU.add)
                    o(last)
                    o(dve.tensor_copy(base[:, :], run[:, :, CHUNK - 1]))
                    o(dve.tensor_tensor(run[:, :, :], run[:, :, :], eq[:, :, :], ALU.mult))
                    o(dve.tensor_reduce(slot, run[:, :, :].rearrange("p b t -> p t b"), X, ALU.add))
                    o(dve.tensor_copy(kd, slot))
                    o(dve.tensor_scalar(km, kd, 7, None, ALU.arith_shift_right))
                    o(dve.tensor_scalar(kd, kd, P - 1, None, ALU.bitwise_and))
                    o(dve.tensor_copy(pt, kd))
                    o(dve.tensor_copy(slot, km))
                    o(dve.scalar_tensor_tensor(slot, pt, float(NT), slot, ALU.mult, ALU.add))
                    o(dve.tensor_scalar(pt, bucket[:, cols], float(NTILE), SKIP, ALU.is_equal, ALU.mult))
                    o(dve.tensor_tensor(slot, slot, pt, ALU.max))
                    if j == 0:
                        dve.sem_inc(s_slots, CHUNK // STEP)
                o(dve.tensor_tensor(cmp[:, :, :], ends[:, :].unsqueeze(1).to_broadcast([P, 4, NTILE]),
                                    tnum[:, :].unsqueeze(2).to_broadcast([P, 4, NTILE]), ALU.is_le))
                o(dve.tensor_reduce(tabf[:, j, :], cmp[:, :, :], X, ALU.add))
                o(dve.tensor_scalar(tabf[:, 2 - j, :], tabf[:, j, :], float(NTILE - 1), None, ALU.min))
                if j == 0:
                    o(dve.tensor_copy(k.ends[:, :], ends[:, :]))
            o(dve.tensor_copy(tabi[:, :, :], tabf[:, :, :]))
            dve.sem_inc(s_tabs, 1)
            dve.wait_ge(s_w, 32)
            dve.wait_ge(s_cp, NTILE + HCH + 2)

            def logits(dst, rows, n, half):
                w = attb[:, :, half * CH:(half + 1) * CH].unsqueeze(1).to_broadcast([P, n, HEADS, CH])
                pv = prod[:, 0:n * FEAT].rearrange("p (i h c) -> p i h c", h=HEADS, c=CH)
                o(dve.tensor_tensor(pv, rows.rearrange("p i (h c) -> p i h c", c=CH), w, ALU.mult))
                o(dve.tensor_reduce(dst, pv, X, ALU.add))
            for r in range(NTILE // 7):
                logits(k.a[:, 7 * r:7 * r + 7, :], k.big1[:, 7 * r:7 * r + 7, :], 7, 0)
            for r in range(2):
                logits(k.bE[:, 5 * r:5 * r + 5, :], eh[:, 5 * r:5 * r + 5, :], 5, 1)
            dve.sem_inc(s_b, 1)


def phase_count(nc, k):
    with ExitStack() as ctx:
        sb = lambda n, s, d: ctx.enter_context(nc.sbuf_tensor(n, s, d))
        sem = k.sem
        Q, U = 4, 4
        edges = sb("edges", [P, NT, 2], F32)
        tab = sb("tabrow", [1, NTM], I32)
        ohn = sb("onehot_node", [P, U, Q, P], BF16)
        ohe = sb("onehot_edge", [P, U, Q, HC], BF16)
        zero = sb("zero", [P, HC], F32)
        snap = sb("snap", [P, 2, HC], F32)
        run = ctx.enter_context(nc.psum_tensor("running", [P, 3 * BANK], F32))

        s_in, loaded = k.inputs(32)
        s_z = sem("zeros_ready")
        s_oh = sem("onehots_ready")
        s_mm = sem("counted")
        s_used = sem("onehots_used")
        s_evac = sem("bucket_passed")
        s_go = sem("pair_may_count")
        s_snap = sem("count_copied")
        s_R = [sem("counts_stored0"), sem("counts_stored1")]
        idle = k.idle
        block = ctx.enter_context(nc.Block())

        @block.sync
        def _(sp):
            sp.dma_start(edges[:, :, :], k.SS.rearrange("(p t) c -> p t c", p=P)).then_inc(s_in, 16)
            sp.dma_start(tab[:, :], k.tab[0:1, :]).then_inc(s_in, 16)
            sp.wait_ge(s_in, loaded)
            with sp.Fori(0, NT // Q) as i:
                for q in range(Q // 2):
                    bucket = sp.value_load(tab[0:1, bass.ds(i * (Q // 2) + q, 1)], min_val=0, max_val=NTILE)
                    sp.wait_ge(s_evac, bucket + 1)
                    sp.sem_inc(s_go, 1)

        @block.vector
        def _(dve):
            dve.memset(zero[:, :], 0.0).then_inc(s_z, 1)
            dve.memset(ohn[:, 1, :, :], 0.0).then_inc(s_z, 1)
            dve.memset(ohe[:, 1, 0, :], 0.0).then_inc(s_z, 1)
            dve.wait_ge(s_in, loaded)
            with dve.Fori(0, NT // (U * Q)) as i:
                for u in range(U):
                    n = i * U + u
                    dve.wait_ge(s_used, n + 1)
                    dve.sem_inc(idle["dve"], 1)
                    for q in range(Q):
                        e = edges[:, bass.ds(n * Q + q, 1), :].rearrange("p a b -> p (a b)")
                        dve.tensor_scalar(ohn[:, u, q, :], k.iota16[:, 0:P], e[:, 0:1], None, ALU.is_equal).then_inc(s_oh, 1)
                        dve.tensor_scalar(ohe[:, u, q, :], k.iota16[:, :], e[:, 1:2], None, ALU.is_equal).then_inc(s_oh, 1)

        @block.tensor
        def _(pe):
            pe.wait_ge(s_z, 3)
            for c, w in banks(0, HC):
                last = pe.matmul(run[:, c:c + w], ohn[:, 1, 0, :], ohe[:, 1, 0, c:c + w], start=True, stop=True)
            last.then_inc(s_mm, 1)
            pe.wait_ge(s_mm, 1)
            pe.sem_inc(s_used, U)
            with pe.Fori(0, NT // (U * Q)) as i:
                for u in range(U):
                    n = i * U + u
                    for q in range(Q):
                        pe.wait_ge(s_oh, n * (2 * Q) + 2 * q + 2)
                        if q % 2 == 0:
                            pe.wait_ge(s_go, n * (Q // 2) + q // 2 + 1)
                        pe.sem_inc(idle["pe"], 1)
                        for c, w in banks(0, HC):
                            last = pe.matmul(run[:, c:c + w], ohn[:, u, q, :], ohe[:, u, q, c:c + w], start=False,
                                             stop=True, skip_group_check=True)
                        last.then_inc(s_mm, 1)
                    pe.wait_ge(s_mm, n * Q + Q + 1)
                    pe.sem_inc(s_used, 1)

        @block.scalar
        def _(act):
            act.sem_inc(s_evac, 1)
            act.wait_ge(s_z, 3)
            act.dma_start(k.R[0, :, :], zero[:, :]).then_inc(s_R[1], 16)
            act.wait_ge(s_in, loaded)

            def bucket(b, u, stored):
                ends = act.value_load(k.ends[0:1, bass.ds(b, 1)], min_val=1, max_val=NT)
                act.wait_ge(s_mm, ends + 1)
                if stored is not None:
                    act.wait_ge(s_R[u], stored)
                act.sem_inc(idle["act"], 1)
                act.activation(snap[:, u, :], run[:, 0:HC], ACT.Copy).then_inc(s_snap, 1)
                act.wait_ge(s_snap, b + 1)
                act.sem_inc(s_evac, 1)
                act.dma_start(k.R[bass.ds(b + 1, 1), :, :].rearrange("a p n -> (a p) n"), snap[:, u, :]).then_inc(s_R[u], 16)
            bucket(0, 0, None)
            bucket(1, 1, None)
            with act.Fori(1, NTILE // 2) as i:
                for u in range(2):
                    bucket(i * 2 + u, u, 16 * i + (16 if u else 0))
            bucket(NTILE - 1, 0, 16 * (NTILE // 2))
            act.wait_ge(s_R[0], 16 * (NTILE // 2 + 1))
            act.wait_ge(s_R[1], 16 * (NTILE // 2 + 1))


def phase_softmax(nc, k):
    with ExitStack() as ctx:
        sb = lambda n, s, d: ctx.enter_context(nc.sbuf_tensor(n, s, d))
        ps = lambda n, s, d: ctx.enter_context(nc.psum_tensor(n, s, d))
        sem = k.sem
        AWAY = (0, 2, 4)
        NA = len(AWAY)
        HALF = HEADS // 2
        bbc = sb("bbc", [P, HEADS, HC], F32)
        Ra = sb("Ra", [P, HC], F32)
        Rb = sb("Rb", [P, HC], F32)
        C = sb("C", [P, 2, HC], F32)
        M = sb("M", [P, HC], F32)
        low = sb("low", [P, 2, HC], F32)
        Pb = sb("Pb", [P, HEADS, HC], F32)
        fill = low[:, :, :].rearrange("p a n -> p (a n)")[:, 0:2 * NT].rearrange("p (t c) -> p t c", c=2)
        bmax = sb("bmax", [P, HEADS], F32)
        top = sb("top", [P, HEADS], F32)
        u16 = sb("u16", [P, 2 * HEADS], F32)
        asum = sb("asum", [P, HEADS], F32)
        dinv = sb("dinv", [P, NTILE], F32)
        degr = sb("degr", [P, 2], F32)
        ai = sb("ai", [P, 2, HEADS], F32)
        xs = sb("xs", [P, HEADS, CH], F32)
        sidx = sb("sidx2", [P, 2, STEP], I32)
        spay = sb("spay2", [P, 2, STEP, 2], F32)
        OE = ps("OE", [P, 2, 3 * BANK], F32)

        s_bbc = sem("b_loaded")
        s_r = sem("R_loaded")
        s_rfree = sem("R_used")
        s_u = sem("u_ready")
        s_t2 = sem("low_branch_ready")
        s_arg = sem("exponent_ready")
        s_e = sem("exp_ready")
        s_xs = sem("xs_ready")
        s_pm = sem("messages_added")
        s_uc = sem("u_kept")
        s_kept = sem("inverse_sums_kept")
        s_stage = sem("target_edges_staged")
        s_scat = [sem("target_edges_scattered0"), sem("target_edges_scattered1")]
        s_pw = sem("pool_weights_ready")
        s_as = sem("pool_weights_summed")
        s_fillr = sem("fillD_ready")
        s_fill = sem("DS_prefilled")
        s_z = sem("oe_zeroed")
        idle = k.idle
        block = ctx.enter_context(nc.Block())

        @block.sync
        def _(sp):
            sp.dma_start(bbc[:, :, :], k.bT[:, 0:HC].partition_broadcast(P)).then_inc(s_bbc, 16)
            sp.wait_ge(s_fillr, 2)
            sp.dma_start(k.DS.rearrange("(p t) c -> p t c", p=P), fill).then_inc(s_fill, 16)

            def load(i):
                sp.wait_ge(s_rfree, i + 1)
                sp.sem_inc(idle["sp"], 1)
                sp.dma_start(Ra[:, :], k.R[bass.ds(i, 1), :, :].rearrange("a p n -> (a p) n")).then_inc(s_r, 16)
                sp.dma_start(Rb[:, :], k.R[bass.ds(i + 1, 1), :, :].rearrange("a p n -> (a p) n")).then_inc(s_r, 16)

            with sp.Fori(0, NTILE) as i:
                load(i)

        @block.gpsimd
        def _(pool):
            pool.memset(fill[:, :, 0:1], -1.0).then_inc(s_fillr, 1)
            pool.memset(fill[:, :, 1:2], 0.0).then_inc(s_fillr, 1)
            bound = pool.to_reg(P * NT - 1)
            pool.wait_ge(s_fill, 16)

            def tile(i, u):
                pool.wait_ge(s_stage, i * 2 + 2)
                pool.sem_inc(idle["pool"], 1)
                for c in range(STEP):
                    if c in (8, 11):
                        weights(i, u, (c - 8) // 3)
                    pool.indirect_dma_start(k.DS[:, :], bass.IndirectOffsetOnAxis(ap=sidx[:, u, c:c + 1], axis=0),
                                            spay[:, u, c, :], None, bounds_check=bound, oob_is_err=False).then_inc(s_scat[u], 16)
                weights(i, u, 2)

            def weights(i, u, a):
                h = AWAY[a]
                pool.wait_ge(s_e, i * HEADS + h + 1)
                pool.sem_inc(idle["pool"], 1)
                pool.tensor_tensor(Pb[:, h, :], Pb[:, h, :], C[:, u, :], ALU.mult).then_inc(s_pw, 1)
            with pool.Fori(0, NTILE // 2) as i:
                for u in range(2):
                    tile(i * 2 + u, u)
            tile(NTILE - 1, 0)
            pool.wait_ge(s_scat[0], 16 * STEP * (NTILE // 2 + 1))
            pool.wait_ge(s_scat[1], 16 * STEP * (NTILE // 2))

        @block.vector
        def _(dve):
            o = k.order.on(dve)
            dve.sem_inc(s_rfree, 1)
            dve.sem_inc(s_arg, 2)
            o(dve.memset(M[:, :], 0.0))
            dve.sem_inc(s_z, 1)
            dve.wait_ge(s_bbc, 16)
            dve.wait_ge(s_pm, HEADS)

            def counts(i, u):
                dve.wait_ge(s_r, i * 32 + 32)
                dve.sem_inc(idle["dve"], 1)
                o(dve.scalar_tensor_tensor(C[:, u, :], Rb[:, :], 1.0, Ra[:, :], ALU.mult, ALU.subtract,
                                           accum_out=degr[:, u:u + 1]))
                dve.sem_inc(s_rfree, 1)
                o(dve.tensor_scalar(M[:, :], C[:, u, :], 0.0, -1e30, ALU.is_equal, ALU.mult))
                dve.sem_inc(idle["dve"], 1)
                dve.tensor_copy(k.deg[:, bass.ds(i, 1)], degr[:, u:u + 1])
                dve.sem_inc(idle["dve"], 1)
                o(dve.tensor_copy(ai[:, u, :], k.a[:, bass.ds(i, 1), :].rearrange("p a n -> p (a n)")))

            def tile(i, u, more):
                row = lambda t: t[:, bass.ds(i, 1), :].rearrange("p a n -> p (a n)")
                def masked(h):
                    dve.wait_ge(s_pm, i * HEADS + h + 1)
                    dve.sem_inc(idle["dve"], 1)
                    return dve.tensor_tensor_reduce(Pb[:, h, :], bbc[:, h, :], M[:, :], 1.0, -3e38, ALU.add, ALU.max, bmax[:, h:h + 1])

                def parts(g):
                    hs = slice(g * HALF, (g + 1) * HALF)
                    o(dve.tensor_tensor(bmax[:, hs], bmax[:, hs], ai[:, u, hs], ALU.add))
                    o(dve.scalar_tensor_tensor(top[:, hs], bmax[:, hs], 0.2, bmax[:, hs], ALU.mult, ALU.max))
                    dve.tensor_tensor(u16[:, hs], ai[:, u, hs], top[:, hs], ALU.subtract)
                    o(dve.scalar_tensor_tensor(u16[:, HEADS + g * HALF:HEADS + (g + 1) * HALF], ai[:, u, hs], 0.2, top[:, hs],
                                               ALU.mult, ALU.subtract))
                    dve.sem_inc(s_u, 1)

                def exponent(h):
                    dve.wait_ge(s_t2, i * HEADS + h + 1)
                    dve.scalar_tensor_tensor(Pb[:, h, :], Pb[:, h, :], u16[:, h:h + 1], low[:, h % 2, :],
                                             ALU.add, ALU.max).then_inc(s_arg, 1)

                def weights(h):
                    if h in AWAY:
                        return
                    dve.wait_ge(s_e, i * HEADS + h + 1)
                    last = dve.scalar_tensor_tensor(Pb[:, h, :], Pb[:, h, :], 1.0, C[:, u, :], ALU.mult, ALU.mult,
                                                    accum_out=asum[:, h:h + 1])
                    if h in (HALF - 1, HEADS - 1):
                        o(last)

                def normalise(g):
                    hs = slice(g * HALF, (g + 1) * HALF)
                    dve.wait_ge(s_as, i * NA + sum(h < (g + 1) * HALF for h in AWAY))
                    dve.sem_inc(idle["dve"], 1)
                    o(dve.tensor_scalar(asum[:, hs], asum[:, hs], 1e-16, None, ALU.add))
                    o(dve.reciprocal(asum[:, hs], asum[:, hs]))
                    dve.tensor_tensor(xs[:, hs, :],
                                      row(k.big1)[:, g * HALF * CH:(g + 1) * HALF * CH].rearrange("p (h c) -> p h c", c=CH),
                                      asum[:, hs].unsqueeze(2).to_broadcast([P, HALF, CH]), ALU.mult).then_inc(s_xs, 1)
                for h in range(HALF):
                    last = masked(h)
                o(last)
                parts(0)
                for h in range(HALF):
                    last = masked(HALF + h)
                    if h == HALF - 1:
                        o(last)
                    exponent(h)
                parts(1)
                if more:
                    counts(i + 1, 1 - u)
                weights(1)
                exponent(4)
                weights(3)
                exponent(5)
                exponent(6)
                normalise(0)
                exponent(7)
                weights(5)
                weights(6)
                weights(7)
                normalise(1)
            counts(0, 0)
            with dve.Fori(0, NTILE // 2) as i:
                o.enter(i, 2 * 17)
                for u in range(2):
                    tile(i * 2 + u, u, True)
                o.leave(NTILE // 2)
            tile(NTILE - 1, 0, False)
            dve.wait_ge(s_pm, HEADS * (NTILE + 1))
            dve.wait_ge(s_kept, NTILE)
            o(dve.tensor_scalar(dinv[:, :], k.deg[:, :], 1.0, None, ALU.max))
            o(dve.reciprocal(dinv[:, :], dinv[:, :]))
            o(dve.tensor_tensor(k.rD[:, :, :], k.rD[:, :, :], dinv[:, :].unsqueeze(2).to_broadcast([P, NTILE, HEADS]), ALU.mult))
            o(dve.tensor_copy(k.oeT[:, :, 0:HYPER], OE[:, :, 0:HYPER]))

        @block.scalar
        def _(act):
            act.wait_ge(s_bbc, 16)
            act.wait_ge(s_fill, 16)

            def tile(i, u, used):
                cols = bass.ds(i * STEP, STEP)
                if used is not None:
                    act.wait_ge(s_scat[u], used)
                    act.sem_inc(idle["act"], 1)
                act.activation(sidx[:, u, :], k.slot[:, 1, cols], ACT.Copy).then_inc(s_stage, 1)
                act.activation(spay[:, u, :, :], k.pay[:, 1, cols, :], ACT.Copy).then_inc(s_stage, 1)
                act.wait_ge(s_u, i * 2 + 1)
                act.sem_inc(idle["act"], 1)
                for h in range(HEADS + 1):
                    if h == HALF:
                        act.wait_ge(s_u, i * 2 + 2)
                        act.sem_inc(idle["act"], 1)
                        act.activation(k.u[:, bass.ds(i, 1), :].rearrange("p a n -> p (a n)"), u16[:, :], ACT.Copy).then_inc(s_uc, 1)
                    if h < HEADS:
                        act.wait_ge(s_arg, i * HEADS + h + 1)
                        act.activation(low[:, h % 2, :], Pb[:, h, :], ACT.Identity, bias=u16[:, HEADS + h:HEADS + h + 1],
                                       scale=0.2).then_inc(s_t2, 1)
                    if h:
                        act.wait_ge(s_arg, i * HEADS + h + 2)
                        act.activation(Pb[:, h - 1, :], Pb[:, h - 1, :], ACT.Exp).then_inc(s_e, 1)
                    if h >= HALF and h % 2 == 0:
                        a = (h - HALF) // 2
                        act.wait_ge(s_pw, i * NA + a + 1)
                        act.sem_inc(idle["act"], 1)
                        act.activation(Pb[:, AWAY[a], :], Pb[:, AWAY[a], :], ACT.Copy,
                                       accum_out=asum[:, AWAY[a]:AWAY[a] + 1]).then_inc(s_as, 1)
                act.wait_ge(s_xs, i * 2 + 2)
                act.sem_inc(idle["act"], 1)
                act.activation(k.rD[:, bass.ds(i, 1), :].rearrange("p a n -> p (a n)"), asum[:, :], ACT.Copy).then_inc(s_kept, 1)
            for u in range(2):
                tile(u, u, None)
            with act.Fori(1, NTILE // 2) as i:
                for u in range(2):
                    tile(i * 2 + u, u, 16 * STEP * i)
            tile(NTILE - 1, 0, 16 * STEP * (NTILE // 2))
            act.wait_ge(s_uc, NTILE)

        @block.tensor
        def _(pe):
            pe.wait_ge(s_z, 1)
            for g in range(2):
                for c, w in banks(0, HC):
                    last = pe.matmul(OE[:, g, c:c + w], M[:, 0:P], M[:, c:c + w], start=True, stop=True)
            last.then_inc(s_pm, 1)
            pe.wait_ge(s_pm, 1)
            pe.sem_inc(s_pm, HEADS - 1)

            def tile(i):
                for h in range(HEADS):
                    g, j = divmod(h, 4)
                    if h % HALF == 0:
                        pe.wait_ge(s_xs, i * 2 + g + 1)
                        pe.sem_inc(idle["pe"], 1)
                    for c, w in banks(0, HYPER):
                        last = pe.matmul(OE[CH * j:CH * j + CH, g, c:c + w], xs[:, h, :], Pb[:, h, c:c + w],
                                         start=False, stop=True, skip_group_check=True)
                    last.then_inc(s_pm, 1)
            with pe.Fori(0, NTILE) as i:
                tile(i)


def phase_messages_back(nc, k):
    with ExitStack() as ctx:
        sb = lambda n, s, d: ctx.enter_context(nc.sbuf_tensor(n, s, d))
        ps = lambda n, s, d: ctx.enter_context(nc.psum_tensor(n, s, d))
        sem = k.sem
        Q, B = 4, 4
        NI = NT // Q
        ROW = FEAT + HEADS
        Rl = sb("R_last", [P, HYPER], F32)
        binv = sb("binv", [P, HYPER], F32)
        oeb = sb("oeb", [P, HCH, ROW], F32)
        edges = sb("edgesS", [P, NT, 2], F32)
        tab = sb("tabrowS", [1, NTM], I32)
        idx = sb("idxS", [P, B, Q], I32)
        oh = sb("ohS", [P, B, Q, P], F32)
        ohT = sb("ohTS", [P, 2, Q, P], BF16)
        u3 = sb("u3", [P, NTILE, 3, 2 * HEADS], BF16)
        rest = sb("u_rest", [P, NTILE, 2 * HEADS], F32)
        uq = sb("uq", [P, 2, Q // 2, 3, 2 * HEADS], BF16)
        rows = sb("rowsS", [P, B, Q, ROW], F32)
        z = sb("zS", [P, Q, HEADS], F32)
        low = sb("lowS", [P, Q, HEADS], F32)
        w = sb("wS", [P, 2, Q, HEADS], F32)
        pO = ps("pO", [P, 2, Q, P], F32)
        pU = ps("pU", [P, 2, BANK], F32)
        pm = ps("pmS", [P, 2 * (Q // 2), BANK], F32)

        s_in, loaded = k.inputs(48)
        s_bc = sem("column_sums")
        s_sc = sem("oe_scaled")
        s_tp = sem("oe_transposed")
        s_oe = sem("oe_ready")
        s_tb = sem("hyperedge_rows_stored")
        s_z = sem("messages_zeroed")
        s_u3 = sem("u_parts_ready")
        s_idx = sem("source_idx_ready")
        s_oh = sem("source_oh_ready")
        s_g = [sem("hyperedge_rows_gathered%d" % b) for b in range(B)]
        s_T = sem("oh_transposed")
        s_Tc = sem("oh_transposes_copied")
        s_uq = sem("bucket_u_copied")
        s_U = sem("edge_u_summed")
        s_arg = sem("edge_exponents_ready")
        s_e = sem("edge_exps_ready")
        s_mul = sem("rows_weighted")
        s_mm = sem("messages_summed")
        s_add = sem("messages_kept")
        idle = k.idle
        block = ctx.enter_context(nc.Block())

        @block.sync
        def _(sp):
            sp.dma_start(Rl[:, :], k.R[NTILE, :, 0:HYPER]).then_inc(s_in, 16)
            sp.dma_start(edges[:, :, :], k.SS.rearrange("(p t) c -> p t c", p=P)).then_inc(s_in, 16)
            sp.dma_start(tab[:, :], k.tab[2:3, :]).then_inc(s_in, 16)
            sp.wait_ge(s_oe, HCH // 2 + 1)
            sp.dma_start(k.OEB.rearrange("(c p) n -> p c n", p=P), oeb[:, :, :]).then_inc(s_tb, 16)

        @block.gpsimd
        def _(pool):
            bound = pool.to_reg(HCH * P - 1)
            pool.wait_ge(s_tb, 16)
            with pool.Fori(0, NI // B) as i:
                for u in range(B):
                    pool.wait_ge(s_idx, i * B + u + 1)
                    pool.sem_inc(idle["pool"], 1)
                    for q in range(Q):
                        pool.indirect_dma_start(rows[:, u, q, :], None, k.OEB[:, :],
                                                bass.IndirectOffsetOnAxis(ap=idx[:, u, q:q + 1], axis=0),
                                                bounds_check=bound).then_inc(s_g[u], 16)

        @block.tensor
        def _(pe):
            pe.wait_ge(s_in, loaded)
            for c, n in banks(0, HYPER):
                last = pe.matmul(pm[:, c // BANK, 0:n], k.ones[:, :], Rl[:, c:c + n], start=True, stop=True)
            last.then_inc(s_bc, 1)
            pe.wait_ge(s_sc, 1)
            for r in range(HCH // 2):
                if r >= 2:
                    pe.wait_ge(s_oe, r)
                for c in range(2):
                    for g in range(2):
                        last = pe.transpose(pO[:, r % 2, 2 * c + g, :], k.oeT[:, g, (2 * r + c) * P:(2 * r + c + 1) * P],
                                            k.ident[:, :])
                last.then_inc(s_tp, 1)
            pe.wait_ge(s_oe, HCH // 2 + 1)

            def transpose(n, u):
                pe.wait_ge(s_oh, n + 1)
                pe.wait_ge(s_Tc, n + 1)
                pe.sem_inc(idle["pe"], 1)
                for q in range(Q):
                    last = pe.transpose(pO[:, u % 2, q, :], oh[:, u % B, q, :], k.ident[:, :])
                last.then_inc(s_T, 1)

            def edge_u(n, u):
                pe.wait_ge(s_Tc, n + 3)
                pe.wait_ge(s_uq, n * (Q // 2) + Q // 2)
                pe.wait_ge(s_arg, n + 1)
                pe.sem_inc(idle["pe"], 1)
                for q in range(Q):
                    for part in range(3):
                        last = pe.matmul(pU[:, u % 2, q * 2 * HEADS:(q + 1) * 2 * HEADS], ohT[:, u % 2, q, :],
                                         uq[:, u % 2, q // 2, part, :], start=(part == 0), stop=(part == 2))
                last.then_inc(s_U, 1)

            def sums(n, u):
                pe.wait_ge(s_mul, n + 1)
                pe.sem_inc(idle["pe"], 1)
                for q in range(Q):
                    g = q // 2
                    if q % 2 == 0:
                        pe.wait_ge(s_add, n * (Q // 2) + g + 1)
                        pe.sem_inc(idle["pe"], 1)
                    last = pe.matmul(pm[:, (u % 2) * (Q // 2) + g, 0:FEAT], oh[:, u % B, q, :], rows[:, u % B, q, 0:FEAT],
                                     start=(q % 2 == 0), stop=(q % 2 == 1))
                    if q % 2:
                        last.then_inc(s_mm, 1)

            transpose(0, 0)
            transpose(1, 1)
            edge_u(0, 0)

            def step(n, u, left):
                if left > 1:
                    edge_u(n + 1, u + 1)
                if left > 2:
                    transpose(n + 2, u + 2)
                sums(n, u)
            with pe.Fori(0, NI // B - 1) as i:
                for u in range(B):
                    step(i * B + u, u, B)
            for u in range(B):
                step(NI - B + u, u, B - u)

        @block.scalar
        def _(act):
            act.wait_ge(s_in, loaded)
            for r in range(HCH // 2):
                act.wait_ge(s_tp, r + 1)
                act.activation(oeb[:, 2 * r:2 * r + 2, 0:FEAT], pO[:, r % 2, :, :].rearrange("p (c g) n -> p c (g n)", c=2),
                               ACT.Copy).then_inc(s_oe, 1)
            act.activation(oeb[:, :, FEAT:], k.bE[:, :, :], ACT.Copy).then_inc(s_oe, 1)
            act.sem_inc(s_Tc, 2)

            def copy(n, u):
                act.wait_ge(s_T, n + 1)
                act.wait_ge(s_U, n + 1)
                act.sem_inc(idle["act"], 1)
                act.activation(ohT[:, u % 2, :, :], pO[:, u % 2, :, :], ACT.Copy).then_inc(s_Tc, 1)
                for q in range(Q // 2):
                    b = act.value_load(tab[0:1, bass.ds(n * (Q // 2) + q, 1)], min_val=0, max_val=NTILE - 1)
                    act.activation(uq[:, u % 2, q, :, :].rearrange("p s n -> p (s n)"),
                                   u3[:, bass.ds(b, 1), :, :].rearrange("p a s n -> p (a s n)"), ACT.Copy).then_inc(s_uq, 1)

            def exp(n, u):
                act.wait_ge(s_arg, n + 3)
                act.sem_inc(idle["act"], 1)
                act.activation(w[:, u % 2, :, :], z[:, :, :], ACT.Exp).then_inc(s_e, 1)
            act.wait_ge(s_u3, 1)
            copy(0, 0)
            copy(1, 1)
            exp(0, 0)

            def step(n, u, left):
                if left > 1:
                    exp(n + 1, u + 1)
                if left > 2:
                    copy(n + 2, u + 2)
            with act.Fori(0, NI // B - 1) as i:
                for u in range(B):
                    step(i * B + u, u, B)
            for u in range(B):
                step(NI - B + u, u, B - u)

        @block.vector
        def _(dve):
            o = k.order.on(dve)
            dve.sem_inc(s_U, 2)
            dve.sem_inc(s_arg, 2)
            dve.sem_inc(s_add, Q)
            o(dve.tensor_copy(u3[:, :, 0, :], k.u[:, :, :]))
            o(dve.tensor_tensor(rest[:, :, :], k.u[:, :, :], u3[:, :, 0, :], ALU.subtract))
            o(dve.tensor_copy(u3[:, :, 1, :], rest[:, :, :]))
            o(dve.tensor_tensor(rest[:, :, :], rest[:, :, :], u3[:, :, 1, :], ALU.subtract))
            o(dve.tensor_copy(u3[:, :, 2, :], rest[:, :, :]))
            dve.sem_inc(s_u3, 1)
            dve.memset(k.big1[:, :, :], 0.0).then_inc(s_z, 1)
            dve.wait_ge(s_bc, 1)
            for c, n in banks(0, HYPER):
                o(dve.tensor_scalar(binv[:, c:c + n], pm[:, c // BANK, 0:n], 1.0, None, ALU.max))
            o(dve.reciprocal(binv[:, :], binv[:, :]))
            o(dve.tensor_tensor(k.oeT[:, :, 0:HYPER], k.oeT[:, :, 0:HYPER],
                                binv[:, :].unsqueeze(1).to_broadcast([P, 2, HYPER]), ALU.mult))
            o(dve.tensor_copy(k.oeT[:, :, HYPER:HC], k.oeT[:, :, HYPER - 1:HYPER]))
            o(dve.memset(k.oeT[:, :, HC:], 0.0))
            dve.sem_inc(s_sc, 1)
            dve.wait_ge(s_in, loaded)
            dve.wait_ge(s_z, 1)

            def prepare(n, u):
                cols = bass.ds(n * Q, Q)
                dve.tensor_scalar(idx[:, u % B, :], edges[:, cols, 1], 0.0, None, ALU.max).then_inc(s_idx, 1)
                dve.tensor_tensor(oh[:, u % B, :, :], k.iota[:, :].unsqueeze(1).to_broadcast([P, Q, P]),
                                  edges[:, cols, 0:1].to_broadcast([P, Q, P]), ALU.is_equal).then_inc(s_oh, 1)

            def exponents(n, u, gathered):
                uu = pU[:, u % 2, 0:Q * 2 * HEADS].rearrange("p (q h) -> p q h", q=Q)
                b = rows[:, u % B, :, FEAT:]
                dve.wait_ge(s_U, n + 3)
                dve.wait_ge(s_g[u % B], gathered)
                dve.sem_inc(idle["dve"], 1)
                o(dve.scalar_tensor_tensor(low[:, :, :], b, 0.2, uu[:, :, HEADS:], ALU.mult, ALU.add))
                o(dve.tensor_tensor(z[:, :, :], b, uu[:, :, 0:HEADS], ALU.add))
                o(dve.tensor_tensor(z[:, :, :], z[:, :, :], low[:, :, :], ALU.max))
                dve.tensor_scalar(z[:, :, :], z[:, :, :], 0.0, None, ALU.min).then_inc(s_arg, 1)

            def weigh(n, u):
                r = rows[:, u % B, :, 0:FEAT].rearrange("p q (h c) -> p q h c", c=CH)
                dve.wait_ge(s_e, n + 1)
                dve.tensor_tensor(r, r, w[:, u % 2, :, :].unsqueeze(3).to_broadcast([P, Q, HEADS, CH]), ALU.mult).then_inc(s_mul, 1)

            def add(n, u):
                for g in range(Q // 2):
                    b = dve.value_load(tab[0:1, bass.ds(n * (Q // 2) + g, 1)], min_val=0, max_val=NTILE - 1)
                    m = k.big1[:, bass.ds(b, 1), :].rearrange("p a n -> p (a n)")
                    dve.wait_ge(s_mm, n * (Q // 2) + g + 1)
                    dve.wait_ge(s_add, n * (Q // 2) + g + Q)
                    dve.sem_inc(idle["dve"], 1)
                    dve.tensor_tensor(m, m, pm[:, (u % 2) * (Q // 2) + g, 0:FEAT], ALU.add).then_inc(s_add, 1)
            for u in range(B):
                prepare(u, u)
            exponents(0, 0, 16 * Q)
            weigh(0, 0)

            def step(n, u, left, gathered):
                if left > 1:
                    exponents(n + 1, u + 1, gathered)
                    weigh(n + 1, u + 1)
                if left == B:
                    dve.wait_ge(s_mm, n * (Q // 2) + Q // 2)
                    dve.sem_inc(idle["dve"], 1)
                    prepare(n + B, u)
                add(n, u)
            with dve.Fori(0, NI // B - 1) as i:
                o.enter(i, 3 * B)
                for u in range(B):
                    step(i * B + u, u, B, i * (16 * Q) + (32 if u == B - 1 else 16) * Q)
                o.leave(NI // B - 1)
            for u in range(B):
                step(NI - B + u, u, min(B - u, B - 1), 16 * Q * (NI // B))
            dve.wait_ge(s_add, NI * (Q // 2) + Q)
            o(dve.tensor_tensor(k.big1[:, :, :].rearrange("p i (h c) -> p i h c", c=CH),
                                k.big1[:, :, :].rearrange("p i (h c) -> p i h c", c=CH),
                                k.rD[:, :, :].unsqueeze(3).to_broadcast([P, NTILE, HEADS, CH]), ALU.mult))


def phase_first_norm(nc, k):
    with ExitStack() as ctx:
        sb = lambda n, s, d: ctx.enter_context(nc.sbuf_tensor(n, s, d))
        sem = k.sem
        K = 7
        xc = sb("xc", [P, 2, K, FEAT], F32)
        sq = sb("sq", [P, 2, K, FEAT], F32)
        mean = sb("mean", [P, NTILE], F32)
        var = sb("var", [P, NTILE], F32)
        dsq = sb("dsq", [P, NTILE], F32)
        s_x = [sem("xc_loaded0"), sem("xc_loaded1")]
        s_z = sem("xc_zeroed")
        s_used = sem("xc_used")
        s_v = sem("variance_ready")
        s_sd = sem("deviation_ready")
        s_h = sem("h_ready")
        s_st = [sem("h_stored0"), sem("h_stored1")]
        block = ctx.enter_context(nc.Block())

        @block.sync
        def _(sp):
            for r in range(NTILE // K):
                u = r % 2
                if r < 2:
                    sp.wait_ge(s_z, 1)
                else:
                    sp.wait_ge(s_used, r - 1)
                full = K if r < NTILE // K - 1 else K - 1
                sp.dma_start(xc[:, u, 0:full, :], k.x[r * K * P:(r * K + full) * P, :].rearrange("(i p) n -> p i n", p=P)).then_inc(s_x[u], 16)
                if full < K:
                    sp.dma_start(xc[0:LAST, u, full, :], k.x[(NTILE - 1) * P:NODES, :]).then_inc(s_x[u], 16)
            for r in range(NTILE // K):
                sp.wait_ge(s_h, r + 1)
                sp.dma_start(k.H[r * K * P:(r + 1) * K * P, :].rearrange("(i p) n -> p i n", p=P), sq[:, r % 2, :, :]).then_inc(s_st[r % 2], 16)
            sp.wait_ge(s_st[0], 64)
            sp.wait_ge(s_st[1], 48)

        @block.scalar
        def _(act):
            act.wait_ge(s_v, 1)
            act.activation(var[:, :], var[:, :], ACT.Sqrt).then_inc(s_sd, 1)
            act.activation(dsq[:, :], dsq[:, :], ACT.Sqrt).then_inc(s_sd, 1)

        @block.vector
        def _(dve):
            o = k.order.on(dve)
            o(dve.memset(xc[:, :, :, :], 0.0))
            dve.sem_inc(s_z, 1)
            bc = lambda t, r: t[:, r * K:(r + 1) * K].unsqueeze(2).to_broadcast([P, K, FEAT])
            for r in range(NTILE // K):
                y = k.big1[:, r * K:(r + 1) * K, :]
                dve.wait_ge(s_x[r % 2], 16 * (r // 2 + 1) + (16 if r == NTILE // K - 1 else 0))
                o(dve.tensor_tensor(y, y, xc[:, r % 2, :, :], ALU.add))
                dve.sem_inc(s_used, 1)
                o(dve.tensor_reduce(mean[:, r * K:(r + 1) * K], y, X, ALU.add))
                o(dve.tensor_scalar(mean[:, r * K:(r + 1) * K], mean[:, r * K:(r + 1) * K], 1.0 / FEAT, None, ALU.mult))
                o(dve.tensor_tensor(y, y, bc(mean, r), ALU.subtract))
                o(dve.tensor_tensor(sq[:, 0, :, :], y, y, ALU.mult))
                o(dve.tensor_reduce(var[:, r * K:(r + 1) * K], sq[:, 0, :, :], X, ALU.add))
            o(dve.tensor_scalar(var[:, :], var[:, :], 1.0 / FEAT, EPS_LN, ALU.mult, ALU.add))
            o(dve.tensor_scalar(dsq[:, :], k.deg[:, :], 1.0, None, ALU.max))
            dve.sem_inc(s_v, 1)
            dve.wait_ge(s_sd, 2)
            o(dve.reciprocal(var[:, :], var[:, :]))
            o(dve.reciprocal(dsq[:, :], dsq[:, :]))
            for r in range(NTILE // K):
                y = k.big1[:, r * K:(r + 1) * K, :]
                o(dve.tensor_tensor(y, y, bc(var, r), ALU.mult))
                if r >= 2:
                    dve.wait_ge(s_st[r % 2], 16 * (r // 2))
                dve.tensor_tensor(sq[:, r % 2, :, :], y, bc(dsq, r), ALU.mult).then_inc(s_h, 1)


def phase_gather(nc, k):
    with ExitStack() as ctx:
        sb = lambda n, s, d: ctx.enter_context(nc.sbuf_tensor(n, s, d))
        ps = lambda n, s, d: ctx.enter_context(nc.psum_tensor(n, s, d))
        sem = k.sem
        Q, B = 4, 4
        edges = sb("edgesT", [P, NT, 2], F32)
        tab = sb("tabrowT", [1, NTM], I32)
        idx = sb("idx", [P, B, Q], I32)
        oh = sb("ohT", [P, B, Q, P], F32)
        rows = sb("rows", [P, B, Q, FEAT + 1], F32)
        zero = sb("zeroE", [P, ZCOLS], F32)
        pm = ps("pm", [P, 2 * (Q // 2), BANK], F32)
        s_z = sem("zeroE_ready")
        s_zf, stored = k.stores(16 * (MT * FEAT // ZCOLS))
        s_in, loaded = k.inputs(32)
        s_m0 = sem("m_zeroed")
        s_idx = sem("idx_ready")
        s_oh = sem("oh_ready")
        s_g = [sem("rows_gathered%d" % b) for b in range(B)]
        s_mm = sem("rows_summed")
        s_add = sem("m_added")
        idle = k.idle
        block = ctx.enter_context(nc.Block())
        NI = NT // Q

        @block.sync
        def _(sp):
            sp.dma_start(edges[:, :, :], k.DS.rearrange("(p t) c -> p t c", p=P)).then_inc(s_in, 16)
            sp.dma_start(tab[:, :], k.tab[1:2, :]).then_inc(s_in, 16)
            sp.wait_ge(s_z, 1)
            flat = k.xbuf.rearrange("(p r) n -> p (r n)", p=P)
            for c in range(MT * FEAT // ZCOLS):
                sp.dma_start(flat[:, c * ZCOLS:(c + 1) * ZCOLS], zero[:, :]).then_inc(s_zf, 16)
            sp.wait_ge(s_zf, stored)

        @block.gpsimd
        def _(pool):
            bound = pool.to_reg(NTILE * P - 1)
            with pool.Fori(0, NI // B) as i:
                for u in range(B):
                    pool.wait_ge(s_idx, i * B + u + 1)
                    pool.sem_inc(idle["pool"], 1)
                    for q in range(Q):
                        pool.indirect_dma_start(rows[:, u, q, 0:FEAT], None, k.H[:, :],
                                                bass.IndirectOffsetOnAxis(ap=idx[:, u, q:q + 1], axis=0),
                                                bounds_check=bound).then_inc(s_g[u], 16)

        @block.tensor
        def _(pe):
            with pe.Fori(0, NI // B) as i:
                for u in range(B):
                    n = i * B + u
                    pe.wait_ge(s_oh, n + 1)
                    pe.wait_ge(s_g[u], i * (16 * Q) + 16 * Q)
                    pe.sem_inc(idle["pe"], 1)
                    for q in range(Q):
                        g = q // 2
                        if q % 2 == 0:
                            pe.wait_ge(s_add, n * (Q // 2) + g + 1)
                            pe.sem_inc(idle["pe"], 1)
                        last = pe.matmul(pm[:, (u % 2) * (Q // 2) + g, 0:FEAT + 1], oh[:, u, q, :], rows[:, u, q, :],
                                         start=(q % 2 == 0), stop=(q % 2 == 1))
                        if q % 2:
                            last.then_inc(s_mm, 1)

        @block.vector
        def _(dve):
            dve.sem_inc(s_add, Q)
            dve.memset(rows[:, :, :, FEAT:], 1.0).then_inc(s_m0, 1)
            dve.memset(zero[:, :], 0.0).then_inc(s_z, 1)
            dve.memset(k.big2[:, :, :], 0.0).then_inc(s_m0, 1)
            dve.wait_ge(s_m0, 2)
            dve.wait_ge(s_in, loaded)

            def prepare(n, u):
                cols = bass.ds(n * Q, Q)
                dve.tensor_copy(idx[:, u, :], edges[:, cols, 1]).then_inc(s_idx, 1)
                dve.tensor_tensor(oh[:, u, :, :], k.iota[:, :].unsqueeze(1).to_broadcast([P, Q, P]),
                                  edges[:, cols, 0:1].to_broadcast([P, Q, P]), ALU.is_equal).then_inc(s_oh, 1)

            def add(n, u, more):
                if more:
                    dve.wait_ge(s_mm, n * (Q // 2) + Q // 2)
                    dve.sem_inc(idle["dve"], 1)
                    prepare(n + B, u)
                for g in range(Q // 2):
                    b = dve.value_load(tab[0:1, bass.ds(n * (Q // 2) + g, 1)], min_val=0, max_val=NTILE - 1)
                    m = k.big2[:, bass.ds(b, 1), :].rearrange("p a n -> p (a n)")
                    dve.wait_ge(s_mm, n * (Q // 2) + g + 1)
                    dve.wait_ge(s_add, n * (Q // 2) + g + Q)
                    dve.sem_inc(idle["dve"], 1)
                    dve.tensor_tensor(m, m, pm[:, (u % 2) * (Q // 2) + g, 0:FEAT + 1], ALU.add).then_inc(s_add, 1)
            for u in range(B):
                prepare(u, u)
            with dve.Fori(0, NI // B - 1) as i:
                for u in range(B):
                    add(i * B + u, u, True)
            for u in range(B):
                add(NI - B + u, u, False)


def phase_route(nc, k):
    with ExitStack() as ctx:
        sb = lambda n, s, d: ctx.enter_context(nc.sbuf_tensor(n, s, d))
        ps = lambda n, s, d: ctx.enter_context(nc.psum_tensor(n, s, d))
        sem = k.sem
        G, E = 7, EXPERTS
        Wc = sb("Wc", [P, 4, FEAT], F32)
        Wg = sb("Wg", [P, 2, E], F32)
        bias = sb("bias3", [P, 2, FEAT], F32)
        bg = sb("bgb", [P, E], F32)
        din = sb("din", [P, NTILE], F32)
        st = sb("st", [P, 2, 4, P], F32)
        sT = sb("sT", [P, 2, 4, P], F32)
        x3 = sb("x3", [P, 2, FEAT], F32)
        x3T = sb("x3T", [P, 2, 2, P], F32)
        L = sb("L", [P, NTILE, E], F32)
        A = [sb("A0", [P, NTILE, E], F32), sb("A1", [P, NTILE, E], F32)]
        T = sb("T", [P, NTILE, E], F32)
        rank = sb("rank", [P, NTILE, E], F32)
        chosen = sb("chosen", [P, NTILE, E], F32)
        v = sb("v", [P, 2, NTILE], F32)
        first = sb("first", [P, NTILE], F32)
        valid = sb("valid", [P, NTILE], F32)
        rowmask = sb("rowmask", [P, 1], F32)
        e3 = sb("e3", [P, 3, E], F32)
        e3i = sb("e3i", [P, E], I32)
        tn2 = sb("tn2", [P, 2], F32)
        cmp2 = sb("cmp2", [P, 2, E], F32)
        t2f = sb("t2f", [P, 2], F32)
        t2i = sb("t2i", [P, 2], I32)
        pT = ps("pTf", [P, 2, 4, P], F32)
        pX = ps("pXf", [P, 2, BANK], F32)
        p3 = ps("p3", [P, 2, BANK], F32)
        pL = ps("pL", [P, 2, BANK], F32)
        pR, pS = pX[:, 0, :], pX[:, 1, :]

        s_w, loaded = k.inputs(96)
        s_cst = sem("f_constants")
        s_sq = sem("indegree_root")
        s_m = sem("m_staged")
        s_x = sem("x2_staged")
        s_tr = sem("f_transposed")
        s_sT = sem("f_transposes_copied")
        s_mm = sem("x3_summed")
        s_x3 = sem("x3_ready")
        s_tr3 = sem("x3_transposed")
        s_x3T = sem("x3T_ready")
        s_lg = sem("logits_summed")
        s_keep = sem("x3_kept")
        s_L = sem("logits_ready")
        s_dv = sem("gate_difference")
        s_ex = sem("gate_exp")
        s_A = sem("choices_ready")
        s_pr = sem("prefix_summed")
        s_prc = sem("prefix_copied")
        s_tab = sem("expert_table_ready")
        s_out, stored = k.stores(16)
        idle = k.idle
        block = ctx.enter_context(nc.Block())

        def tiles(eng, body):
            with eng.Fori(0, NTILE // 2) as i:
                for u in range(2):
                    body(i * 2 + u, u)
            body(NTILE - 1, 0)

        def skewed(eng, step):
            step(-2, 0, 1, 0, 0)
            step(-1, 1, 1, 1, 0)
            with eng.Fori(0, NTILE // 2 - 1) as i:
                for u in range(2):
                    step(i * 2 + u, u, 1, 1, 1)
            step(NTILE - 3, 0, 1, 1, 1)
            step(NTILE - 2, 1, 0, 1, 1)
            step(NTILE - 1, 0, 0, 0, 1)

        @block.sync
        def _(sp):
            sp.dma_start(Wc[:, 0:2, :], k.W_gc.rearrange("(c p) n -> p c n", p=P)).then_inc(s_w, 16)
            sp.dma_start(Wc[:, 2:4, :], k.W_res.rearrange("(c p) n -> p c n", p=P)).then_inc(s_w, 16)
            sp.dma_start(Wg[:, :, :], k.Wg.rearrange("(c p) n -> p c n", p=P)).then_inc(s_w, 16)
            sp.dma_start(bias[:, 0, :], k.b_gc.partition_broadcast(P)).then_inc(s_w, 16)
            sp.dma_start(bias[:, 1, :], k.b_res.partition_broadcast(P)).then_inc(s_w, 16)
            sp.dma_start(bg[:, :], k.bg.partition_broadcast(P)).then_inc(s_w, 16)
            sp.wait_ge(s_tab, 1)
            sp.dma_start(k.etab.rearrange("a (p t) -> (a p) t", p=P), t2i[:, :]).then_inc(s_out, 16)
            sp.wait_ge(s_out, stored)

        @block.gpsimd
        def _(pool):
            pool.iota(tn2[:, :], [[1, 2]], base=0, channel_multiplier=2,
                      allow_small_or_imprecise_dtypes=True).then_inc(s_cst, 1)
            pool.affine_select(out=rowmask[:, :], in_=k.ones[:, 0:1], compare_op=ALU.is_ge, fill=0.0,
                               base=LAST - 1, pattern=[[0, 1]], channel_multiplier=-1).then_inc(s_cst, 1)

            def body(t, u):
                pool.wait_ge(s_tr, t + 1)
                pool.sem_inc(idle["pool"], 1)
                pool.tensor_copy(st[:, u, 2:4, :].rearrange("p c n -> p (c n)"),
                                 k.big1[:, bass.ds(t, 1), :].rearrange("p a n -> p (a n)")).then_inc(s_x, 1)
            tiles(pool, body)

        @block.tensor
        def _(pe):
            pe.wait_ge(s_w, loaded)
            pe.sem_inc(s_tr, 2)
            pe.sem_inc(s_mm, 2)

            def transpose(t, u):
                pe.wait_ge(s_m, t + 1)
                pe.wait_ge(s_x, t + 1)
                pe.wait_ge(s_sT, t + 1)
                pe.sem_inc(idle["pe"], 1)
                for c in range(4):
                    last = pe.transpose(pT[:, u, c, :], st[:, u, c, :], k.ident[:, :])
                last.then_inc(s_tr, 1)

            def transpose3(t, u):
                pe.wait_ge(s_x3, t + 3)
                pe.wait_ge(s_x3T, t + 1)
                pe.sem_inc(idle["pe"], 1)
                for c in range(2):
                    last = pe.transpose(p3[:, u, c * P:(c + 1) * P], x3[:, u, c * P:(c + 1) * P], k.ident[:, :])
                last.then_inc(s_tr3, 1)

            def multiply(t, u):
                pe.wait_ge(s_sT, t + 3)
                pe.wait_ge(s_x3, t + 1)
                pe.sem_inc(idle["pe"], 1)
                for c in range(4):
                    last = pe.matmul(pX[:, u, 0:FEAT], sT[:, u, c, :], Wc[:, c, :], start=(c == 0), stop=(c == 3))
                last.then_inc(s_mm, 1)

            def logits(t, u):
                pe.wait_ge(s_x3T, t + 3)
                pe.wait_ge(s_L, t + 1)
                pe.sem_inc(idle["pe"], 1)
                for c in range(2):
                    last = pe.matmul(pL[:, u, 0:E], x3T[:, u, c, :], Wg[:, c, :], start=(c == 0), stop=(c == 1))
                last.then_inc(s_lg, 1)

            def step(t, u, one, two, three):
                if one:
                    transpose(t + 2, u)
                if three:
                    transpose3(t, u)
                if two:
                    multiply(t + 1, 1 - u)
                if three:
                    logits(t, u)
            skewed(pe, step)
            pe.wait_ge(s_A, 1)
            for r in range(NTILE // G):
                rhs = T[:, r * G:(r + 1) * G, :].rearrange("p i e -> p (i e)")
                if r:
                    pe.wait_ge(s_prc, 2 * r)
                pe.matmul(pR[:, 0:G * E], k.upper[:, :], rhs, start=True, stop=True)
                pe.matmul(pS[:, 0:G * E], k.ones[:, :], rhs, start=True, stop=True).then_inc(s_pr, 1)

        @block.scalar
        def _(act):
            act.sem_inc(s_sT, 2)
            act.sem_inc(s_x3T, 2)
            act.sem_inc(s_keep, 2)
            act.wait_ge(s_sq, 1)
            act.activation(din[:, :], din[:, :], ACT.Sqrt).then_inc(s_sq, 1)

            def copy(t, u):
                act.wait_ge(s_mm, t + 1)
                act.wait_ge(s_tr, t + 3)
                act.sem_inc(idle["act"], 1)
                act.activation(sT[:, u, :, :], pT[:, u, :, :], ACT.Copy).then_inc(s_sT, 1)

            def copy3(t, u):
                act.wait_ge(s_tr3, t + 1)
                act.sem_inc(idle["act"], 1)
                act.activation(x3T[:, u, :, :].rearrange("p c n -> p (c n)"), p3[:, u, 0:2 * P], ACT.Copy).then_inc(s_x3T, 1)

            def keep(t, u):
                act.wait_ge(s_x3, t + 3)
                act.sem_inc(idle["act"], 1)
                act.activation(k.big2[:, bass.ds(t, 1), 0:FEAT].rearrange("p a n -> p (a n)"), x3[:, u, :],
                               ACT.Copy).then_inc(s_keep, 1)

            def step(t, u, one, two, three):
                if one:
                    copy(t + 2, u)
                if three:
                    copy3(t, u)
                if two:
                    keep(t + 1, 1 - u)
            skewed(act, step)
            act.wait_ge(s_dv, 1)
            act.activation(k.gate[:, 1, :], v[:, 1, :], ACT.Exp).then_inc(s_ex, 1)

        @block.vector
        def _(dve):
            o = k.order.on(dve)
            dve.sem_inc(s_x3, 2)
            dve.sem_inc(s_L, 2)
            o(dve.tensor_scalar(din[:, :], k.big2[:, :, FEAT], 1.0, None, ALU.max))
            dve.sem_inc(s_sq, 1)
            dve.wait_ge(s_sq, 2)
            o(dve.reciprocal(din[:, :], din[:, :]))
            dve.wait_ge(s_w, loaded)
            o(dve.tensor_tensor(bias[:, 0, :], bias[:, 0, :], bias[:, 1, :], ALU.add))

            def stage(t, u):
                dve.wait_ge(s_tr, t + 1)
                dve.sem_inc(idle["dve"], 1)
                dve.tensor_scalar(st[:, u, 0:2, :].rearrange("p c n -> p (c n)"),
                                  k.big2[:, bass.ds(t, 1), 0:FEAT].rearrange("p a n -> p (a n)"),
                                  din[:, bass.ds(t, 1)], None, ALU.mult).then_inc(s_m, 1)

            def add(t, u):
                dve.wait_ge(s_mm, t + 3)
                dve.wait_ge(s_keep, t + 1)
                dve.sem_inc(idle["dve"], 1)
                dve.tensor_tensor(x3[:, u, :], pX[:, u, 0:FEAT], bias[:, 0, :], ALU.add).then_inc(s_x3, 1)

            def logits(t, u):
                dve.wait_ge(s_lg, t + 1)
                dve.sem_inc(idle["dve"], 1)
                dve.tensor_tensor(L[:, bass.ds(t, 1), :].rearrange("p a n -> p (a n)"), pL[:, u, 0:E], bg[:, :],
                                  ALU.add).then_inc(s_L, 1)

            def step(t, u, one, two, three):
                if one and (isinstance(t, int) is False or t < NTILE - 3):
                    stage(t + 3, 1 - u)
                if two:
                    add(t + 1, 1 - u)
                if three:
                    logits(t, u)
            stage(0, 0)
            skewed(dve, step)
            dve.wait_ge(s_L, NTILE + 2)
            dve.wait_ge(s_cst, 2)
            wide = lambda t: t.unsqueeze(2).to_broadcast([P, NTILE, E])
            num = k.iota[:, 0:E].unsqueeze(1).to_broadcast([P, NTILE, E])
            for j in range(2):
                o(dve.tensor_reduce(v[:, j, :], L[:, :, :], X, ALU.max))
                o(dve.tensor_tensor(T[:, :, :], L[:, :, :], wide(v[:, j, :]), ALU.is_lt))
                o(dve.scalar_tensor_tensor(T[:, :, :], T[:, :, :], 1024.0, num, ALU.mult, ALU.add))
                o(dve.tensor_reduce(first[:, :], T[:, :, :], X, ALU.min))
                o(dve.tensor_tensor(A[j][:, :, :], num, wide(first[:, :]), ALU.is_equal))
                if j == 0:
                    o(dve.scalar_tensor_tensor(L[:, :, :], A[0][:, :, :], -1e30, L[:, :, :], ALU.mult, ALU.add))
                o(dve.tensor_scalar(A[j][:, NTILE - 1, :], A[j][:, NTILE - 1, :], rowmask[:, :], None, ALU.mult))
            o(dve.tensor_tensor(v[:, 1, :], v[:, 1, :], v[:, 0, :], ALU.subtract))
            dve.sem_inc(s_dv, 1)
            o(dve.tensor_tensor(T[:, :, :], A[0][:, :, :], A[1][:, :, :], ALU.add))
            dve.sem_inc(s_A, 1)
            for r in range(NTILE // G):
                dve.wait_ge(s_pr, r + 1)
                dve.tensor_copy(rank[:, r * G:(r + 1) * G, :].rearrange("p i e -> p (i e)"), pR[:, 0:G * E]).then_inc(s_prc, 1)
                dve.tensor_copy(chosen[:, r * G:(r + 1) * G, :].rearrange("p i e -> p (i e)"),
                                pS[:, 0:G * E]).then_inc(s_prc, 1)
            dve.wait_ge(s_prc, 2 * (NTILE // G))
            for e in range(E):
                last = dve.tensor_tensor_scan(T[:, :, e], k.ones[:, 0:NTILE], chosen[:, :, e], 0.0, ALU.mult, ALU.add)
            o(last)
            o(dve.tensor_tensor(rank[:, 1:, :], rank[:, 1:, :], T[:, 0:NTILE - 1, :], ALU.add))
            o(dve.tensor_scalar(e3[:, 0, :], T[:, NTILE - 1, :], float(CAP), float(P - 1), ALU.min, ALU.add))
            o(dve.tensor_copy(e3i[:, :], e3[:, 0, :]))
            o(dve.tensor_scalar(e3i[:, :], e3i[:, :], 7, None, ALU.arith_shift_right))
            o(dve.tensor_copy(e3[:, 0, :], e3i[:, :]))
            o(dve.tensor_tensor_scan(e3[:, 1, :], k.ones[:, 0:E], e3[:, 0, :], 0.0, ALU.mult, ALU.add))
            o(dve.tensor_tensor(e3[:, 2, :], e3[:, 1, :], e3[:, 0, :], ALU.subtract))
            o(dve.tensor_scalar(e3[:, 2, :], e3[:, 2, :], float(P), None, ALU.mult))
            o(dve.tensor_tensor(cmp2[:, :, :], e3[:, 1, :].unsqueeze(1).to_broadcast([P, 2, E]),
                                tn2[:, :].unsqueeze(2).to_broadcast([P, 2, E]), ALU.is_le))
            o(dve.tensor_reduce(t2f[:, :], cmp2[:, :, :], X, ALU.add))
            o(dve.tensor_scalar(t2f[:, :], t2f[:, :], float(E - 1), None, ALU.min))
            o(dve.tensor_copy(t2i[:, :], t2f[:, :]))
            dve.sem_inc(s_tab, 1)
            dve.wait_ge(s_ex, 1)
            o(dve.tensor_scalar(k.gate[:, 0, :], k.gate[:, 1, :], 1.0, None, ALU.add))
            o(dve.reciprocal(k.gate[:, 0, :], k.gate[:, 0, :]))
            o(dve.tensor_tensor(k.gate[:, 1, :], k.gate[:, 1, :], k.gate[:, 0, :], ALU.mult))
            o(dve.tensor_scalar(L[:, :, :], rank[:, :, :], float(CAP), None, ALU.is_lt))
            o(dve.tensor_tensor(rank[:, :, :], rank[:, :, :], e3[:, 2, :].unsqueeze(1).to_broadcast([P, NTILE, E]), ALU.add))
            for j in range(2):
                o(dve.tensor_tensor(T[:, :, :], A[j][:, :, :], L[:, :, :], ALU.mult))
                o(dve.tensor_reduce(valid[:, :], T[:, :, :], X, ALU.add))
                o(dve.tensor_tensor(T[:, :, :], T[:, :, :], rank[:, :, :], ALU.mult))
                o(dve.tensor_reduce(k.gidx[:, :, j], T[:, :, :], X, ALU.add))
                o(dve.tensor_tensor(k.gate[:, j, :], k.gate[:, j, :], valid[:, :], ALU.mult))
                o(dve.tensor_scalar(valid[:, :], valid[:, :], -SKIP, SKIP, ALU.mult, ALU.add))
                o(dve.tensor_tensor(k.sidx[:, :, j], k.gidx[:, :, j], valid[:, :], ALU.add))


def phase_dispatch(nc, k):
    with ExitStack() as ctx:
        sb = lambda n, s, d: ctx.enter_context(nc.sbuf_tensor(n, s, d))
        sem = k.sem
        idx = sb("didx", [P, 2, 2], I32)
        rows = sb("drows", [P, 2, FEAT], F32)
        s_st = sem("rows_staged")
        s_sc = [sem("rows_scattered0"), sem("rows_scattered1")]
        idle = k.idle
        block = ctx.enter_context(nc.Block())

        @block.scalar
        def _(act):
            def stage(t, u, used):
                if used is not None:
                    act.wait_ge(s_sc[u], used)
                    act.sem_inc(idle["act"], 1)
                act.activation(idx[:, u, :], k.sidx[:, bass.ds(t, 1), :].rearrange("p a n -> p (a n)"), ACT.Copy).then_inc(s_st, 1)
                act.activation(rows[:, u, :], k.big2[:, bass.ds(t, 1), 0:FEAT].rearrange("p a n -> p (a n)"), ACT.Copy).then_inc(s_st, 1)
            for u in range(2):
                stage(u, u, None)
            with act.Fori(1, NTILE // 2) as i:
                for u in range(2):
                    stage(i * 2 + u, u, i * 32)
            stage(NTILE - 1, 0, 32 * (NTILE // 2))

        @block.gpsimd
        def _(pool):
            bound = pool.to_reg(MT * P - 1)

            def scatter(t, u):
                pool.wait_ge(s_st, t * 2 + 2)
                pool.sem_inc(idle["pool"], 1)
                for j in range(2):
                    pool.indirect_dma_start(k.xbuf[:, :], bass.IndirectOffsetOnAxis(ap=idx[:, u, j:j + 1], axis=0),
                                            rows[:, u, :], None, bounds_check=bound, oob_is_err=False).then_inc(s_sc[u], 16)
            with pool.Fori(0, NTILE // 2) as i:
                for u in range(2):
                    scatter(i * 2 + u, u)
            scatter(NTILE - 1, 0)
            pool.wait_ge(s_sc[0], 32 * (NTILE // 2 + 1))
            pool.wait_ge(s_sc[1], 32 * (NTILE // 2))


def phase_experts(nc, k):
    with ExitStack() as ctx:
        sb = lambda n, s, d: ctx.enter_context(nc.sbuf_tensor(n, s, d))
        ps = lambda n, s, d: ctx.enter_context(nc.psum_tensor(n, s, d))
        sem = k.sem
        HK = HID // P
        B = 4
        tab = sb("etab", [1, 2 * P], I32)
        b1r = sb("b1r", [EXPERTS, HID], F32)
        b1T = sb("b1T", [P, HK, EXPERTS], F32)
        w1 = sb("w1", [P, B, 2, HID], F32)
        w2 = sb("w2", [P, B, HK, FEAT], F32)
        b2 = sb("b2", [1, B, FEAT], F32)
        xt = sb("xt", [P, B, FEAT], F32)
        xT = sb("xTe", [P, 2, 2, P], F32)
        hT = sb("hT", [P, 2, HK, P], F32)
        y = sb("ye", [P, 2, FEAT], F32)
        pT = ps("pTe", [P, 2, BANK], F32)
        pH = ps("pH", [P, 2, HK, P], F32)
        pY = ps("pY", [P, 2, BANK], F32)
        s_in, loaded = k.inputs(32)
        s_bt = sem("b1_transposed")
        s_b = sem("b1T_ready")
        s_ld = [sem("expert_loaded%d" % b) for b in range(B)]
        s_tr = sem("xt_transposed")
        s_xT = sem("xTe_ready")
        s_h = sem("hidden_summed")
        s_g = sem("gelu_ready")
        s_y = sem("outputs_summed")
        s_yc = sem("outputs_copied")
        s_st = [sem("outputs_stored0"), sem("outputs_stored1")]
        s_yfree = sem("output_buffer_free")
        idle = k.idle
        block = ctx.enter_context(nc.Block())

        def tiles(eng, body):
            with eng.Fori(0, MT // B) as i:
                for u in range(B):
                    body(i * B + u, u, i)
            body(MT - 1, 0, MT // B)

        @block.sync
        def _(sp):
            sp.dma_start(tab[:, :], k.etab[:, :]).then_inc(s_in, 16)
            sp.dma_start(b1r[:, :], k.b1[:, :]).then_inc(s_in, 16)
            sp.wait_ge(s_in, loaded)

            def load(t, u, i):
                e = sp.value_load(tab[0:1, bass.ds(t, 1)], min_val=0, max_val=EXPERTS - 1)
                sp.wait_ge(s_y, t + 1)
                sp.sem_inc(idle["sp"], 1)
                sp.dma_start(xt[:, u, :], k.xbuf[bass.ds(t * P, P), :]).then_inc(s_ld[u], 16)
                sp.dma_start(w1[:, u, :, :], k.w1[bass.ds(e, 1), :, :].rearrange("a (c p) n -> p (a c) n", p=P)).then_inc(s_ld[u], 16)
                sp.dma_start(w2[:, u, :, :], k.w2[bass.ds(e, 1), :, :].rearrange("a (c p) n -> p (a c) n", p=P)).then_inc(s_ld[u], 16)
                sp.dma_start(b2[:, u, :], k.b2[bass.ds(e, 1), :]).then_inc(s_ld[u], 16)
            tiles(sp, load)

        @block.tensor
        def _(pe):
            pe.wait_ge(s_in, loaded)
            for c in range(HK):
                last = pe.transpose(pT[:, 0, c * EXPERTS:(c + 1) * EXPERTS], b1r[:, c * P:(c + 1) * P],
                                    k.ident[0:EXPERTS, 0:EXPERTS])
            last.then_inc(s_bt, 1)
            pe.sem_inc(s_y, B)
            pe.sem_inc(s_h, 2)
            pe.wait_ge(s_b, 1)

            def hidden(t, w, loaded):
                u = w % 2
                pe.wait_ge(s_ld[w], loaded)
                pe.wait_ge(s_xT, t + 1)
                pe.sem_inc(idle["pe"], 1)
                for c in range(2):
                    last = pe.transpose(pT[:, u, c * P:(c + 1) * P], xt[:, w, c * P:(c + 1) * P], k.ident[:, :])
                last.then_inc(s_tr, 1)
                pe.wait_ge(s_xT, t + 3)
                pe.wait_ge(s_g, t + 1)
                pe.sem_inc(idle["pe"], 1)
                for c in range(HK):
                    for d in range(2):
                        last = pe.matmul(pH[:, u, c, :], w1[:, w, d, c * P:(c + 1) * P], xT[:, u, d, :],
                                         start=(d == 0), stop=(d == 1))
                last.then_inc(s_h, 1)

            def outputs(t, w):
                u = w % 2
                pe.wait_ge(s_yc, t + 1)
                pe.sem_inc(idle["pe"], 1)
                pe.matmul(pY[:, u, 0:FEAT], k.ones[0:1, :], b2[:, w, :], start=True, stop=False)
                pe.wait_ge(s_g, t + 3)
                pe.sem_inc(idle["pe"], 1)
                for c in range(HK):
                    last = pe.matmul(pY[:, u, 0:FEAT], hT[:, u, c, :], w2[:, w, c, :], start=False, stop=(c == HK - 1))
                last.then_inc(s_y, 1)

            hidden(0, 0, 64)
            with pe.Fori(0, MT // B) as i:
                for u in range(B):
                    hidden(i * B + u + 1, (u + 1) % B, i * 64 + (128 if u == B - 1 else 64))
                    outputs(i * B + u, u)
            outputs(MT - 1, 0)

        @block.scalar
        def _(act):
            act.wait_ge(s_in, loaded)
            act.sem_inc(s_g, 2)
            act.wait_ge(s_b, 1)

            def body(t, u, i):
                e = act.value_load(tab[0:1, bass.ds(t, 1)], min_val=0, max_val=EXPERTS - 1)
                act.wait_ge(s_h, t + 3)
                act.wait_ge(s_y, t + B - 1)
                act.sem_inc(idle["act"], 1)
                for c in range(HK):
                    last = act.activation(hT[:, u % 2, c, :], pH[:, u % 2, c, :], ACT.Gelu, bias=b1T[:, c, bass.ds(e, 1)])
                last.then_inc(s_g, 1)
            tiles(act, body)

        @block.vector
        def _(dve):
            dve.wait_ge(s_bt, 1)
            dve.tensor_copy(b1T[:, :, :].rearrange("p c e -> p (c e)"), pT[:, 0, 0:HK * EXPERTS]).then_inc(s_b, 1)
            dve.sem_inc(s_xT, 2)
            dve.sem_inc(s_yc, 2)

            def rows(t, u):
                dve.wait_ge(s_tr, t + 1)
                dve.wait_ge(s_h, t + 1)
                dve.tensor_copy(xT[:, u % 2, :, :].rearrange("p c n -> p (c n)"), pT[:, u % 2, 0:FEAT]).then_inc(s_xT, 1)

            def outputs(t, u):
                dve.wait_ge(s_y, t + B + 1)
                dve.wait_ge(s_yfree, t + 1)
                dve.tensor_copy(y[:, u % 2, :], pY[:, u % 2, 0:FEAT]).then_inc(s_yc, 1)
            rows(0, 0)
            with dve.Fori(0, MT // B) as i:
                for u in range(B):
                    rows(i * B + u + 1, u + 1)
                    outputs(i * B + u, u)
            outputs(MT - 1, 0)

        @block.gpsimd
        def _(pool):
            pool.sem_inc(s_yfree, 2)

            def store(t, u, stored):
                pool.wait_ge(s_yc, t + 3)
                pool.sem_inc(idle["pool"], 1)
                pool.dma_start(k.ybuf[bass.ds(t * P, P), :], y[:, u, :]).then_inc(s_st[u], 16)
                pool.wait_ge(s_st[u], stored)
                pool.sem_inc(s_yfree, 1)
            with pool.Fori(0, MT // 2) as i:
                for u in range(2):
                    store(i * 2 + u, u, i * 16 + 16)
            store(MT - 1, 0, 16 * (MT // 2) + 16)


def phase_combine(nc, k):
    with ExitStack() as ctx:
        sb = lambda n, s, d: ctx.enter_context(nc.sbuf_tensor(n, s, d))
        sem = k.sem
        idx = sb("cidx", [P, 2, 2], I32)
        rows = sb("crows", [P, 2, 2, FEAT], F32)
        s_idx = sem("cidx_ready")
        s_g = [sem("y_gathered0"), sem("y_gathered1")]
        s_add = sem("y_added")
        idle = k.idle
        block = ctx.enter_context(nc.Block())

        @block.gpsimd
        def _(pool):
            bound = pool.to_reg(MT * P - 1)

            def gather(t, u):
                pool.wait_ge(s_idx, t + 1)
                pool.sem_inc(idle["pool"], 1)
                for j in range(2):
                    pool.indirect_dma_start(rows[:, u, j, :], None, k.ybuf[:, :],
                                            bass.IndirectOffsetOnAxis(ap=idx[:, u, j:j + 1], axis=0),
                                            bounds_check=bound).then_inc(s_g[u], 16)
            with pool.Fori(0, NTILE // 2) as i:
                for u in range(2):
                    gather(i * 2 + u, u)
            gather(NTILE - 1, 0)

        @block.vector
        def _(dve):
            def prepare(t, u):
                dve.tensor_copy(idx[:, u, :], k.gidx[:, bass.ds(t, 1), :].rearrange("p a n -> p (a n)")).then_inc(s_idx, 1)

            def add(t, u, i):
                y = k.big2[:, bass.ds(t, 1), 0:FEAT].rearrange("p a n -> p (a n)")
                dve.wait_ge(s_g[u], i * 32 + 32)
                dve.sem_inc(idle["dve"], 1)
                for j in range(2):
                    dve.scalar_tensor_tensor(y, rows[:, u, j, :], k.gate[:, j, bass.ds(t, 1)], y, ALU.mult, ALU.add).then_inc(s_add, 1)
                    dve.wait_ge(s_add, t * 2 + j + 1)
                    dve.sem_inc(idle["dve"], 1)
            for u in range(2):
                prepare(u, u)
            with dve.Fori(0, NTILE // 2 - 1) as i:
                for u in range(2):
                    add(i * 2 + u, u, i)
                    prepare(i * 2 + u + 2, u)
            add(NTILE - 3, 0, NTILE // 2 - 1)
            prepare(NTILE - 1, 0)
            add(NTILE - 2, 1, NTILE // 2 - 1)
            add(NTILE - 1, 0, NTILE // 2)


def phase_last_norm(nc, k):
    with ExitStack() as ctx:
        sb = lambda n, s, d: ctx.enter_context(nc.sbuf_tensor(n, s, d))
        ps = lambda n, s, d: ctx.enter_context(nc.psum_tensor(n, s, d))
        sem = k.sem
        K = 7
        NR = NTILE // K
        mask = sb("maskL", [P, 1], F32)
        col = sb("col", [P, FEAT], F32)
        col2 = sb("col2", [P, FEAT], F32)
        mean = sb("meanL", [P, FEAT], F32)
        scale = sb("scaleL", [P, FEAT], F32)
        gb = sb("gb", [P, 2, FEAT], F32)
        sq = sb("sqL", [P, 2, K, FEAT], F32)
        mu = sb("mu", [P, NTILE], F32)
        var = sb("varL", [P, NTILE], F32)
        sums = sb("row_sums", [P, K], F32)
        pc = ps("pc", [P, 2, BANK], F32)
        s_in, loaded = k.inputs(32)
        s_mask = sem("maskL_ready")
        s_c = sem("columns_ready")
        s_y = sem("y_centred")
        s_sq = sem("squares_ready")
        s_sqf = sem("squares_used")
        s_xb = sem("beta_added")
        s_mu = sem("row_means_ready")
        s_var = sem("row_variances_ready")
        s_p = sem("columns_summed")
        s_r = sem("root_wanted")
        s_rd = sem("root_ready")
        s_o = sem("chunk_ready")
        s_out, stored = k.stores(16 * (NR + 1))
        idle = k.idle
        block = ctx.enter_context(nc.Block())

        @block.sync
        def _(sp):
            sp.dma_start(gb[:, 0, :], k.gamma.partition_broadcast(P)).then_inc(s_in, 16)
            sp.dma_start(gb[:, 1, :], k.beta.partition_broadcast(P)).then_inc(s_in, 16)
            for r in range(NR):
                sp.wait_ge(s_o, r + 1)
                full = K if r < NR - 1 else K - 1
                sp.dma_start(k.out[r * K * P:(r * K + full) * P, :].rearrange("(i p) n -> p i n", p=P),
                             k.big1[:, r * K:r * K + full, :]).then_inc(s_out, 16)
            sp.dma_start(k.out[(NTILE - 1) * P:NODES, :], k.big1[0:LAST, NTILE - 1, :]).then_inc(s_out, 16)
            sp.wait_ge(s_out, stored)

        @block.gpsimd
        def _(pool):
            pool.affine_select(out=mask[:, :], in_=k.ones[:, 0:1], compare_op=ALU.is_ge, fill=0.0,
                               base=LAST - 1, pattern=[[0, 1]], channel_multiplier=-1).then_inc(s_mask, 1)
            pool.wait_ge(s_in, loaded)
            pool.tensor_tensor(k.big1[:, :, :], k.big1[:, :, :], gb[:, 1, :].unsqueeze(1).to_broadcast([P, NTILE, FEAT]),
                               ALU.add).then_inc(s_xb, 1)

        @block.tensor
        def _(pe):
            for j, c in enumerate((col, col2)):
                pe.wait_ge(s_c, j + 1)
                pe.matmul(pc[:, j, 0:FEAT], k.ones[:, :], c[:, :], start=True, stop=True).then_inc(s_p, 1)

        @block.scalar
        def _(act):
            act.wait_ge(s_y, 1)
            for r in range(NR):
                if r >= 2:
                    act.wait_ge(s_sqf, r - 1)
                act.activation(sq[:, r % 2, :, :], k.big2[:, r * K:(r + 1) * K, 0:FEAT], ACT.Square).then_inc(s_sq, 1)
            act.wait_ge(s_r, 1)
            act.activation(scale[:, :], scale[:, :], ACT.Sqrt).then_inc(s_rd, 1)
            act.sem_inc(s_var, 1)
            with act.Fori(0, NR) as r:
                act.wait_ge(s_mu, r + 1)
                act.wait_ge(s_var, r + 1)
                act.sem_inc(idle["act"], 1)
                for c in range(K):
                    t = bass.ds(r * K + c, 1)
                    last = act.activation(sq[:, 0, c, :], k.big1[:, t, :].rearrange("p a n -> p (a n)"), ACT.Square,
                                          bias=mu[:, t], accum_out=var[:, t])
                last.then_inc(s_var, 1)
            act.wait_ge(s_r, 2)
            act.activation(var[:, :], var[:, :], ACT.Sqrt).then_inc(s_rd, 1)

        @block.vector
        def _(dve):
            o = k.order.on(dve)
            y = k.big2[:, :, 0:FEAT]
            dve.wait_ge(s_mask, 1)
            dve.wait_ge(s_in, loaded)
            o(dve.tensor_scalar(y[:, NTILE - 1, :], y[:, NTILE - 1, :], mask[:, :], None, ALU.mult))
            o(dve.tensor_reduce(col[:, :], y.rearrange("p i n -> p n i"), X, ALU.add))
            dve.sem_inc(s_c, 1)
            dve.wait_ge(s_p, 1)
            o(dve.tensor_scalar(mean[:, :], pc[:, 0, 0:FEAT], 1.0 / NODES, None, ALU.mult))
            o(dve.tensor_tensor(y, y, mean[:, :].unsqueeze(1).to_broadcast([P, NTILE, FEAT]), ALU.subtract))
            o(dve.tensor_scalar(y[:, NTILE - 1, :], y[:, NTILE - 1, :], mask[:, :], None, ALU.mult))
            dve.sem_inc(s_y, 1)
            for r in range(NR):
                dve.wait_ge(s_sq, r + 1)
                o(dve.tensor_reduce((col if r else col2)[:, :], sq[:, r % 2, :, :].rearrange("p i n -> p n i"), X, ALU.add))
                dve.sem_inc(s_sqf, 1)
                if r:
                    o(dve.tensor_tensor(col2[:, :], col2[:, :], col[:, :], ALU.add))
            dve.sem_inc(s_c, 1)
            dve.wait_ge(s_p, 2)
            o(dve.tensor_scalar(scale[:, :], pc[:, 1, 0:FEAT], 1.0 / NODES, EPS_LN, ALU.mult, ALU.add))
            dve.sem_inc(s_r, 1)
            dve.wait_ge(s_rd, 1)
            o(dve.reciprocal(scale[:, :], scale[:, :]))
            o(dve.tensor_tensor(scale[:, :], scale[:, :], gb[:, 0, :], ALU.mult))
            o(dve.tensor_tensor(y, y, scale[:, :].unsqueeze(1).to_broadcast([P, NTILE, FEAT]), ALU.mult))
            dve.wait_ge(s_xb, 1)
            tile = lambda m, r, c: m[:, bass.ds(r * K + c, 1), 0:FEAT].rearrange("p a n -> p (a n)")
            with dve.Fori(0, NR) as r:
                o.enter(r, 2)
                for c in range(K):
                    last = dve.scalar_tensor_tensor(tile(k.big1, r, c), tile(k.big2, r, c), 1.0, tile(k.big1, r, c), ALU.mult, ALU.add,
                                                    accum_out=sums[:, c:c + 1])
                o(last)
                dve.sem_inc(idle["dve"], 1)
                o(dve.tensor_scalar(mu[:, bass.ds(r * K, K)], sums[:, :], -1.0 / FEAT, None, ALU.mult))
                dve.sem_inc(s_mu, 1)
                o.leave(NR)
            dve.wait_ge(s_var, NR + 1)
            o(dve.tensor_scalar(var[:, :], var[:, :], 1.0 / FEAT, EPS_LN, ALU.mult, ALU.add))
            dve.sem_inc(s_r, 1)
            dve.wait_ge(s_rd, 2)
            o(dve.reciprocal(var[:, :], var[:, :]))
            with dve.Fori(0, NR) as r:
                for c in range(K):
                    t = bass.ds(r * K + c, 1)
                    last = dve.tensor_scalar(tile(k.big1, r, c), tile(k.big1, r, c), mu[:, t], var[:, t], ALU.add, ALU.mult)
                last.then_inc(s_o, 1)


PHASES = [phase_sort_and_project, phase_count, phase_softmax, phase_messages_back, phase_first_norm, phase_gather, phase_route,
          phase_dispatch, phase_experts, phase_combine, phase_last_norm]


def gnn_resnorm_kernel(nc, x, src, dst, attr, W, att, W_gc, b_gc, W_res, b_res, Wg, bg, w1, b1, w2, b2, gamma, beta, out):
    with ExitStack() as ctx:
        k = Ctx()
        k.x, k.src, k.dst, k.attr, k.W, k.att, k.out = x, src, dst, attr, W, att, out
        k.W_gc, k.b_gc, k.W_res, k.b_res, k.Wg, k.bg = W_gc, b_gc, W_res, b_res, Wg, bg
        k.w1, k.b1, k.w2, k.b2, k.gamma, k.beta = w1, b1, w2, b2, gamma, beta
        k.sem = lambda n: ctx.enter_context(nc.semaphore(n))
        k.idle = {e: k.sem("idle_" + e) for e in ("pool", "act", "pe", "sp", "dve")}
        k.inputs = Shared(k.sem("inputs_loaded"))
        k.stores = Shared(k.sem("stores_landed"))
        k.order = Order(None, k.sem("dve_order"))
        k.dram = lambda n, s, d: nc.dram_tensor(n, s, d, kind="Internal").ap()
        sb = lambda n, s, d: ctx.enter_context(nc.sbuf_tensor(n, s, d))
        k.SS = k.dram("slots_by_source", (P * NT, 2), F32)
        k.DS = k.dram("slots_by_target", (P * NT, 2), F32)
        k.tab = k.dram("tile_tables", (3, NTM), I32)
        k.R = k.dram("running_counts", (NTILE + 1, P, HC), F32)
        k.OEB = k.dram("hyperedge_rows", (HCH * P, FEAT + HEADS), F32)
        k.H = k.dram("h_table", (NTILE * P, FEAT), F32)
        k.xbuf = k.dram("expert_inputs", (MT * P, FEAT), F32)
        k.ybuf = k.dram("expert_outputs", (MT * P, FEAT), F32)
        k.etab = k.dram("expert_of_tile", (1, 2 * P), I32)
        k.bT = k.dram("b_rows", (HEADS, HCH * P), F32)
        k.ident = sb("ident", [P, P], F32)
        k.upper = sb("upper", [P, P], F32)
        k.ones = sb("ones", [P, P], F32)
        k.iota = sb("iota", [P, P], F32)
        k.a = sb("a", [P, NTILE, HEADS], F32)
        k.bE = sb("bE", [P, HCH, HEADS], F32)
        k.ends = sb("ends_int", [P, NTILE], I32)
        k.deg = sb("deg", [P, NTILE], F32)
        k.u = sb("u", [P, NTILE, 2 * HEADS], F32)
        k.rD = sb("rD", [P, NTILE, HEADS], F32)
        k.big1 = sb("big1", [P, NTILE, FEAT], F32)
        sort = ExitStack()
        with sort:
            k.oeT = sort.enter_context(nc.sbuf_tensor("oeT", [P, 2, HCH * P], F32))
            with ExitStack() as edges:
                k.iota16 = edges.enter_context(nc.sbuf_tensor("iota16", [P, HC], F16))
                k.slot = edges.enter_context(nc.sbuf_tensor("slot", [P, 2, ECOL], F32))
                k.pay = edges.enter_context(nc.sbuf_tensor("pay", [P, 2, ECOL, 2], F32))
                for phase in PHASES[:3]:
                    phase(nc, k)
            for phase in PHASES[3:4]:
                phase(nc, k)
        k.gate = sb("gate", [P, 2, NTILE], F32)
        k.sidx = sb("scatter_slot", [P, NTILE, 2], F32)
        k.gidx = sb("gather_slot", [P, NTILE, 2], F32)
        k.big2 = sb("big2", [P, NTILE, FEAT + 1], F32)
        for phase in PHASES[4:]:
            phase(nc, k)


_INS = ["x", "src", "dst", "L0_gnn_hyperedge_attr", "L0_gnn_W", "L0_gnn_att", "L1_gnn_W_gc", "L1_gnn_b_gc",
        "L1_gnn_W_res", "L1_gnn_b_res", "L1_gnn_Wg", "L1_gnn_bg", "L1_gnn_w1", "L1_gnn_b1", "L1_gnn_w2",
        "L1_gnn_b2", "L1_gnn_gamma", "L1_gnn_beta"]


def kernel(**inputs):
    import numpy as _np
    import concourse.bacc as _bacc
    from concourse import mybir as _mybir
    from concourse.bass_utils import run_bass_kernel_spmd as _run

    nc = _bacc.Bacc("TRN2", target_bir_lowering=False, num_devices=1)
    arrays, args = {}, []
    for name in _INS:
        a = _np.ascontiguousarray(inputs[name])
        arrays[f"in_{name}_dram"] = a
        args.append(nc.dram_tensor(f"in_{name}_dram", a.shape, _mybir.dt.from_np(a.dtype), kind="ExternalInput").ap())
    args.append(nc.dram_tensor("out_0_dram", (NODES, FEAT), F32, kind="ExternalOutput").ap())
    gnn_resnorm_kernel(nc, *args)
    r = _run(nc, [arrays], core_ids=[0])
    return r.results[0]["out_0_dram"]
```
